# Optimizing a Trainium2 kernel written in Bass

```python
import numpy as np
import jax
import jax.numpy as jnp

def _softmax(x, axis=-1):
    return jax.nn.softmax(x, axis=axis)

def _gelu(x):
    return jax.nn.gelu(x, approximate=True)

def _silu(x):
    return jax.nn.silu(x)

def _sigmoid(x):
    return jax.nn.sigmoid(x)

def _layernorm(x, axis=-1, eps=1e-05):
    m = jnp.mean(x, axis=axis, keepdims=True)
    v = jnp.var(x, axis=axis, keepdims=True)
    return (x - m) / jnp.sqrt(v + eps)

def _scatter_add(tgt, idx, src, axis=0):
    return tgt.at[idx].add(src)

def _segment_sum(src, seg, n):
    return jax.ops.segment_sum(src, seg, n)
kernel_name = 'mk_lm_tower_d1_tok_ids256_r4_1782e4'

def setup_inputs(seed: int=0):
    np.random.seed(seed)
    _w = jnp.asarray

    def _rec_inputs():
        import jax
        import jax.numpy as jnp
        _rk = jax.random.key(seed)
        x = jax.random.randint(jax.random.fold_in(_rk, 1), (64, 200), 0, 50001, jnp.int32)
        return x
    x = _rec_inputs()

    def _L0_tok_setup():
        import jax, jax.numpy as jnp
        import numpy as np
        L = 2
        MAXLEN = 200
        HID = 64
        DFF = 4 * HID
        NITEM = 50001
        EPS = 1e-12

        def _ln(x, w, b):
            u = jnp.mean(x, axis=-1, keepdims=True)
            s = jnp.mean((x - u) ** 2, axis=-1, keepdims=True)
            return w * (x - u) / jnp.sqrt(s + EPS) + b
        key = jax.random.key(seed)
        ks = jax.random.split(key, 12)
        inp = {'input_ids': jax.random.randint(ks[0], (128, MAXLEN), 0, NITEM, dtype=jnp.int64), 'item_emb': jax.random.normal(ks[1], (NITEM, HID), jnp.float32) * 0.02, 'pos_emb': jax.random.normal(ks[2], (MAXLEN, HID), jnp.float32) * 0.02, 'ln0_w': jnp.ones((HID,), jnp.float32), 'ln0_b': jnp.zeros((HID,), jnp.float32), 'cw': jax.random.normal(ks[3], (L, MAXLEN // 2 + 1, HID, 2), jnp.float32) * 0.02, 'fln_w': jnp.ones((L, HID), jnp.float32), 'fln_b': jnp.zeros((L, HID), jnp.float32), 'd1_w': jax.random.normal(ks[4], (L, HID, DFF), jnp.float32) * 0.02, 'd1_b': jnp.zeros((L, DFF), jnp.float32), 'd2_w': jax.random.normal(ks[5], (L, DFF, HID), jnp.float32) * 0.02, 'd2_b': jnp.zeros((L, HID), jnp.float32), 'iln_w': jnp.ones((L, HID), jnp.float32), 'iln_b': jnp.zeros((L, HID), jnp.float32)}
        return inp
    _L0_tok_all = _L0_tok_setup()
    _L0_tok_in = {k: v for k, v in _L0_tok_all.items() if k in ('item_emb', 'pos_emb', 'ln0_w', 'ln0_b', 'cw', 'fln_w', 'fln_b', 'd1_w', 'd1_b', 'd2_w', 'd2_b', 'iln_w', 'iln_b')}
    del _L0_tok_all

    def _L0_attn_setup():
        import jax, jax.numpy as jnp
        import numpy as np
        B, S, F, H = (4, 256, 64, 8)
        SCALE = float(F) ** 0.5
        key = jax.random.key(seed)
        ks = jax.random.split(key, 5)
        return {'q_input': jax.random.normal(ks[0], (B, S, F), dtype=jnp.float32), 'Wq': jax.random.normal(ks[1], (F, F * H), dtype=jnp.float32) * 0.02, 'Wk': jax.random.normal(ks[2], (F, F * H), dtype=jnp.float32) * 0.02, 'Wv': jax.random.normal(ks[3], (F, F * H), dtype=jnp.float32) * 0.02, 'Wo': jax.random.normal(ks[4], (F * H, F), dtype=jnp.float32) * 0.02}
    _L0_attn_all = _L0_attn_setup()
    _L0_attn_in = {k: v for k, v in _L0_attn_all.items() if k in ('Wq', 'Wk', 'Wv', 'Wo')}
    del _L0_attn_all

    def _L0_ffn_setup():
        import jax, jax.numpy as jnp
        import numpy as np
        TOP_K = 2
        LN_EPS = 1e-05
        key = jax.random.key(seed)
        ks = jax.random.split(key, 8)
        B, S, D, E, H = (16, 256, 64, 8, 256)
        x = jax.random.normal(ks[0], (B, S, D), dtype=jnp.float32)
        Wr = jax.random.normal(ks[1], (D, E), dtype=jnp.float32) * 0.1
        br = jnp.zeros((E,), dtype=jnp.float32)
        ln_g = jnp.ones((E, D), dtype=jnp.float32)
        ln_b = jnp.zeros((E, D), dtype=jnp.float32)
        W1 = jax.random.normal(ks[2], (E, D, H), dtype=jnp.float32) * (1.0 / np.sqrt(D))
        b1 = jnp.zeros((E, H), dtype=jnp.float32)
        W2 = jax.random.normal(ks[3], (E, H, D), dtype=jnp.float32) * (1.0 / np.sqrt(H))
        b2 = jnp.zeros((E, D), dtype=jnp.float32)
        return {'x': x, 'Wr': Wr, 'br': br, 'ln_g': ln_g, 'ln_b': ln_b, 'W1': W1, 'b1': b1, 'W2': W2, 'b2': b2}
    _L0_ffn_all = _L0_ffn_setup()
    _L0_ffn_in = {k: v for k, v in _L0_ffn_all.items() if k in ('Wr', 'br', 'ln_g', 'ln_b', 'W1', 'b1', 'W2', 'b2')}
    del _L0_ffn_all
    return {'x': x, 'L0_tok_item_emb': _L0_tok_in['item_emb'], 'L0_tok_pos_emb': _L0_tok_in['pos_emb'], 'L0_tok_ln0_w': _L0_tok_in['ln0_w'], 'L0_tok_ln0_b': _L0_tok_in['ln0_b'], 'L0_tok_cw': _L0_tok_in['cw'], 'L0_tok_fln_w': _L0_tok_in['fln_w'], 'L0_tok_fln_b': _L0_tok_in['fln_b'], 'L0_tok_d1_w': _L0_tok_in['d1_w'], 'L0_tok_d1_b': _L0_tok_in['d1_b'], 'L0_tok_d2_w': _L0_tok_in['d2_w'], 'L0_tok_d2_b': _L0_tok_in['d2_b'], 'L0_tok_iln_w': _L0_tok_in['iln_w'], 'L0_tok_iln_b': _L0_tok_in['iln_b'], 'L0_attn_Wq': _L0_attn_in['Wq'], 'L0_attn_Wk': _L0_attn_in['Wk'], 'L0_attn_Wv': _L0_attn_in['Wv'], 'L0_attn_Wo': _L0_attn_in['Wo'], 'L0_ffn_Wr': _L0_ffn_in['Wr'], 'L0_ffn_br': _L0_ffn_in['br'], 'L0_ffn_ln_g': _L0_ffn_in['ln_g'], 'L0_ffn_ln_b': _L0_ffn_in['ln_b'], 'L0_ffn_W1': _L0_ffn_in['W1'], 'L0_ffn_b1': _L0_ffn_in['b1'], 'L0_ffn_W2': _L0_ffn_in['W2'], 'L0_ffn_b2': _L0_ffn_in['b2']}

def reference(x, L0_tok_item_emb, L0_tok_pos_emb, L0_tok_ln0_w, L0_tok_ln0_b, L0_tok_cw, L0_tok_fln_w, L0_tok_fln_b, L0_tok_d1_w, L0_tok_d1_b, L0_tok_d2_w, L0_tok_d2_b, L0_tok_iln_w, L0_tok_iln_b, L0_attn_Wq, L0_attn_Wk, L0_attn_Wv, L0_attn_Wo, L0_ffn_Wr, L0_ffn_br, L0_ffn_ln_g, L0_ffn_ln_b, L0_ffn_W1, L0_ffn_b1, L0_ffn_W2, L0_ffn_b2):
    import jax
    import jax.numpy as jnp

    def _L0_tok_ref(input_ids, item_emb, pos_emb, ln0_w, ln0_b, cw, fln_w, fln_b, d1_w, d1_b, d2_w, d2_b, iln_w, iln_b):
        import jax, jax.numpy as jnp
        import numpy as np
        L = 2
        MAXLEN = 200
        HID = 64
        DFF = 4 * HID
        NITEM = 50001
        EPS = 1e-12

        def _ln(x, w, b):
            u = jnp.mean(x, axis=-1, keepdims=True)
            s = jnp.mean((x - u) ** 2, axis=-1, keepdims=True)
            return w * (x - u) / jnp.sqrt(s + EPS) + b
        seq_len = input_ids.shape[1]
        x = item_emb[input_ids] + pos_emb[None, :, :]
        x = _ln(x, ln0_w, ln0_b)
        for l in range(L):
            f = jnp.fft.rfft(x, axis=1, norm='ortho')
            w = (cw[l, :, :, 0] + 1j * cw[l, :, :, 1])[None]
            y = jnp.fft.irfft(f * w, n=seq_len, axis=1, norm='ortho')
            x = _ln(y + x, fln_w[l], fln_b[l])
            h = jax.nn.gelu(jnp.einsum('bsh,hf->bsf', x, d1_w[l]) + d1_b[l], approximate=False)
            h = jnp.einsum('bsf,fh->bsh', h, d2_w[l]) + d2_b[l]
            x = _ln(h + x, iln_w[l], iln_b[l])
        return x

    def _L0_attn_ref(q_input, Wq, Wk, Wv, Wo):
        import jax, jax.numpy as jnp
        import numpy as np
        B, S, F, H = (4, 256, 64, 8)
        SCALE = float(F) ** 0.5
        b, s, f = q_input.shape
        h = Wq.shape[1] // f
        q = (q_input.reshape(b * s, f) @ Wq).reshape(b, s, f, h)
        k = (q_input.reshape(b * s, f) @ Wk).reshape(b, s, f, h)
        v = (q_input.reshape(b * s, f) @ Wv).reshape(b, s, f, h)
        qkt = jnp.einsum('bifh,bjfh->bijh', q, k)
        attn = jax.nn.sigmoid(qkt * SCALE)
        wv = jnp.einsum('bijh,bjfh->bifh', attn, v)
        wv = wv.reshape(b * s, f * h)
        out = jax.nn.relu(wv @ Wo)
        return out.reshape(b, s, f)

    def _L0_ffn_ref(x, Wr, br, ln_g, ln_b, W1, b1, W2, b2):
        import jax, jax.numpy as jnp
        import numpy as np
        TOP_K = 2
        LN_EPS = 1e-05
        B, S, D = x.shape
        N = B * S
        xt = x.reshape(N, D)
        logits = xt @ Wr + br
        probs = jax.nn.softmax(logits, axis=-1)
        top_p, top_idx = jax.lax.top_k(probs, TOP_K)
        weights = top_p / top_p.sum(axis=-1, keepdims=True)
        mu = xt.mean(axis=-1, keepdims=True)
        var = ((xt - mu) ** 2).mean(axis=-1, keepdims=True)
        xn = (xt - mu) * jax.lax.rsqrt(var + LN_EPS)
        xe = xn[None, :, :] * ln_g[:, None, :] + ln_b[:, None, :]
        h = jax.nn.gelu(jnp.einsum('end,edh->enh', xe, W1) + b1[:, None, :], approximate=False)
        y = jnp.einsum('enh,ehd->end', h, W2) + b2[:, None, :]
        y_tok = jnp.transpose(y, (1, 0, 2))
        sel = jnp.take_along_axis(y_tok, top_idx[:, :, None], axis=1)
        out = (weights[:, :, None] * sel).sum(axis=1)
        return out.reshape(B, S, D)
    h = _L0_tok_ref(x, L0_tok_item_emb, L0_tok_pos_emb, L0_tok_ln0_w, L0_tok_ln0_b, L0_tok_cw, L0_tok_fln_w, L0_tok_fln_b, L0_tok_d1_w, L0_tok_d1_b, L0_tok_d2_w, L0_tok_d2_b, L0_tok_iln_w, L0_tok_iln_b)
    h = h + _L0_attn_ref(_layernorm(h, axis=-1), L0_attn_Wq, L0_attn_Wk, L0_attn_Wv, L0_attn_Wo)
    h = h + _L0_ffn_ref(_layernorm(h, axis=-1), L0_ffn_Wr, L0_ffn_br, L0_ffn_ln_g, L0_ffn_ln_b, L0_ffn_W1, L0_ffn_b1, L0_ffn_W2, L0_ffn_b2)
    return h

_drawn_inputs = setup_inputs


def setup_inputs(seed=0):
    import zlib

    import numpy as np

    out = dict(_drawn_inputs(seed))
    spreads = {'L0_tok_ln0_w': (1.0, 0.2),
     'L0_tok_ln0_b': (0.0, 0.1),
     'L0_tok_fln_w': (1.0, 0.2),
     'L0_tok_fln_b': (0.0, 0.1),
     'L0_tok_d1_b': (0.0, 0.1),
     'L0_tok_d2_b': (0.0, 0.1),
     'L0_tok_iln_w': (1.0, 0.2),
     'L0_tok_iln_b': (0.0, 0.1),
     'L0_ffn_br': (0.0, 0.1),
     'L0_ffn_ln_g': (1.0, 0.2),
     'L0_ffn_ln_b': (0.0, 0.1),
     'L0_ffn_b1': (0.0, 0.1),
     'L0_ffn_b2': (0.0, 0.1)}
    factors = {}
    for name, (base, spread) in spreads.items():
        noise = np.random.default_rng([zlib.crc32(name.encode()), seed]).standard_normal(out[name].shape)
        drawn = base * np.exp(spread * noise) if base else spread * noise
        out[name] = jnp.asarray(drawn.astype(out[name].dtype))
    for name, factor in factors.items():
        out[name] = (out[name] * factor).astype(out[name].dtype)
    return out
```

```python
from contextlib import ExitStack

import concourse.bass as bass
from concourse import mybir

F32 = mybir.dt.float32
F16 = mybir.dt.float16
I32 = mybir.dt.int32
ALU = mybir.AluOpType
ACT = mybir.ActivationFunctionType
AX_X = mybir.AxisListType.X
RMAX = bass.bass_isa.ReduceOp.max

BATCH = 64
SEQ = 200
HID = 64
DFF = 256
HEADS = 8
EXPERTS = 8
EDIM = 256
LAYERS = 2
P = 128
S = SEQ // 2
TILES = 2 * BATCH
GT = 8
GROUPS = TILES // GT
NC = GT // 2 * S
PT_ = 4
PAIRS = BATCH // 2
NBIN = SEQ // 2 + 1
LAGS = SEQ + S
CH = 4
CSTEPS = HID // CH
EPS_TOK = 1e-12
EPS_LN = 1e-5
ds = bass.ds


def need(eng, sem, value):
    if not (isinstance(value, int) and value <= 0):
        eng.wait_ge(sem, value)


def late(g):
    return not isinstance(g, int) or g >= 2


def pipelined(eng, count, unroll, stages):
    lag = max(k for _, k in stages)
    start = unroll
    while start < lag + 2 * 2:
        start += unroll
    start = min(start, count)
    rounds = (count - start) // unroll

    def one(step, phase):
        for stage, k in stages:
            if isinstance(step, int) and not 0 <= step - k < count:
                continue
            stage(step - k, (phase - k) % unroll)

    for step in range(start):
        one(step, step % unroll)
    if rounds:
        with eng.Fori(start // unroll, start // unroll + rounds) as i:
            for u in range(unroll):
                for stage, k in stages:
                    stage(i * unroll + (u - k), (u - k) % unroll)
    for step in range(start + rounds * unroll, count + lag):
        one(step, step % unroll)


def build(nc, x, emb, pos, ln0_w, ln0_b, cw, fln_w, fln_b, d1_w, d1_b, d2_w, d2_b, iln_w, iln_b,
          wq, wk, wv, wo, wr, br, ln_g, ln_b, w1, b1, w2, b2, dft_re, dft_im, eye, selector, iota8,
          kern_dram, out):
    ctx = ExitStack()
    names = {}

    def sem(name):
        if name not in names:
            names[name] = ctx.enter_context(nc.semaphore(name))
        return names[name]

    def sb(stack, name, shape, dt=F32):
        return stack.enter_context(nc.sbuf_tensor(name, shape, dt))

    def pb(stack, name, shape, dt=F32):
        return stack.enter_context(nc.psum_tensor(name, shape, dt))

    with ctx:
        X = sb(ctx, "X", [P, TILES, HID])
        EYE = sb(ctx, "EYE", [P, P])
        NHALF, PHALF = sb(ctx, "NHALF", [P, GT]), sb(ctx, "PHALF", [P, GT])
        EPS_T, EPS_L = sb(ctx, "EPS_T", [P, GT]), sb(ctx, "EPS_L", [P, GT])
        D1Z = sb(ctx, "D1Z", [P, LAYERS, 2, DFF])
        D2 = sb(ctx, "D2", [P, LAYERS, 2, HID])
        D1B = sb(ctx, "D1B", [P, LAYERS, 2])
        D2B = sb(ctx, "D2B", [P, LAYERS])
        FW = sb(ctx, "FW", [P, LAYERS])
        FB = sb(ctx, "FB", [P, LAYERS])
        LASTW = sb(ctx, "LASTW", [S, HID])
        LASTB = sb(ctx, "LASTB", [S, HID])
        CBIAS = sb(ctx, "CBIAS", [S, LAYERS, HID])
        AS = sb(ctx, "AS", [P, HEADS, P], F16)
        BS = sb(ctx, "BS", [P, HEADS, HID], F16)
        W1S = sb(ctx, "W1S", [P, EXPERTS, EDIM], F16)
        WRS = sb(ctx, "WRS", [P, EXPERTS], F16)
        W2S = sb(ctx, "W2S", [P, EXPERTS, 2, HID])
        B1S = sb(ctx, "B1S", [P, EXPERTS, 2])
        B2S = sb(ctx, "B2S", [P, EXPERTS])
        BR = sb(ctx, "BR", [S, EXPERTS])
        SEL = sb(ctx, "SEL", [P, EXPERTS, HID], F16)
        IOTA = sb(ctx, "IOTA", [S, EXPERTS])
        MX = sb(ctx, "MX", [P, 4])
        SC = sb(ctx, "SC", [P, 4])

        with ExitStack() as st:
            IDX = sb(st, "IDX", [S, TILES], I32)
            POS = sb(st, "POS", [S, 2, HID])
            CWT = sb(st, "CWT", [NBIN, LAYERS, HID, 2])
            DRE = sb(st, "DRE", [NBIN, LAYERS, LAGS])
            DIM = sb(st, "DIM", [NBIN, LAYERS, LAGS])
            GAIN = sb(st, "GAIN", [HID, LAYERS])
            GB = sb(st, "GB", [S, LAYERS, HID])
            CW0 = sb(st, "CW0", [S, LAYERS, HID, 2])
            KERN = sb(st, "KERN", [HID, LAYERS, LAGS])
            WX = sb(st, "WX", [HID, 3, HEADS * HID])
            WXT = sb(st, "WXT", [HID, 3, HEADS, 2, HID])
            WO = sb(st, "WO", [HID, HEADS, HID])
            AN = sb(st, "AN", [P, HEADS, HID])
            BN = sb(st, "BN", [P, HEADS, HID])
            W1N = sb(st, "W1N", [P, EXPERTS, EDIM])
            W1R = sb(st, "W1R", [HID, EXPERTS, EDIM])
            LG = sb(st, "LG", [P, EXPERTS])
            LB = sb(st, "LB", [HID, EXPERTS])
            WRN = sb(st, "WRN", [P, EXPERTS])
            MXP = sb(st, "MXP", [P, 4])
            INV = sb(st, "INV", [P, 4])
            KP = pb(st, "KP", [HID, LAYERS, 512])
            TP = pb(st, "TP", [HID, 3, HEADS, HID])
            AP_ = pb(st, "AP_", [P, HEADS, HID])
            BP_ = pb(st, "BP_", [P, HEADS, HID])
            B1P = pb(st, "B1P", [P, EXPERTS, 2])
            LOADS = {}

            block = st.enter_context(nc.Block())

            @block.sync
            def _(sp):
                small = sem("small_loads")
                n = 0
                with nc.allow_non_contiguous_dma(reason="small parameters"):
                    sp.dma_start(IDX[:], x.rearrange("b (u s) -> s (b u)", u=2)).then_inc(sem("ids_loaded"), 16)
                    todo = [
                        (CWT[:], cw.rearrange("l k h c -> k l h c")),
                        (DRE[:], dft_re.rearrange("l k n -> k l n")), (DIM[:], dft_im.rearrange("l k n -> k l n")),
                        (GAIN[:, 0:1], ln0_w.rearrange("(h o) -> h o", o=1)),
                        (GAIN[:, 1:2], iln_w[0:1, :].rearrange("l h -> h l")),
                        (GB[:, 0, :], ln0_b.partition_broadcast(S)),
                        (GB[:, 1, :], iln_b[0, :].partition_broadcast(S)),
                        (CW0[:], cw[:, 0, :, :].partition_broadcast(S)),
                        (EYE[:], eye),
                        (WX[:, 0, :], wq), (WX[:, 1, :], wk), (WX[:, 2, :], wv),
                        (WO[:], wo.rearrange("(m h) d -> m h d", h=HEADS)),
                        (W1R[:], w1.rearrange("e d f -> d e f")),
                        (LB[:], ln_b.rearrange("e d -> d e")),
                        (B1S[:], b1.rearrange("e (c f) -> f e c", c=2)),
                        (W2S[:], w2.rearrange("e (c f) d -> f e c d", c=2)),
                        (POS[:], pos.rearrange("(u s) h -> s u h", u=2)),
                        (BR[:], br.partition_broadcast(S)),
                        (IOTA[:], iota8.partition_broadcast(S)),
                        (SEL[:], selector),
                        (LASTW[:], iln_w[1, :].partition_broadcast(S)),
                        (LASTB[:], iln_b[1, :].partition_broadcast(S)),
                        (D2[:], d2_w.rearrange("l (c f) h -> f l c h", c=2)),
                        (D1B[:], d1_b.rearrange("l (c f) -> f l c", c=2)),
                    ]
                    for half in range(2):
                        r = slice(half * HID, (half + 1) * HID)
                        todo += [
                            (W1N[r, :, :], w1.rearrange("e d f -> d e f")),
                            (LG[r, :], ln_g.rearrange("e d -> d e")),
                            (WRN[r, :], wr),
                            (B2S[r, :], b2.rearrange("e d -> d e")),
                            (D2B[r, :], d2_b.rearrange("l h -> h l")),
                            (FW[r, :], fln_w.rearrange("l h -> h l")),
                            (FB[r, :], fln_b.rearrange("l h -> h l")),
                        ]
                    for dst, src in todo:
                        sp.dma_start(dst, src).then_inc(small, 16)
                        n += 16
                    sp.wait_ge(sem("cleared"), 1)
                    for half in range(2):
                        r = slice(half * HID, (half + 1) * HID)
                        sp.dma_start(D1Z[r, :, half, :], d1_w.rearrange("l h f -> h l f")).then_inc(small, 16)
                        n += 16
                LOADS["small"] = n
                sp.wait_ge(sem("kernel_ready"), LAYERS)
                for l in range(LAYERS):
                    sp.dma_start(kern_dram[l], KERN[:, l, :]).then_inc(sem("kernel_stored"), 16)
                sp.wait_ge(sem("kernel_stored"), 16 * LAYERS)
                sp.wait_ge(small, n)

            n_small = LOADS["small"]

            @block.gpsimd
            def _(pool):
                pool.wait_ge(sem("ids_loaded"), 16)
                for t in range(TILES):
                    nc.gpsimd.indirect_dma_start(
                        X[0:S, t, :], None, emb, bass.IndirectOffsetOnAxis(ap=IDX[:, t:t + 1], axis=0)
                    ).then_inc(sem(f"gathered{t // GT}"), 16)
                pool.wait_ge(sem("maxima"), 4)
                nc.gpsimd.partition_all_reduce(MX[:], MXP[:], P, RMAX).then_inc(sem("max_all"), 1)
                for g in range(GROUPS):
                    pool.wait_ge(sem(f"gathered{g}"), 16 * GT)

            @block.scalar
            def _(act):
                act.wait_ge(sem("wx_transposed"), 1)
                for i in range(3):
                    for d in range(2):
                        nc.scalar.copy(WXT[:, i, :, d, :], TP[:, i, :, :]).then_inc(sem("wxt_ready"), 1)

            @block.tensor
            def _(pe):
                pe.wait_ge(sem("small_loads"), n_small)
                for l in range(LAYERS):
                    nc.tensor.matmul(KP[:, l, 0:LAGS], CWT[:, l, :, 0], DRE[:, l, :], start=True, stop=False)
                    nc.tensor.matmul(KP[:, l, 0:LAGS], CWT[:, l, :, 1], DIM[:, l, :], start=False,
                                     stop=True).then_inc(sem("kernel_summed"), 1)
                for i in range(3):
                    for h in range(HEADS):
                        last = nc.tensor.transpose(TP[:, i, h, :], WX[:, i, h::HEADS], EYE[0:HID, 0:HID])
                last.then_inc(sem("wx_transposed"), 1)
                pe.wait_ge(sem("wxt_ready"), 6)
                for h in range(HEADS):
                    last = nc.tensor.matmul(AP_[:, h, :], WXT[:, 0, h, :, :], WXT[:, 1, h, 0, :], start=True, stop=True)
                last.then_inc(sem("a_done"), 1)
                for h in range(HEADS):
                    last = nc.tensor.matmul(BP_[:, h, :], WXT[:, 2, h, :, :], WO[:, h, :], start=True, stop=True)
                last.then_inc(sem("b_done"), 1)
                for e in range(EXPERTS):
                    for c in range(2):
                        last = nc.tensor.matmul(B1P[:, e, c:c + 1], W1R[:, e, c * P:(c + 1) * P], LB[:, e:e + 1],
                                                start=True, stop=True)
                last.then_inc(sem("b1_done"), 1)

            @block.vector
            def _(dve):
                nc.vector.memset(D1Z[:], 0.0).then_inc(sem("cleared"), 1)
                for tile, value in ((NHALF, -0.5), (PHALF, 0.5), (EPS_T, EPS_TOK), (EPS_L, EPS_LN)):
                    nc.vector.memset(tile[:], value).then_inc(sem("consts"), 1)
                dve.wait_ge(sem("small_loads"), n_small)
                for l in range(LAYERS):
                    dve.wait_ge(sem("kernel_summed"), l + 1)
                    nc.vector.tensor_copy(KERN[:, l, :], KP[:, l, 0:LAGS]).then_inc(sem("k_a"), 1)
                    dve.wait_ge(sem("k_a"), l + 1)
                    nc.vector.tensor_scalar(KERN[:, l, S - 1:S], KERN[:, l, S - 1:S], 1.0, None,
                                            ALU.add).then_inc(sem("k_b"), 1)
                    dve.wait_ge(sem("k_b"), l + 1)
                    nc.vector.tensor_scalar(KERN[:, l, :], KERN[:, l, :], GAIN[:, l:l + 1], None,
                                            ALU.mult).then_inc(sem("kernel_ready"), 1)
                    nc.vector.tensor_scalar(CBIAS[:, l, :], CW0[:, l, :, 0], 1.0, None, ALU.add).then_inc(sem("cb_a"), 1)
                    dve.wait_ge(sem("cb_a"), l + 1)
                    nc.vector.tensor_tensor(CBIAS[:, l, :], CBIAS[:, l, :], GB[:, l, :], ALU.mult).then_inc(sem("cb_b"), 1)
                nc.vector.tensor_tensor(W1N[:], W1N[:], LG[:].unsqueeze(2).broadcast_to([P, EXPERTS, EDIM]),
                                        ALU.mult).then_inc(sem("w1_scaled"), 1)
                dve.wait_ge(sem("b1_done"), 1)
                nc.vector.tensor_tensor(B1S[:], B1S[:], B1P[:], ALU.add).then_inc(sem("b1_ready"), 1)
                dve.wait_ge(sem("a_done"), 1)
                nc.vector.tensor_copy(AN[:], AP_[:]).then_inc(sem("ab_copied"), 1)
                dve.wait_ge(sem("b_done"), 1)
                nc.vector.tensor_copy(BN[:], BP_[:]).then_inc(sem("ab_copied"), 1)
                dve.wait_ge(sem("ab_copied"), 2)
                dve.wait_ge(sem("w1_scaled"), 1)
                flat = [AN[:].rearrange("p h d -> p (h d)"), BN[:].rearrange("p h d -> p (h d)"),
                        W1N[:].rearrange("p h d -> p (h d)"), WRN[:]]
                for i, w in enumerate(flat):
                    nc.vector.reduce_max(MXP[:, i:i + 1], w, AX_X, apply_absolute_value=True).then_inc(sem("maxima"), 1)
                dve.wait_ge(sem("max_all"), 1)
                nc.vector.tensor_scalar(MX[:], MX[:], 1e-30, None, ALU.max).then_inc(sem("mx_guard"), 1)
                dve.wait_ge(sem("mx_guard"), 1)
                nc.vector.reciprocal(INV[:], MX[:]).then_inc(sem("mx_inv"), 1)
                nc.vector.tensor_copy(SC[:], MX[:]).then_inc(sem("sc_a"), 1)
                dve.wait_ge(sem("sc_a"), 1)
                nc.vector.tensor_scalar(SC[:, 0:1], SC[:, 0:1], float(HID) ** 0.5, None, ALU.mult).then_inc(sem("sc_b"), 1)
                dve.wait_ge(sem("mx_inv"), 1)
                dst = [AS[:, :, 0:HID], BS[:], W1S[:], WRS[:]]
                src = [AN[:], BN[:], W1N[:], WRN[:]]
                for i in range(4):
                    nc.vector.tensor_scalar(src[i], src[i], INV[:, i:i + 1], None, ALU.mult).then_inc(sem("normed"), 1)
                    dve.wait_ge(sem("normed"), i + 1)
                    nc.vector.tensor_copy(dst[i], src[i]).then_inc(sem("high"), 1)
                    dve.wait_ge(sem("high"), i + 1)
                    nc.vector.tensor_tensor(dst[i][HID:], src[i][HID:], dst[i][HID:], ALU.subtract).then_inc(sem("low"), 1)
                dve.wait_ge(sem("low"), 4)
                nc.vector.tensor_copy(AS[:, :, HID:], AS[:, :, 0:HID]).then_inc(sem("a_twice"), 1)
                dve.wait_ge(sem("a_twice"), 1)
                for g in range(GROUPS):
                    dve.wait_ge(sem(f"gathered{g}"), 16 * GT)
                    xv = X[0:S, g * GT:(g + 1) * GT, :].rearrange("s (b u) h -> s b u h", u=2)
                    nc.vector.tensor_tensor(xv, xv, POS[:].unsqueeze(1).broadcast_to([S, GT // 2, 2, HID]),
                                            ALU.add).then_inc(sem("pos_added"), 1)

        with ExitStack() as st:
            SUM = sb(st, "n_SUM", [S, 2, GT])
            SS = sb(st, "n_SS", [S, 2, GT])
            CEN = sb(st, "n_CEN", [S, 2, GT, HID])
            SQ = sb(st, "n_SQ", [S, 2, GT, HID])
            RS = sb(st, "n_RS", [S, 2, GT])
            block = st.enter_context(nc.Block())

            @block.vector
            def _(dve):
                def centre(g, b):
                    xg = X[0:S, ds(g * GT, GT), :]
                    nc.vector.reduce_sum(SUM[:, b, :], xg, AX_X).then_inc(sem("n_sum"), 1)
                    dve.wait_ge(sem("n_sum"), g + 1)
                    need(dve, sem("n_sq"), g - 1)
                    nc.vector.scalar_tensor_tensor(CEN[:, b], SUM[:, b, :].unsqueeze(2).broadcast_to([S, GT, HID]),
                                                   -1.0 / HID, xg, ALU.mult, ALU.add).then_inc(sem("n_cen"), 1)

                def squares(g, b):
                    dve.wait_ge(sem("n_sq"), g + 1)
                    nc.vector.reduce_sum(SS[:, b, :], SQ[:, b], AX_X).then_inc(sem("n_ss"), 1)

                def scale(g, b):
                    dve.wait_ge(sem("n_rs"), g + 1)
                    nc.vector.tensor_tensor(X[0:S, ds(g * GT, GT), :], CEN[:, b],
                                            RS[:, b, :].unsqueeze(2).broadcast_to([S, GT, HID]),
                                            ALU.mult).then_inc(sem("n_out"), 1)
                pipelined(dve, GROUPS, 2, [(scale, 1), (centre, 0), (squares, 0)])

            @block.scalar
            def _(act):
                def square(g, b):
                    act.wait_ge(sem("n_cen"), g + 1)
                    need(act, sem("n_ss"), g - 1)
                    nc.scalar.activation(SQ[:, b], CEN[:, b], ACT.Square, scale=HID ** -0.5).then_inc(sem("n_sq"), 1)
                pipelined(act, GROUPS, 2, [(square, 0)])

            @block.gpsimd
            def _(pool):
                def rstd(g, b):
                    pool.wait_ge(sem("n_ss"), g + 1)
                    need(pool, sem("n_out"), g - 1)
                    nc.gpsimd.tensor_tensor(RS[:, b, :], SS[:, b, :], EPS_T[0:S, :], ALU.add).then_inc(sem("n_var"), 1)
                    pool.wait_ge(sem("n_var"), g + 1)
                    nc.gpsimd.tensor_tensor(RS[:, b, :], RS[:, b, :], NHALF[0:S, 0:GT], ALU.pow).then_inc(sem("n_rs"), 1)
                pipelined(pool, GROUPS, 2, [(rstd, 0)])

        for l in range(LAYERS):
            with ExitStack() as lay:
                Z = sb(lay, f"Z{l}", [P, TILES, HID])

                with ExitStack() as st:
                    NT = 4
                    T = [sb(st, f"T{l}_{i}", [S, CH, SEQ]) for i in range(NT)]
                    YP = [pb(st, f"YP{l}_{i}", [S, CH, TILES]) for i in range(NT)]
                    block = st.enter_context(nc.Block())
                    cb = l * CSTEPS

                    @block.sync
                    def _(sp):
                        def load(g, b):
                            need(sp, sem("conv_mm"), cb + g - NT + 1 if not isinstance(g, int) or g >= NT else 0)
                            src = bass.AP(tensor=kern_dram.tensor,
                                          offset=(l * HID + g * CH) * LAGS, ap=[[1, S], [LAGS, CH], [1, SEQ]])
                            sp.dma_start(T[b][:], src).then_inc(sem(f"filter_loaded{b}"), 16)
                        for g in range(CSTEPS):
                            load(g, g % NT)

                    @block.tensor
                    def _(pe):
                        def conv(g, b):
                            pe.wait_ge(sem(f"filter_loaded{b}"), 16 * (l * CSTEPS // NT + g // NT + 1))
                            if g >= NT:
                                pe.wait_ge(sem("conv_out"), cb + g - NT + 1)
                            for c in range(CH):
                                h = g * CH + c
                                xh = X[0:S, :, h]
                                swap = xh.rearrange("s (b u) -> s b u", u=2)[:, :, ::-1]
                                yp = YP[b][:, c, :]
                                nc.tensor.matmul(yp, T[b][:, c, 0:S], xh, start=True, stop=False)
                                last = nc.tensor.matmul(yp, T[b][:, c, S:], swap, start=False, stop=True)
                            last.then_inc(sem("conv_mm"), 1)
                        for g in range(CSTEPS):
                            conv(g, g % NT)

                    @block.vector
                    def _(dve):
                        def store(g, b):
                            dve.wait_ge(sem("conv_mm"), cb + g + 1)
                            nc.vector.tensor_tensor(
                                Z[0:S, :, g * CH:(g + 1) * CH].rearrange("s t c -> s c t"), YP[b][:],
                                CBIAS[:, l, g * CH:(g + 1) * CH].unsqueeze(2).broadcast_to([S, CH, TILES]),
                                ALU.add).then_inc(sem("conv_out"), 1)
                        for g in range(CSTEPS):
                            store(g, g % NT)

                with ExitStack() as st:
                    def two(name, shape, dt=F32):
                        return [sb(st, f"{name}{l}_{i}", shape, dt) for i in range(2)]
                    SUM, SS, RS = two("f_SUM", [S, 2, GT]), two("f_SS", [S, 2, GT]), two("f_RS", [S, 2, GT])
                    CEN, SQ = two("f_CEN", [S, 2, GT, HID]), two("f_SQ", [S, 2, GT, HID])
                    XN = two("f_XN", [S, GT, HID])
                    XT = two("f_XT", [P, NC])
                    G = two("f_G", [P, 2, 2, NC])
                    R = two("f_R", [P, NC])
                    HB = two("f_HB", [S, GT, HID])
                    PT = [pb(st, f"f_PT{l}_{i}", [P, 512]) for i in range(2)]
                    PH = [pb(st, f"f_PH{l}_{i}", [P, 512]) for i in range(2)]
                    PY = [pb(st, f"f_PY{l}_{i}", [P, 512]) for i in range(2)]
                    PR = [pb(st, f"f_PR{l}_{i}", [S, GT, HID]) for i in range(2)]
                    block = st.enter_context(nc.Block())
                    gb = l * GROUPS
                    last_layer = l == LAYERS - 1

                    @block.vector
                    def _(dve):
                        def norm(k, src, g, b, out_, reuse):
                            nc.vector.reduce_sum(SUM[b][:, k, :], src, AX_X).then_inc(sem(f"f_sum{k}"), 1)
                            dve.wait_ge(sem(f"f_sum{k}"), gb + g + 1)
                            nc.vector.scalar_tensor_tensor(
                                CEN[b][:, k], SUM[b][:, k, :].unsqueeze(2).broadcast_to([S, GT, HID]),
                                -1.0 / HID, src, ALU.mult, ALU.add).then_inc(sem(f"f_cen{k}"), 1)
                            dve.wait_ge(sem(f"f_sq{k}"), gb + g + 1)
                            nc.vector.reduce_sum(SS[b][:, k, :], SQ[b][:, k], AX_X).then_inc(sem(f"f_ss{k}"), 1)
                            dve.wait_ge(sem(f"f_rs{k}"), gb + g + 1)
                            reuse()
                            nc.vector.tensor_tensor(out_, CEN[b][:, k], RS[b][:, k, :].unsqueeze(2).broadcast_to([S, GT, HID]),
                                                    ALU.mult).then_inc(sem(f"f_norm{k}"), 1)

                        def first(g, b):
                            norm(0, Z[0:S, ds(g * GT, GT), :], g, b, XN[b][:],
                                 lambda: need(dve, sem("f_xt"), gb + g - 1 if late(g) else 0))

                        def residual(g, b):
                            dve.wait_ge(sem("f_y"), gb + g + 1)
                            dve.wait_ge(sem("f_xt_sb"), gb + g + 1)
                            if late(g):
                                dve.wait_ge(sem("f_rt"), gb + g - 1)
                            nc.vector.scalar_tensor_tensor(R[b][:], PY[b][:, 0:NC], D2B[:, l:l + 1], XT[b][:], ALU.add,
                                                           ALU.add).then_inc(sem("f_r"), 1)

                        def second(g, b):
                            dve.wait_ge(sem("f_rt"), gb + g + 1)
                            if not last_layer:
                                norm(1, PR[b][:], g, b, X[0:S, ds(g * GT, GT), :], lambda: None)
                                return
                            norm(1, PR[b][:], g, b, HB[b][:], lambda: None)
                            dve.wait_ge(sem("f_norm1"), gb + g + 1)
                            nc.vector.tensor_tensor(HB[b][:], HB[b][:], LASTW[:].unsqueeze(1).broadcast_to([S, GT, HID]),
                                                    ALU.mult).then_inc(sem("f_lastw"), 1)
                            dve.wait_ge(sem("f_lastw"), g + 1)
                            nc.vector.tensor_tensor(X[0:S, ds(g * GT, GT), :], HB[b][:],
                                                    LASTB[:].unsqueeze(1).broadcast_to([S, GT, HID]),
                                                    ALU.add).then_inc(sem("f_lastb"), 1)
                        pipelined(dve, GROUPS, 2, [(residual, 1), (first, 0), (second, 1)])

                    @block.scalar
                    def _(act):
                        def square(k, g, b):
                            act.wait_ge(sem(f"f_cen{k}"), gb + g + 1)
                            nc.scalar.activation(SQ[b][:, k], CEN[b][:, k], ACT.Square, scale=HID ** -0.5).then_inc(sem(f"f_sq{k}"), 1)

                        def affine(g, b):
                            act.wait_ge(sem("f_xt"), gb + g + 1)
                            if late(g):
                                act.wait_ge(sem("f_r"), gb + g - 1)
                            nc.scalar.activation(XT[b][:], PT[b][:, 0:NC], ACT.Identity, bias=FB[:, l:l + 1],
                                                 scale=FW[:, l:l + 1]).then_inc(sem("f_xt_sb"), 1)

                        def gelu(g, b):
                            if late(g):
                                act.wait_ge(sem("f_y"), gb + g - 1)
                            for i in range(4):
                                par, c = divmod(i, 2)
                                act.wait_ge(sem("f_h"), 4 * (gb + g) + i + 1)
                                nc.scalar.activation(G[b][:, par, c, :], PH[i % 2][:, 0:NC], ACT.Gelu,
                                                     bias=D1B[:, l, c:c + 1]).then_inc(sem("f_gelu"), 1)
                        pipelined(act, GROUPS, 2, [(lambda g, b: square(0, g, b), 0), (affine, 0),
                                                   (lambda g, b: square(1, g, b), 1), (gelu, 0)])

                    @block.gpsimd
                    def _(pool):
                        def rstd(k, g, b):
                            pool.wait_ge(sem(f"f_ss{k}"), gb + g + 1)
                            nc.gpsimd.tensor_tensor(RS[b][:, k, :], SS[b][:, k, :], EPS_T[0:S, :], ALU.add).then_inc(sem(f"f_var{k}"), 1)
                            pool.wait_ge(sem(f"f_var{k}"), gb + g + 1)
                            nc.gpsimd.tensor_tensor(RS[b][:, k, :], RS[b][:, k, :], NHALF[0:S, 0:GT],
                                                    ALU.pow).then_inc(sem(f"f_rs{k}"), 1)
                        pipelined(pool, GROUPS, 2, [(lambda g, b: rstd(0, g, b), 0), (lambda g, b: rstd(1, g, b), 1)])

                    @block.tensor
                    def _(pe):
                        def transpose_in(g, b):
                            pe.wait_ge(sem("f_norm0"), gb + g + 1)
                            if late(g):
                                pe.wait_ge(sem("f_xt_sb"), gb + g - 1)
                            for p in range(GT // 2):
                                last = nc.tensor.transpose(PT[b][:, p * S:(p + 1) * S], XN[b][:, 2 * p:2 * p + 2, :],
                                                           EYE[0:S, 0:S])
                            last.then_inc(sem("f_xt"), 1)

                        def up(g, b):
                            pe.wait_ge(sem("f_xt_sb"), gb + g + 1)
                            for i in range(4):
                                par, c = divmod(i, 2)
                                if not (isinstance(g, int) and g == 0 and i < 2):
                                    pe.wait_ge(sem("f_gelu"), 4 * (gb + g) + i - 1)
                                nc.tensor.matmul(PH[i % 2][:, 0:NC], D1Z[:, l, par, c * P:(c + 1) * P], XT[b][:],
                                                 start=True, stop=True).then_inc(sem("f_h"), 1)

                        def down(g, b):
                            pe.wait_ge(sem("f_gelu"), 4 * (gb + g) + 4)
                            if late(g):
                                pe.wait_ge(sem("f_r"), gb + g - 1)
                            for c in range(2):
                                for par in range(2):
                                    last = nc.tensor.matmul(PY[b][par * HID:(par + 1) * HID, 0:NC], D2[:, l, c, :],
                                                            G[b][:, par, c, :], start=(c == 0), stop=(c == 1))
                            last.then_inc(sem("f_y"), 1)

                        def transpose_out(g, b):
                            pe.wait_ge(sem("f_r"), gb + g + 1)
                            if late(g):
                                pe.wait_ge(sem("f_cen1"), gb + g - 1)
                            for p in range(GT // 2):
                                last = nc.tensor.transpose(PR[b][:, 2 * p:2 * p + 2, :], R[b][:, p * S:(p + 1) * S],
                                                           EYE[:])
                            last.then_inc(sem("f_rt"), 1)
                        pipelined(pe, GROUPS, 2, [(transpose_out, 1), (transpose_in, 0), (up, 0), (down, 0)])

        with ExitStack() as st:
            def two(name, shape, dt=F32):
                return [sb(st, f"{name}_{i}", shape, dt) for i in range(2)]
            SUM, SS, RS = two("a_SUM", [S, PT_]), two("a_SS", [S, PT_]), two("a_RS", [S, PT_])
            CEN, SQ, XN = two("a_CEN", [S, PT_, HID]), two("a_SQ", [S, PT_, HID]), two("a_XN", [S, PT_, 2, HID])
            H2, L2 = two("a_H2", [P, NC], F16), two("a_L2", [P, NC], F16)
            U = two("a_U", [S, PT_, HEADS, HID])
            TS = two("a_TS", [P, NC], F16)
            AT = two("a_AT", [S, 2, NC])
            RO = two("a_RO", [P, SEQ])
            PT = pb(st, "a_PT", [P, 512])
            PU = pb(st, "a_PU", [P, 512])
            PTT = pb(st, "a_PTT", [P, 512])
            PO = pb(st, "a_PO", [P, 512])
            PS = [pb(st, f"a_PS{i}", [P, 2, 512]) for i in range(2)]
            block = st.enter_context(nc.Block())

            def exists(p):
                return not isinstance(p, int) or 0 <= p < PAIRS

            def tiles_of(p):
                return X[0:S, ds(p * PT_, PT_), :]

            @block.vector
            def _(dve):
                def centre(p, b):
                    nc.vector.reduce_sum(SUM[b][:], tiles_of(p), AX_X).then_inc(sem("a_sum"), 1)
                    dve.wait_ge(sem("a_sum"), p + 1)
                    nc.vector.scalar_tensor_tensor(CEN[b][:], SUM[b][:].unsqueeze(2).broadcast_to([S, PT_, HID]),
                                                   -1.0 / HID, tiles_of(p), ALU.mult, ALU.add).then_inc(sem("a_cen"), 1)

                def squares(p, b):
                    dve.wait_ge(sem("a_sq"), p + 1)
                    nc.vector.reduce_sum(SS[b][:], SQ[b][:], AX_X).then_inc(sem("a_ss"), 1)

                def scale(p, b):
                    dve.wait_ge(sem("a_rs"), p + 1)
                    if late(p):
                        dve.wait_ge(sem("a_xt"), p - 1)
                    nc.vector.tensor_tensor(XN[b][:], CEN[b][:].unsqueeze(2).broadcast_to([S, PT_, 2, HID]),
                                            RS[b][:].unsqueeze(2).unsqueeze(3).broadcast_to([S, PT_, 2, HID]),
                                            ALU.mult).then_inc(sem("a_norm"), 1)

                def low(p, b):
                    dve.wait_ge(sem("a_h2"), p + 1)
                    nc.vector.tensor_tensor(L2[b][:], PT[:, 0:NC], H2[b][:], ALU.subtract).then_inc(sem("a_l2"), 1)

                def values(p, b, i):
                    dve.wait_ge(sem("a_u"), p * PT_ + i + 1)
                    nc.vector.tensor_copy(U[b][:, i, :, :].rearrange("s h d -> s (h d)"),
                                          PU[0:S, :]).then_inc(sem("a_u_sb"), 1)

                def query_low(n, k):
                    dve.wait_ge(sem("a_tcast"), n + 1)
                    nc.vector.tensor_tensor(TS[k][HID:, :], PTT[HID:, 0:NC], TS[k][HID:, :],
                                            ALU.subtract).then_inc(sem("a_tlow"), 1)

                def add(p):
                    dve.wait_ge(sem("a_ot"), p + 1)
                    xv = tiles_of(p).rearrange("s (b u) d -> s u b d", u=2)
                    nc.vector.tensor_tensor(xv, xv, PU[0:S, 0:2 * P].rearrange("s (u b d) -> s u b d", u=2, b=2),
                                            ALU.add).then_inc(sem("a_added"), 1)

                def begin(p, b):
                    if isinstance(p, int) and p == 0:
                        centre(0, 0)
                        squares(0, 0)
                        scale(0, 0)
                        low(0, 0)
                        for i in range(PT_):
                            values(0, 0, i)
                        query_low(0, 0)

                def main(p, b):
                    nxt, nb = p + 1, 1 - b
                    for h in range(HEADS):
                        n = p * HEADS + h
                        if h < HEADS - 1 or exists(nxt):
                            query_low(n + 1, (h + 1) % 2)
                        if h == 2 and exists(p - 1):
                            add(p - 1)
                        if exists(nxt):
                            if h == 0:
                                centre(nxt, nb)
                            if h == 1:
                                squares(nxt, nb)
                            if h == 2:
                                scale(nxt, nb)
                            if h == 3:
                                low(nxt, nb)
                            if h >= 4:
                                values(nxt, nb, h - 4)
                pipelined(dve, PAIRS, 2, [(begin, 0), (main, 1)])
                add(PAIRS - 1)

            @block.gpsimd
            def _(pool):
                def rstd(p, b):
                    pool.wait_ge(sem("a_ss"), p + 1)
                    nc.gpsimd.tensor_tensor(RS[b][:], SS[b][:], EPS_L[0:S, 0:PT_], ALU.add).then_inc(sem("a_var"), 1)
                    pool.wait_ge(sem("a_var"), p + 1)
                    nc.gpsimd.tensor_tensor(RS[b][:], RS[b][:], NHALF[0:S, 0:PT_], ALU.pow).then_inc(sem("a_rs"), 1)
                pipelined(pool, PAIRS, 2, [(rstd, 0)])

            @block.scalar
            def _(act):
                def square(p, b):
                    act.wait_ge(sem("a_cen"), p + 1)
                    nc.scalar.activation(SQ[b][:], CEN[b][:], ACT.Square, scale=HID ** -0.5).then_inc(sem("a_sq"), 1)

                def high(p, b):
                    act.wait_ge(sem("a_xt"), p + 1)
                    nc.scalar.copy(H2[b][:], PT[:, 0:NC]).then_inc(sem("a_h2"), 1)

                def query_high(n, k):
                    act.wait_ge(sem("a_t"), n + 1)
                    nc.scalar.copy(TS[k][:], PTT[:, 0:NC]).then_inc(sem("a_tcast"), 1)

                def sigmoid(n, k):
                    act.wait_ge(sem("a_s"), n + 1)
                    if late(n):
                        act.wait_ge(sem("a_av"), n - 1)
                    nc.scalar.activation(AT[k][:], PS[k][0:S, :, 0:NC], ACT.Sigmoid,
                                         scale=SC[0:S, 0:1]).then_inc(sem("a_sig"), 1)

                def relu(p, b):
                    act.wait_ge(sem("a_av"), (p + 1) * HEADS)
                    if late(p):
                        act.wait_ge(sem("a_ot"), p - 1)
                    nc.scalar.activation(RO[b][:], PO[:, 0:SEQ], ACT.Relu, scale=SC[:, 1:2]).then_inc(sem("a_relu"), 1)

                def begin(p, b):
                    if isinstance(p, int) and p == 0:
                        square(0, 0)
                        high(0, 0)
                        query_high(0, 0)

                def main(p, b):
                    nxt, nb = p + 1, 1 - b
                    for h in range(HEADS):
                        n = p * HEADS + h
                        if h < HEADS - 1 or exists(nxt):
                            query_high(n + 1, (h + 1) % 2)
                        sigmoid(n, h % 2)
                        if h == 0 and exists(p - 1):
                            relu(p - 1, nb)
                        if exists(nxt):
                            if h == 0:
                                square(nxt, nb)
                            if h == 2:
                                high(nxt, nb)
                pipelined(act, PAIRS, 2, [(begin, 0), (main, 1)])
                relu(PAIRS - 1, (PAIRS - 1) % 2)

            @block.tensor
            def _(pe):
                def transpose_in(p, b):
                    pe.wait_ge(sem("a_norm"), p + 1)
                    if not (isinstance(p, int) and p == 0):
                        pe.wait_ge(sem("a_l2"), p)
                    for i in range(PT_):
                        last = nc.tensor.transpose(PT[:, i * S:(i + 1) * S],
                                                   XN[b][:, i, :, :], EYE[0:S, 0:S])
                    last.then_inc(sem("a_xt"), 1)

                def values(p, b, i):
                    pe.wait_ge(sem("a_l2"), p + 1)
                    if not (isinstance(p, int) and p == 0 and i == 0):
                        pe.wait_ge(sem("a_u_sb"), p * PT_ + i)
                    cols = slice(i * S, (i + 1) * S)
                    nc.tensor.matmul(PU[0:S, :], H2[b][:, cols], BS[:], start=True, stop=False)
                    nc.tensor.matmul(PU[0:S, :], L2[b][:, cols], BS[:], start=False, stop=True).then_inc(sem("a_u"), 1)

                def query(n, b, h):
                    if not (isinstance(n, int) and n == 0):
                        pe.wait_ge(sem("a_tlow"), n)
                    nc.tensor.matmul(PTT[:, 0:NC], AS[:, h, :], H2[b][:], start=True, stop=False)
                    nc.tensor.matmul(PTT[:, 0:NC], AS[:, h, :], L2[b][:], start=False, stop=True).then_inc(sem("a_t"), 1)

                def scores(n, b, h):
                    pe.wait_ge(sem("a_tlow"), n + 1)
                    if late(n):
                        pe.wait_ge(sem("a_sig"), n - 1)
                    for bb in range(2):
                        for jc in range(2):
                            cols = slice((2 * bb + jc) * S, (2 * bb + jc + 1) * S)
                            o = PS[h % 2][0:S, bb, jc * SEQ:(jc + 1) * SEQ]
                            q = TS[h % 2][:, bb * SEQ:(bb + 1) * SEQ]
                            nc.tensor.matmul(o, H2[b][:, cols], q, start=True, stop=False)
                            last = nc.tensor.matmul(o, L2[b][:, cols], q, start=False, stop=True)
                    last.then_inc(sem("a_s"), 1)

                def mix(n, b, h):
                    pe.wait_ge(sem("a_sig"), n + 1)
                    for jc in range(2):
                        for bb in range(2):
                            last = nc.tensor.matmul(PO[bb * HID:(bb + 1) * HID, 0:SEQ], U[b][:, 2 * bb + jc, h, :],
                                                    AT[h % 2][:, bb, jc * SEQ:(jc + 1) * SEQ],
                                                    start=(h == 0 and jc == 0), stop=(h == HEADS - 1 and jc == 1))
                    last.then_inc(sem("a_av"), 1)

                def transpose_out(p, b):
                    pe.wait_ge(sem("a_relu"), p + 1)
                    for u in range(2):
                        last = nc.tensor.transpose(PU[0:S, u * P:(u + 1) * P], RO[b][:, u * S:(u + 1) * S], EYE[:])
                    last.then_inc(sem("a_ot"), 1)

                def begin(p, b):
                    if isinstance(p, int) and p == 0:
                        transpose_in(0, 0)
                        for i in range(PT_):
                            values(0, 0, i)
                        query(0, 0, 0)

                def main(p, b):
                    nxt, nb = p + 1, 1 - b
                    for h in range(HEADS):
                        n = p * HEADS + h
                        if h < HEADS - 1:
                            query(n + 1, b, h + 1)
                        elif exists(nxt):
                            query(n + 1, nb, 0)
                        scores(n, b, h)
                        if h > 0:
                            if h == 1 and exists(p - 1):
                                pe.wait_ge(sem("a_relu"), p)
                            mix(n - 1, b, h - 1)
                        elif exists(p - 1):
                            mix(n - 1, nb, HEADS - 1)
                        if h == 1 and exists(p - 1):
                            transpose_out(p - 1, nb)
                        if exists(nxt):
                            if h == 2:
                                transpose_in(nxt, nb)
                            if h == 4 and exists(p - 1):
                                pe.wait_ge(sem("a_added"), p)
                            if h >= 4:
                                values(nxt, nb, h - 4)
                pipelined(pe, PAIRS, 2, [(begin, 0), (main, 1)])
                mix(PAIRS * HEADS - 1, (PAIRS - 1) % 2, HEADS - 1)
                transpose_out(PAIRS - 1, (PAIRS - 1) % 2)

        with ExitStack() as st:
            def two(name, shape, dt=F32):
                return [sb(st, f"{name}_{i}", shape, dt) for i in range(2)]
            SUM, SS, RS, RV, VR = (two(f"m_{n}", [S, GT]) for n in ("SUM", "SS", "RS", "RV", "VR"))
            CEN, SQ, XN = two("m_CEN", [S, GT, HID]), two("m_SQ", [S, GT, HID]), two("m_XN", [S, GT, 2, HID])
            H2, L2 = two("m_H2", [P, 2, NC], F16), two("m_L2", [P, 2, NC], F16)
            LOG, EQ, OH1, OH2 = (sb(st, f"m_{n}", [S, GT, EXPERTS]) for n in ("LOG", "EQ", "OH1", "OH2"))
            M1, M2, I1, I2, DF, EX, WA, WB_ = (sb(st, f"m_{n}", [S, GT]) for n in
                                               ("M1", "M2", "I1", "I2", "DF", "EX", "WA", "WB"))
            ETILE = sb(st, "m_E", [S, GT])
            WG = sb(st, "m_WG", [S, GT, EXPERTS])
            WP = sb(st, "m_WP", [S, GT, P], F16)
            EYE16 = sb(st, "m_EYE16", [S, S], F16)
            WT = two("m_WT", [P, 2, NC], F16)
            G = two("m_G", [P, 2, 2, NC])
            WBS = two("m_WBS", [P, NC])
            YW = two("m_YW", [P, NC])
            ACC = two("m_ACC", [P, NC])
            ZERO = sb(st, "m_ZERO", [P, NC])
            OUT = two("m_OUT", [S, GT, HID])
            PT = [pb(st, f"m_PT{i}", [P, 512]) for i in range(2)]
            PL = pb(st, "m_PL", [P, 512])
            PH = [pb(st, f"m_PH{i}", [P, 512]) for i in range(2)]
            PY = [pb(st, f"m_PY{i}", [P, 512]) for i in range(2)]
            PW = pb(st, "m_PW", [P, 512])
            PW16 = PT[1][:, 0:NC].bitcast(F16)
            out_v = out.rearrange("b (u s) h -> s (b u) h", u=2)
            block = st.enter_context(nc.Block())

            def exists(g):
                return not isinstance(g, int) or 0 <= g < GROUPS

            @block.sync
            def _(sp):
                for g in range(GROUPS):
                    sp.wait_ge(sem("m_out"), g + 1)
                    sp.dma_start(out_v[:, g * GT:(g + 1) * GT, :], OUT[g % 2][:]).then_inc(sem(f"m_stored{g % 2}"), 16)
                for b in range(2):
                    sp.wait_ge(sem(f"m_stored{b}"), 16 * (GROUPS // 2))

            NR = 17

            @block.vector
            def _(dve):
                nc.vector.memset(WP[:], 0.0).then_inc(sem("m_init"), 1)
                nc.vector.memset(ZERO[:], 0.0).then_inc(sem("m_init"), 1)
                nc.vector.memset(ETILE[:], 2.718281828459045).then_inc(sem("m_init"), 1)
                nc.vector.tensor_copy(EYE16[:], EYE[0:S, 0:S]).then_inc(sem("m_init"), 1)
                dve.wait_ge(sem("m_init"), 4)

                def tiles_of(g):
                    return X[0:S, ds(g * GT, GT), :]

                def centre(g, b):
                    nc.vector.reduce_sum(SUM[b][:], tiles_of(g), AX_X).then_inc(sem("m_sum"), 1)
                    dve.wait_ge(sem("m_sum"), g + 1)
                    nc.vector.scalar_tensor_tensor(CEN[b][:], SUM[b][:].unsqueeze(2).broadcast_to([S, GT, HID]),
                                                   -1.0 / HID, tiles_of(g), ALU.mult, ALU.add).then_inc(sem("m_cen"), 1)

                def squares(g, b):
                    dve.wait_ge(sem("m_sq"), g + 1)
                    nc.vector.reduce_sum(SS[b][:], SQ[b][:], AX_X).then_inc(sem("m_ss"), 1)

                def scale(g, b):
                    dve.wait_ge(sem("m_rs"), g + 1)
                    nc.vector.tensor_tensor(XN[b][:], CEN[b][:].unsqueeze(2).broadcast_to([S, GT, 2, HID]),
                                            RS[b][:].unsqueeze(2).unsqueeze(3).broadcast_to([S, GT, 2, HID]),
                                            ALU.mult).then_inc(sem("m_norm"), 1)

                def low(g, b):
                    for i in range(2):
                        dve.wait_ge(sem("m_h2"), 2 * g + i + 1)
                        nc.vector.tensor_tensor(L2[b][:, i, :], PT[i][:, 0:NC], H2[b][:, i, :],
                                                ALU.subtract).then_inc(sem("m_l2"), 1)

                def route(g, b, part):
                    step = [NR * g]

                    def link(ins):
                        ins.then_inc(sem("m_route"), 1)
                        step[0] = step[0] + 1
                        dve.wait_ge(sem("m_route"), step[0])

                    def bc(t):
                        return t[:].unsqueeze(2).broadcast_to([S, GT, EXPERTS])
                    iota = IOTA[:].unsqueeze(1).broadcast_to([S, GT, EXPERTS])
                    v = nc.vector
                    if part == 0:
                        dve.wait_ge(sem("m_logits"), g + 1)
                        dve.wait_ge(sem("m_rv"), g + 1)
                        link(v.tensor_tensor(LOG[:], PL[0:S, 0:GT * EXPERTS].rearrange("s (t e) -> s t e", e=EXPERTS),
                                             bc(RV[b]), ALU.mult))
                        link(v.tensor_tensor(LOG[:], LOG[:], BR[:].unsqueeze(1).broadcast_to([S, GT, EXPERTS]), ALU.add))
                        link(v.reduce_max(M1[:], LOG[:], AX_X))
                        link(v.tensor_tensor(EQ[:], LOG[:], bc(M1), ALU.is_equal))
                        link(v.tensor_tensor(EQ[:], EQ[:], iota, ALU.mult))
                        link(v.tensor_reduce(I1[:], EQ[:], AX_X, ALU.min))
                        link(v.tensor_tensor(OH1[:], iota, bc(I1), ALU.is_equal))
                        link(v.scalar_tensor_tensor(LOG[:], OH1[:], -1e38, LOG[:], ALU.mult, ALU.add))
                        link(v.reduce_max(M2[:], LOG[:], AX_X))
                        link(v.tensor_tensor(EQ[:], LOG[:], bc(M2), ALU.is_equal))
                        link(v.tensor_tensor(EQ[:], EQ[:], iota, ALU.mult))
                        link(v.tensor_reduce(I2[:], EQ[:], AX_X, ALU.min))
                        link(v.tensor_tensor(OH2[:], iota, bc(I2), ALU.is_equal))
                        v.tensor_tensor(DF[:], M2[:], M1[:], ALU.subtract).then_inc(sem("m_diff"), 1)
                    else:
                        step[0] = NR * g + 13
                        dve.wait_ge(sem("m_exp"), g + 1)
                        link(v.tensor_scalar(WA[:], EX[:], 1.0, None, ALU.add))
                        link(v.reciprocal(WA[:], WA[:]))
                        link(v.tensor_tensor(WB_[:], EX[:], WA[:], ALU.mult))
                        v.tensor_tensor(OH1[:], OH1[:], bc(WA), ALU.mult).then_inc(sem("m_oh1"), 1)
                        link(v.tensor_tensor(OH2[:], OH2[:], bc(WB_), ALU.mult))
                        dve.wait_ge(sem("m_oh1"), g + 1)
                        v.tensor_tensor(WG[:], OH1[:], OH2[:], ALU.add).then_inc(sem("m_wg"), 1)
                        dve.wait_ge(sem("m_wg"), g + 1)
                        if not (isinstance(g, int) and g == 0):
                            dve.wait_ge(sem("m_wt_ps"), g)
                        v.tensor_copy(WP[:, :, 0:EXPERTS], WG[:]).then_inc(sem("m_wphigh"), 1)
                        dve.wait_ge(sem("m_wphigh"), g + 1)
                        v.tensor_tensor(WP[:, :, HID:HID + EXPERTS], WG[:], WP[:, :, 0:EXPERTS],
                                        ALU.subtract).then_inc(sem("m_wp"), 1)

                def weigh(n, e):
                    dve.wait_ge(sem("m_w"), n + 1)
                    nc.vector.tensor_copy(WBS[e % 2][:], PW[:, 0:NC]).then_inc(sem("m_wbs"), 1)
                    dve.wait_ge(sem("m_wbs"), n + 1)
                    dve.wait_ge(sem("m_y"), n + 1)
                    if late(n):
                        dve.wait_ge(sem("m_acc"), n - 1)
                    nc.vector.scalar_tensor_tensor(YW[e % 2][:], PY[e % 2][:, 0:NC], B2S[:, e:e + 1], WBS[e % 2][:],
                                                   ALU.add, ALU.mult).then_inc(sem("m_yw"), 1)

                def finish(g, b):
                    dve.wait_ge(sem("m_ot"), g + 1)
                    if late(g):
                        if isinstance(g, int):
                            dve.wait_ge(sem(f"m_stored{b}"), 16 * (g // 2))
                        else:
                            dve.wait_ge(sem(f"m_stored{b}"), (g - b) * 8)
                    nc.vector.tensor_tensor(OUT[b][:].rearrange("s (k p) d -> s p k d", k=2),
                                            tiles_of(g).rearrange("s (k p) d -> s p k d", k=2),
                                            PT[0][0:S, :].rearrange("s (p k d) -> s p k d", p=GT // 2, k=2),
                                            ALU.add).then_inc(sem("m_out"), 1)

                def begin(g, b):
                    if isinstance(g, int) and g == 0:
                        centre(0, 0)
                        squares(0, 0)
                        scale(0, 0)
                        low(0, 0)
                        route(0, 0, 0)
                        route(0, 0, 1)

                def main(g, b):
                    nxt, nb = g + 1, 1 - b
                    for e in range(EXPERTS):
                        n = g * EXPERTS + e
                        if e > 0:
                            weigh(n - 1, e - 1)
                        elif exists(g - 1):
                            weigh(n - 1, EXPERTS - 1)
                        if e == 1 and exists(g - 1):
                            finish(g - 1, nb)
                        if exists(nxt):
                            if e == 0:
                                centre(nxt, nb)
                            if e == 1:
                                squares(nxt, nb)
                            if e == 2:
                                scale(nxt, nb)
                            if e == 4:
                                low(nxt, nb)
                            if e == 5:
                                route(nxt, nb, 0)
                            if e == 6:
                                route(nxt, nb, 1)
                pipelined(dve, GROUPS, 2, [(begin, 0), (main, 1)])
                weigh(GROUPS * EXPERTS - 1, EXPERTS - 1)
                finish(GROUPS - 1, (GROUPS - 1) % 2)

            @block.gpsimd
            def _(pool):
                pool.wait_ge(sem("m_init"), 4)

                def rstd(g, b):
                    step = [7 * g]

                    def link(ins):
                        ins.then_inc(sem("m_stat"), 1)
                        step[0] = step[0] + 1
                        pool.wait_ge(sem("m_stat"), step[0])
                    q = nc.gpsimd
                    pool.wait_ge(sem("m_ss"), g + 1)
                    link(q.tensor_tensor(RV[b][:], SS[b][:], EPS_L[0:S, :], ALU.add))
                    link(q.tensor_tensor(RS[b][:], RV[b][:], NHALF[0:S, 0:GT], ALU.pow))
                    link(q.tensor_tensor(VR[b][:], RS[b][:], RS[b][:], ALU.mult))
                    link(q.tensor_tensor(VR[b][:], VR[b][:], SS[b][:], ALU.mult))
                    link(q.tensor_tensor(VR[b][:], VR[b][:], EPS_L[0:S, :], ALU.add))
                    link(q.tensor_tensor(RV[b][:], VR[b][:], NHALF[0:S, 0:GT], ALU.pow))
                    q.tensor_tensor(RS[b][:], RS[b][:], RV[b][:], ALU.mult).then_inc(sem("m_rs"), 1)
                    pool.wait_ge(sem("m_rs"), g + 1)
                    link(q.tensor_tensor(RV[b][:], VR[b][:], PHALF[0:S, 0:GT], ALU.pow))
                    q.tensor_tensor(RV[b][:], RV[b][:], SC[0:S, 3:4].broadcast_to([S, GT]), ALU.mult).then_inc(sem("m_rv"), 1)

                def exponent(g, b):
                    pool.wait_ge(sem("m_diff"), g + 1)
                    nc.gpsimd.tensor_tensor(EX[:], ETILE[:], DF[:], ALU.pow).then_inc(sem("m_exp"), 1)

                def accumulate(n, e, b):
                    pool.wait_ge(sem("m_yw"), n + 1)
                    if e == 0:
                        nc.gpsimd.tensor_tensor(ACC[b][:], YW[0][:], ZERO[:], ALU.add).then_inc(sem("m_acc"), 1)
                    else:
                        pool.wait_ge(sem("m_acc"), n)
                        nc.gpsimd.tensor_tensor(ACC[b][:], ACC[b][:], YW[e % 2][:], ALU.add).then_inc(sem("m_acc"), 1)

                def begin(g, b):
                    if isinstance(g, int) and g == 0:
                        rstd(0, 0)
                        exponent(0, 0)

                def main(g, b):
                    nxt, nb = g + 1, 1 - b
                    for e in range(EXPERTS):
                        n = g * EXPERTS + e
                        if e > 0:
                            accumulate(n - 1, e - 1, b)
                        elif exists(g - 1):
                            accumulate(n - 1, EXPERTS - 1, nb)
                        if exists(nxt):
                            if e == 1:
                                rstd(nxt, nb)
                            if e == 5:
                                exponent(nxt, nb)
                pipelined(pool, GROUPS, 2, [(begin, 0), (main, 1)])
                accumulate(GROUPS * EXPERTS - 1, EXPERTS - 1, (GROUPS - 1) % 2)

            @block.scalar
            def _(act):
                def square(g, b):
                    act.wait_ge(sem("m_cen"), g + 1)
                    nc.scalar.activation(SQ[b][:], CEN[b][:], ACT.Square, scale=HID ** -0.5).then_inc(sem("m_sq"), 1)

                def high(g, b):
                    act.wait_ge(sem("m_xt"), g + 1)
                    for i in range(2):
                        nc.scalar.copy(H2[b][:, i, :], PT[i][:, 0:NC]).then_inc(sem("m_h2"), 1)

                def weights(g, b):
                    act.wait_ge(sem("m_wt_ps"), g + 1)
                    nc.scalar.copy(WT[b][:].rearrange("p k c -> p (k c)"), PW16).then_inc(sem("m_wt"), 1)

                def gelu(n, e):
                    if late(n):
                        act.wait_ge(sem("m_y"), n - 1)
                    for i in range(4):
                        k, c = divmod(i, 2)
                        act.wait_ge(sem("m_h"), 4 * n + i + 1)
                        nc.scalar.activation(G[e % 2][:, k, c, :], PH[i % 2][:, 0:NC], ACT.Gelu, bias=B1S[:, e, c:c + 1],
                                             scale=SC[:, 2:3]).then_inc(sem("m_gelu"), 1)

                def begin(g, b):
                    if isinstance(g, int) and g == 0:
                        square(0, 0)
                        high(0, 0)
                        weights(0, 0)

                def main(g, b):
                    nxt, nb = g + 1, 1 - b
                    for e in range(EXPERTS):
                        gelu(g * EXPERTS + e, e)
                        if exists(nxt):
                            if e == 0:
                                square(nxt, nb)
                            if e == 3:
                                high(nxt, nb)
                            if e == 7:
                                weights(nxt, nb)
                pipelined(act, GROUPS, 2, [(begin, 0), (main, 1)])

            @block.tensor
            def _(pe):
                pe.wait_ge(sem("m_init"), 4)

                def transpose_in(g, b):
                    pe.wait_ge(sem("m_norm"), g + 1)
                    if not (isinstance(g, int) and g == 0):
                        pe.wait_ge(sem("m_wt"), g)
                    if not isinstance(g, int) or g >= 2:
                        pe.wait_ge(sem("m_out"), g - 1)
                    for t in range(GT):
                        last = nc.tensor.transpose(PT[t // 4][:, (t % 4) * S:(t % 4 + 1) * S],
                                                   XN[b][:, t, :, :], EYE[0:S, 0:S])
                    last.then_inc(sem("m_xt"), 1)

                def logits(g, b):
                    pe.wait_ge(sem("m_l2"), 2 * g + 2)
                    for t in range(GT):
                        cols = slice((t % 4) * S, (t % 4 + 1) * S)
                        o = PL[0:S, t * EXPERTS:(t + 1) * EXPERTS]
                        nc.tensor.matmul(o, H2[b][:, t // 4, cols], WRS[:], start=True, stop=False)
                        last = nc.tensor.matmul(o, L2[b][:, t // 4, cols], WRS[:], start=False, stop=True)
                    last.then_inc(sem("m_logits"), 1)

                def transpose_weights(g, b):
                    pe.wait_ge(sem("m_wp"), g + 1)
                    for t in range(GT):
                        last = nc.tensor.transpose(PW16[:, t * S:(t + 1) * S], WP[:, t, :], EYE16[:])
                    last.then_inc(sem("m_wt_ps"), 1)

                def up(n, e, b, i):
                    k, c = divmod(i, 2)
                    if not (isinstance(n, int) and n == 0 and i < 2):
                        pe.wait_ge(sem("m_gelu"), 4 * n + i - 1)
                    w = W1S[:, e, c * P:(c + 1) * P]
                    nc.tensor.matmul(PH[i % 2][:, 0:NC], w, H2[b][:, k, :], start=True, stop=False)
                    nc.tensor.matmul(PH[i % 2][:, 0:NC], w, L2[b][:, k, :], start=False, stop=True).then_inc(sem("m_h"), 1)

                def down(n, e, b):
                    if late(n):
                        pe.wait_ge(sem("m_yw"), n - 1)
                    if not (isinstance(n, int) and n == 0):
                        pe.wait_ge(sem("m_wbs"), n)
                    for k in range(2):
                        last = nc.tensor.matmul(PW[k * HID:(k + 1) * HID, 0:NC], SEL[:, e, :], WT[b][:, k, :],
                                                start=True, stop=True)
                    last.then_inc(sem("m_w"), 1)
                    pe.wait_ge(sem("m_gelu"), 4 * n + 4)
                    for c in range(2):
                        for k in range(2):
                            last = nc.tensor.matmul(PY[e % 2][k * HID:(k + 1) * HID, 0:NC], W2S[:, e, c, :],
                                                    G[e % 2][:, k, c, :], start=(c == 0), stop=(c == 1))
                    last.then_inc(sem("m_y"), 1)

                def transpose_out(g, b):
                    pe.wait_ge(sem("m_acc"), EXPERTS * (g + 1))
                    for p in range(GT // 2):
                        last = nc.tensor.transpose(PT[0][0:S, p * P:(p + 1) * P], ACC[b][:, p * S:(p + 1) * S], EYE[:])
                    last.then_inc(sem("m_ot"), 1)

                def begin(g, b):
                    if isinstance(g, int) and g == 0:
                        transpose_in(0, 0)
                        logits(0, 0)
                        transpose_weights(0, 0)
                        pe.wait_ge(sem("m_wt"), 1)

                def main(g, b):
                    nxt, nb = g + 1, 1 - b
                    for e in range(EXPERTS):
                        n = g * EXPERTS + e
                        up(n, e, b, 0)
                        up(n, e, b, 1)
                        if e > 0:
                            down(n - 1, e - 1, b)
                        elif exists(g - 1):
                            down(n - 1, EXPERTS - 1, nb)
                            pe.wait_ge(sem("m_wt"), g + 1)
                        up(n, e, b, 2)
                        up(n, e, b, 3)
                        if e == 1 and exists(g - 1):
                            transpose_out(g - 1, nb)
                        if exists(nxt):
                            if e == 3:
                                transpose_in(nxt, nb)
                            if e == 4:
                                logits(nxt, nb)
                            if e == 7:
                                transpose_weights(nxt, nb)
                pipelined(pe, GROUPS, 2, [(begin, 0), (main, 1)])
                down(GROUPS * EXPERTS - 1, EXPERTS - 1, (GROUPS - 1) % 2)
                transpose_out(GROUPS - 1, (GROUPS - 1) % 2)


_INS = ["x", "L0_tok_item_emb", "L0_tok_pos_emb", "L0_tok_ln0_w", "L0_tok_ln0_b", "L0_tok_cw", "L0_tok_fln_w",
        "L0_tok_fln_b", "L0_tok_d1_w", "L0_tok_d1_b", "L0_tok_d2_w", "L0_tok_d2_b", "L0_tok_iln_w", "L0_tok_iln_b",
        "L0_attn_Wq", "L0_attn_Wk", "L0_attn_Wv", "L0_attn_Wo", "L0_ffn_Wr", "L0_ffn_br", "L0_ffn_ln_g",
        "L0_ffn_ln_b", "L0_ffn_W1", "L0_ffn_b1", "L0_ffn_W2", "L0_ffn_b2"]


def kernel(**inputs):
    import numpy as _np
    import concourse.bacc as _bacc
    from concourse import mybir as _mybir
    from concourse.bass_utils import run_bass_kernel_spmd as _run

    nc = _bacc.Bacc("TRN2", target_bir_lowering=False, num_devices=1)
    k = _np.arange(NBIN)[:, None]
    lag = _np.arange(LAGS)
    lags = _np.stack([S - 1 - lag, lag - (S - 1)]) % SEQ
    fold = _np.where((k == 0) | (k == SEQ // 2), 1.0, 2.0) / SEQ
    sel = _np.zeros((P, EXPERTS, HID), _np.float16)
    for e in range(EXPERTS):
        sel[e, e, :] = 1
        sel[HID + e, e, :] = 1
    angle = 2 * _np.pi * ((k * lags[:, None]) % SEQ) / SEQ
    consts = {
        "dft_re": (fold * _np.cos(angle)).astype(_np.float32),
        "dft_im": (-fold * _np.sin(angle)).astype(_np.float32),
        "eye": _np.eye(P, dtype=_np.float32),
        "selector": sel,
        "iota8": (_np.arange(EXPERTS) - EXPERTS).astype(_np.float32),
    }
    arrays, args = {}, []
    for name in _INS + list(consts):
        a = _np.ascontiguousarray(inputs[name] if name in inputs else consts[name])
        arrays[f"in_{name}_dram"] = a
        args.append(nc.dram_tensor(f"in_{name}_dram", a.shape, _mybir.dt.from_np(a.dtype), kind="ExternalInput").ap())
    args.append(nc.dram_tensor("kernels_dram", (LAYERS, HID, LAGS), F32, kind="Internal").ap())
    args.append(nc.dram_tensor("out_0_dram", (BATCH, SEQ, HID), F32, kind="ExternalOutput").ap())
    build(nc, *args)
    r = _run(nc, [arrays], core_ids=[0])
    return r.results[0]["out_0_dram"]
```

```python
from contextlib import ExitStack

import concourse.bass as bass
from concourse import mybir

F32 = mybir.dt.float32
F16 = mybir.dt.float16
I32 = mybir.dt.int32
ALU = mybir.AluOpType
ACT = mybir.ActivationFunctionType
AX_X = mybir.AxisListType.X
RMAX = bass.bass_isa.ReduceOp.max

BATCH = 64
SEQ = 200
HID = 64
DFF = 256
HEADS = 8
EXPERTS = 8
EDIM = 256
LAYERS = 2
P = 128
S = SEQ // 2
TILES = 2 * BATCH
GT = 8
GROUPS = TILES // GT
NC = GT // 2 * S
PT_ = 4
PAIRS = BATCH // 2
NBIN = SEQ // 2 + 1
LAGS = SEQ + S
CH = 4
CSTEPS = HID // CH
EPS_TOK = 1e-12
EPS_LN = 1e-5
ds = bass.ds


def need(eng, sem, value):
    if not (isinstance(value, int) and value <= 0):
        eng.wait_ge(sem, value)


def late(g):
    return not isinstance(g, int) or g >= 2


def first(g):
    return isinstance(g, int) and g == 0


def pipelined(eng, count, unroll, stages):
    lag = max(k for _, k in stages)
    start = unroll
    while start < lag + 2:
        start += unroll
    start = min(start, count)
    rounds = (count - start) // unroll

    def one(step, phase):
        for stage, k in stages:
            if isinstance(step, int) and not 0 <= step - k < count:
                continue
            stage(step - k, (phase - k) % unroll)

    for step in range(start):
        one(step, step % unroll)
    if rounds:
        with eng.Fori(start // unroll, start // unroll + rounds) as i:
            for u in range(unroll):
                for stage, k in stages:
                    stage(i * unroll + (u - k), (u - k) % unroll)
    for step in range(start + rounds * unroll, count + lag):
        one(step, step % unroll)


def build(nc, x, emb, pos, ln0_w, ln0_b, cw, fln_w, fln_b, d1_w, d1_b, d2_w, d2_b, iln_w, iln_b,
          wq, wk, wv, wo, wr, br, ln_g, ln_b, w1, b1, w2, b2, dft_re, dft_im, eye, selector, iota8,
          kern_dram, out):
    ctx = ExitStack()
    names = {}

    def sem(name):
        if name not in names:
            names[name] = ctx.enter_context(nc.semaphore(name))
        return names[name]

    def sb(stack, name, shape, dt=F32):
        return stack.enter_context(nc.sbuf_tensor(name, shape, dt))

    def pb(stack, name, shape, dt=F32):
        return stack.enter_context(nc.psum_tensor(name, shape, dt))

    with ctx:
        X = sb(ctx, "X", [P, TILES, HID])
        EYE = sb(ctx, "EYE", [P, P])
        NHALF, PHALF = sb(ctx, "NHALF", [P, GT]), sb(ctx, "PHALF", [P, GT])
        EPS_T, EPS_L = sb(ctx, "EPS_T", [P, GT]), sb(ctx, "EPS_L", [P, GT])
        D1Z = sb(ctx, "D1Z", [P, LAYERS, 2, DFF])
        D2 = sb(ctx, "D2", [P, LAYERS, 2, HID])
        D1B = sb(ctx, "D1B", [P, LAYERS, 2])
        D2B = sb(ctx, "D2B", [P, LAYERS])
        FW = sb(ctx, "FW", [P, LAYERS])
        FB = sb(ctx, "FB", [P, LAYERS])
        LASTW = sb(ctx, "LASTW", [S, HID])
        LASTB = sb(ctx, "LASTB", [S, HID])
        CBIAS = sb(ctx, "CBIAS", [S, LAYERS, HID])
        AS = sb(ctx, "AS", [P, HEADS, P], F16)
        BS = sb(ctx, "BS", [P, HEADS, HID], F16)
        W1S = sb(ctx, "W1S", [P, EXPERTS, EDIM], F16)
        WRS = sb(ctx, "WRS", [P, EXPERTS], F16)
        W2S = sb(ctx, "W2S", [P, EXPERTS, 2, HID])
        B1S = sb(ctx, "B1S", [P, EXPERTS, 2])
        B2S = sb(ctx, "B2S", [P, EXPERTS])
        BR = sb(ctx, "BR", [S, EXPERTS])
        SEL = sb(ctx, "SEL", [P, EXPERTS, HID], F16)
        IOTA = sb(ctx, "IOTA", [S, EXPERTS])
        MX = sb(ctx, "MX", [P, 4])
        SC = sb(ctx, "SC", [P, 4])

        with ExitStack() as st:
            IDX = sb(st, "IDX", [S, TILES], I32)
            POS = sb(st, "POS", [S, 2, HID])
            CWT = sb(st, "CWT", [NBIN, LAYERS, HID, 2])
            DRE = sb(st, "DRE", [NBIN, LAYERS, LAGS])
            DIM = sb(st, "DIM", [NBIN, LAYERS, LAGS])
            GAIN = sb(st, "GAIN", [HID, LAYERS])
            GB = sb(st, "GB", [S, LAYERS, HID])
            CW0 = sb(st, "CW0", [S, LAYERS, HID, 2])
            KERN = sb(st, "KERN", [HID, LAYERS, LAGS])
            WX = sb(st, "WX", [HID, 3, HEADS * HID])
            WXT = sb(st, "WXT", [HID, 3, HEADS, 2, HID])
            WO = sb(st, "WO", [HID, HEADS, HID])
            AN = sb(st, "AN", [P, HEADS, HID])
            BN = sb(st, "BN", [P, HEADS, HID])
            W1N = sb(st, "W1N", [P, EXPERTS, EDIM])
            W1R = sb(st, "W1R", [HID, EXPERTS, EDIM])
            LG = sb(st, "LG", [P, EXPERTS])
            LB = sb(st, "LB", [HID, EXPERTS])
            WRN = sb(st, "WRN", [P, EXPERTS])
            MXP = sb(st, "MXP", [P, 4])
            INV = sb(st, "INV", [P, 4])
            KP = pb(st, "KP", [HID, LAYERS, 512])
            TP = pb(st, "TP", [HID, 3, HEADS, HID])
            AP_ = pb(st, "AP_", [P, HEADS, HID])
            BP_ = pb(st, "BP_", [P, HEADS, HID])
            B1P = pb(st, "B1P", [P, EXPERTS, 2])
            LOADS = {}
            NEWTON = 15
            SUM, CEN, SQ = ([sb(st, f"n_{n}{i}", shape) for i in range(2)] for n, shape in
                            (("SUM", [S, GT]), ("CEN", [S, GT, HID]), ("SQ", [S, GT, HID])))
            SS, RS, RT = (sb(st, f"n_{n}", [S, GT]) for n in ("SS", "RS", "RT"))

            block = st.enter_context(nc.Block())

            @block.sync
            def _(sp):
                small = sem("small_loads")
                n = 0
                with nc.allow_non_contiguous_dma(reason="small parameters"):
                    sp.dma_start(IDX[:], x.rearrange("b (u s) -> s (b u)", u=2)).then_inc(sem("ids_loaded"), 16)
                    todo = [
                        (CWT[:], cw.rearrange("l k h c -> k l h c")),
                        (DRE[:], dft_re.rearrange("l k n -> k l n")), (DIM[:], dft_im.rearrange("l k n -> k l n")),
                        (GAIN[:, 0:1], ln0_w.rearrange("(h o) -> h o", o=1)),
                        (GAIN[:, 1:2], iln_w[0:1, :].rearrange("l h -> h l")),
                        (GB[:, 0, :], ln0_b.partition_broadcast(S)),
                        (GB[:, 1, :], iln_b[0, :].partition_broadcast(S)),
                        (CW0[:], cw[:, 0, :, :].partition_broadcast(S)),
                        (EYE[:], eye),
                        (WX[:, 0, :], wq), (WX[:, 1, :], wk), (WX[:, 2, :], wv),
                        (WO[:], wo.rearrange("(m h) d -> m h d", h=HEADS)),
                        (W1R[:], w1.rearrange("e d f -> d e f")),
                        (LB[:], ln_b.rearrange("e d -> d e")),
                        (B1S[:], b1.rearrange("e (c f) -> f e c", c=2)),
                        (W2S[:], w2.rearrange("e (c f) d -> f e c d", c=2)),
                        (POS[:], pos.rearrange("(u s) h -> s u h", u=2)),
                        (BR[:], br.partition_broadcast(S)),
                        (IOTA[:], iota8.partition_broadcast(S)),
                        (SEL[:], selector),
                        (LASTW[:], iln_w[1, :].partition_broadcast(S)),
                        (LASTB[:], iln_b[1, :].partition_broadcast(S)),
                        (D2[:], d2_w.rearrange("l (c f) h -> f l c h", c=2)),
                        (D1B[:], d1_b.rearrange("l (c f) -> f l c", c=2)),
                    ]
                    for half in range(2):
                        r = slice(half * HID, (half + 1) * HID)
                        todo += [
                            (W1N[r, :, :], w1.rearrange("e d f -> d e f")),
                            (LG[r, :], ln_g.rearrange("e d -> d e")),
                            (WRN[r, :], wr),
                            (B2S[r, :], b2.rearrange("e d -> d e")),
                            (D2B[r, :], d2_b.rearrange("l h -> h l")),
                            (FW[r, :], fln_w.rearrange("l h -> h l")),
                            (FB[r, :], fln_b.rearrange("l h -> h l")),
                        ]
                    for dst, src in todo:
                        sp.dma_start(dst, src).then_inc(small, 16)
                        n += 16
                    sp.wait_ge(sem("cleared"), 1)
                    for half in range(2):
                        r = slice(half * HID, (half + 1) * HID)
                        sp.dma_start(D1Z[r, :, half, :], d1_w.rearrange("l h f -> h l f")).then_inc(small, 16)
                        n += 16
                LOADS["small"] = n
                sp.wait_ge(sem("kernel_ready"), LAYERS)
                for l in range(LAYERS):
                    sp.dma_start(kern_dram[l], KERN[:, l, :]).then_inc(sem("kernel_stored"), 16)
                sp.wait_ge(sem("kernel_stored"), 16 * LAYERS)
                sp.wait_ge(small, n)

            n_small = LOADS["small"]

            @block.gpsimd
            def _(pool):
                pool.wait_ge(sem("ids_loaded"), 16)
                for t in range(TILES):
                    nc.gpsimd.indirect_dma_start(
                        X[0:S, t, :], None, emb, bass.IndirectOffsetOnAxis(ap=IDX[:, t:t + 1], axis=0)
                    ).then_inc(sem(f"gathered{t // GT}"), 16)
                    if t == 7 * GT:
                        pool.wait_ge(sem("maxima"), 4)
                        nc.gpsimd.partition_all_reduce(MX[:], MXP[:], P, RMAX).then_inc(sem("max_all"), 1)
                for g in range(GROUPS):
                    pool.wait_ge(sem(f"gathered{g}"), 16 * GT)

            @block.scalar
            def _(act):
                act.wait_ge(sem("wx_transposed"), 1)
                for i in range(3):
                    for d in range(2):
                        nc.scalar.copy(WXT[:, i, :, d, :], TP[:, i, :, :]).then_inc(sem("wxt_ready"), 1)
                for g in range(GROUPS):
                    act.wait_ge(sem("n_cen"), g + 1)
                    nc.scalar.activation(SQ[g % 2][:], CEN[g % 2][:], ACT.Square, scale=HID ** -0.5).then_inc(sem("n_sq"), 1)

            @block.tensor
            def _(pe):
                pe.wait_ge(sem("small_loads"), n_small)
                for l in range(LAYERS):
                    nc.tensor.matmul(KP[:, l, 0:LAGS], CWT[:, l, :, 0], DRE[:, l, :], start=True, stop=False)
                    nc.tensor.matmul(KP[:, l, 0:LAGS], CWT[:, l, :, 1], DIM[:, l, :], start=False,
                                     stop=True).then_inc(sem("kernel_summed"), 1)
                for i in range(3):
                    for h in range(HEADS):
                        last = nc.tensor.transpose(TP[:, i, h, :], WX[:, i, h::HEADS], EYE[0:HID, 0:HID])
                last.then_inc(sem("wx_transposed"), 1)
                pe.wait_ge(sem("wxt_ready"), 6)
                for h in range(HEADS):
                    last = nc.tensor.matmul(AP_[:, h, :], WXT[:, 0, h, :, :], WXT[:, 1, h, 0, :], start=True, stop=True)
                last.then_inc(sem("a_done"), 1)
                for h in range(HEADS):
                    last = nc.tensor.matmul(BP_[:, h, :], WXT[:, 2, h, :, :], WO[:, h, :], start=True, stop=True)
                last.then_inc(sem("b_done"), 1)
                for e in range(EXPERTS):
                    for c in range(2):
                        last = nc.tensor.matmul(B1P[:, e, c:c + 1], W1R[:, e, c * P:(c + 1) * P], LB[:, e:e + 1],
                                                start=True, stop=True)
                last.then_inc(sem("b1_done"), 1)

            @block.vector
            def _(dve):
                nc.vector.memset(D1Z[:], 0.0).then_inc(sem("cleared"), 1)
                for tile, value in ((NHALF, -0.5), (PHALF, 0.5), (EPS_T, EPS_TOK), (EPS_L, EPS_LN)):
                    nc.vector.memset(tile[:], value).then_inc(sem("consts"), 1)
                dve.wait_ge(sem("small_loads"), n_small)
                for l in range(LAYERS):
                    dve.wait_ge(sem("kernel_summed"), l + 1)
                    nc.vector.tensor_copy(KERN[:, l, :], KP[:, l, 0:LAGS]).then_inc(sem("k_a"), 1)
                    dve.wait_ge(sem("k_a"), l + 1)
                    nc.vector.tensor_scalar(KERN[:, l, S - 1:S], KERN[:, l, S - 1:S], 1.0, None,
                                            ALU.add).then_inc(sem("k_b"), 1)
                    dve.wait_ge(sem("k_b"), l + 1)
                    nc.vector.tensor_scalar(KERN[:, l, :], KERN[:, l, :], GAIN[:, l:l + 1], None,
                                            ALU.mult).then_inc(sem("kernel_ready"), 1)
                    nc.vector.tensor_scalar(CBIAS[:, l, :], CW0[:, l, :, 0], 1.0, None, ALU.add).then_inc(sem("cb_a"), 1)
                    dve.wait_ge(sem("cb_a"), l + 1)
                    nc.vector.tensor_tensor(CBIAS[:, l, :], CBIAS[:, l, :], GB[:, l, :], ALU.mult).then_inc(sem("cb_b"), 1)
                nc.vector.tensor_tensor(W1N[:], W1N[:], LG[:].unsqueeze(2).broadcast_to([P, EXPERTS, EDIM]),
                                        ALU.mult).then_inc(sem("w1_scaled"), 1)
                dve.wait_ge(sem("b1_done"), 1)
                nc.vector.tensor_tensor(B1S[:], B1S[:], B1P[:], ALU.add).then_inc(sem("b1_ready"), 1)
                dve.wait_ge(sem("a_done"), 1)
                nc.vector.tensor_copy(AN[:], AP_[:]).then_inc(sem("ab_copied"), 1)
                dve.wait_ge(sem("b_done"), 1)
                nc.vector.tensor_copy(BN[:], BP_[:]).then_inc(sem("ab_copied"), 1)
                dve.wait_ge(sem("ab_copied"), 2)
                dve.wait_ge(sem("w1_scaled"), 1)
                flat = [AN[:].rearrange("p h d -> p (h d)"), BN[:].rearrange("p h d -> p (h d)"),
                        W1N[:].rearrange("p h d -> p (h d)"), WRN[:]]
                for i, w in enumerate(flat):
                    nc.vector.reduce_max(MXP[:, i:i + 1], w, AX_X, apply_absolute_value=True).then_inc(sem("maxima"), 1)
                dve.wait_ge(sem("max_all"), 1)
                nc.vector.tensor_scalar(MX[:], MX[:], 1e-30, None, ALU.max).then_inc(sem("mx_guard"), 1)
                dve.wait_ge(sem("mx_guard"), 1)
                nc.vector.reciprocal(INV[:], MX[:]).then_inc(sem("mx_inv"), 1)
                nc.vector.tensor_copy(SC[:], MX[:]).then_inc(sem("sc_a"), 1)
                dve.wait_ge(sem("sc_a"), 1)
                nc.vector.tensor_scalar(SC[:, 0:1], SC[:, 0:1], float(HID) ** 0.5, None, ALU.mult).then_inc(sem("sc_b"), 1)
                dve.wait_ge(sem("mx_inv"), 1)
                dst = [AS[:, :, 0:HID], BS[:], W1S[:], WRS[:]]
                src = [AN[:], BN[:], W1N[:], WRN[:]]
                for i in range(4):
                    nc.vector.tensor_scalar(src[i], src[i], INV[:, i:i + 1], None, ALU.mult).then_inc(sem("normed"), 1)
                    dve.wait_ge(sem("normed"), i + 1)
                    nc.vector.tensor_copy(dst[i], src[i]).then_inc(sem("high"), 1)
                    dve.wait_ge(sem("high"), i + 1)
                    nc.vector.tensor_tensor(dst[i][HID:], src[i][HID:], dst[i][HID:], ALU.subtract).then_inc(sem("low"), 1)
                dve.wait_ge(sem("low"), 4)
                nc.vector.tensor_copy(AS[:, :, HID:], AS[:, :, 0:HID]).then_inc(sem("a_twice"), 1)
                dve.wait_ge(sem("a_twice"), 1)
                def centre(g, b):
                    dve.wait_ge(sem(f"gathered{g}"), 16 * GT)
                    xg = X[0:S, g * GT:(g + 1) * GT, :]
                    xv = xg.rearrange("s (b u) h -> s b u h", u=2)
                    nc.vector.tensor_tensor(xv, xv, POS[:].unsqueeze(1).broadcast_to([S, GT // 2, 2, HID]),
                                            ALU.add).then_inc(sem("pos_added"), 1)
                    dve.wait_ge(sem("pos_added"), g + 1)
                    nc.vector.reduce_sum(SUM[b][:], xg, AX_X).then_inc(sem("n_sum"), 1)
                    dve.wait_ge(sem("n_sum"), g + 1)
                    nc.vector.scalar_tensor_tensor(CEN[b][:], SUM[b][:].unsqueeze(2).broadcast_to([S, GT, HID]),
                                                   -1.0 / HID, xg, ALU.mult, ALU.add).then_inc(sem("n_cen"), 1)

                def scale(g, b):
                    dve.wait_ge(sem("n_sq"), g + 1)
                    count = [NEWTON * g]

                    def link(ins):
                        ins.then_inc(sem("n_newton"), 1)
                        count[0] += 1
                        dve.wait_ge(sem("n_newton"), count[0])
                    v = nc.vector
                    link(v.reduce_sum(SS[:], SQ[b][:], AX_X))
                    link(v.tensor_scalar(SS[:], SS[:], EPS_TOK, None, ALU.add))
                    link(v.tensor_scalar(RS[:].bitcast(I32), SS[:].bitcast(I32), -0.5, float(0x5F3759DF), ALU.mult, ALU.add))
                    for _ in range(4):
                        link(v.tensor_tensor(RT[:], RS[:], RS[:], ALU.mult))
                        link(v.scalar_tensor_tensor(RT[:], RT[:], -0.5, SS[:], ALU.mult, ALU.mult))
                        link(v.scalar_tensor_tensor(RS[:], RT[:], 1.5, RS[:], ALU.add, ALU.mult))
                    v.tensor_tensor(X[0:S, g * GT:(g + 1) * GT, :], CEN[b][:],
                                    RS[:].unsqueeze(2).broadcast_to([S, GT, HID]), ALU.mult).then_inc(sem("n_out"), 1)
                for g in range(GROUPS + 1):
                    if g < GROUPS:
                        centre(g, g % 2)
                    if g > 0:
                        scale(g - 1, (g - 1) % 2)

        for l in range(LAYERS):
            with ExitStack() as lay:
                Z = sb(lay, f"Z{l}", [P, TILES, HID])

                with ExitStack() as st:
                    NT = 4
                    T = [sb(st, f"T{l}_{i}", [S, CH, SEQ]) for i in range(NT)]
                    YP = [pb(st, f"YP{l}_{i}", [S, CH, TILES]) for i in range(NT)]
                    block = st.enter_context(nc.Block())
                    cb = l * CSTEPS

                    @block.sync
                    def _(sp):
                        def load(g, b):
                            need(sp, sem("conv_mm"), cb + g - NT + 1 if not isinstance(g, int) or g >= NT else 0)
                            src = bass.AP(tensor=kern_dram.tensor,
                                          offset=(l * HID + g * CH) * LAGS, ap=[[1, S], [LAGS, CH], [1, SEQ]])
                            sp.dma_start(T[b][:], src).then_inc(sem(f"filter_loaded{b}"), 16)
                        for g in range(CSTEPS):
                            load(g, g % NT)

                    @block.tensor
                    def _(pe):
                        def conv(g, b):
                            pe.wait_ge(sem(f"filter_loaded{b}"), 16 * (l * CSTEPS // NT + g // NT + 1))
                            if g >= NT:
                                pe.wait_ge(sem("conv_out"), cb + g - NT + 1)
                            for c in range(CH):
                                h = g * CH + c
                                xh = X[0:S, :, h]
                                swap = xh.rearrange("s (b u) -> s b u", u=2)[:, :, ::-1]
                                yp = YP[b][:, c, :]
                                nc.tensor.matmul(yp, T[b][:, c, 0:S], xh, start=True, stop=False)
                                last = nc.tensor.matmul(yp, T[b][:, c, S:], swap, start=False, stop=True)
                            last.then_inc(sem("conv_mm"), 1)
                        for g in range(CSTEPS):
                            conv(g, g % NT)

                    @block.vector
                    def _(dve):
                        def store(g, b):
                            dve.wait_ge(sem("conv_mm"), cb + g + 1)
                            nc.vector.tensor_tensor(
                                Z[0:S, :, g * CH:(g + 1) * CH].rearrange("s t c -> s c t"), YP[b][:],
                                CBIAS[:, l, g * CH:(g + 1) * CH].unsqueeze(2).broadcast_to([S, CH, TILES]),
                                ALU.add).then_inc(sem("conv_out"), 1)
                        for g in range(CSTEPS):
                            store(g, g % NT)

                with ExitStack() as st:
                    def two(name, shape, dt=F32):
                        return [sb(st, f"{name}{l}_{i}", shape, dt) for i in range(2)]
                    SUM, SS, RS = two("f_SUM", [S, 2, GT]), two("f_SS", [S, 2, GT]), two("f_RS", [S, 2, GT])
                    CEN, SQ = two("f_CEN", [S, 2, GT, HID]), two("f_SQ", [S, 2, GT, HID])
                    XN = two("f_XN", [S, GT, HID])
                    XT = two("f_XT", [P, NC])
                    G = two("f_G", [P, 2, 2, NC])
                    R = two("f_R", [P, NC])
                    HB = two("f_HB", [S, GT, HID])
                    PT = pb(st, f"f_PT{l}", [P, 512])
                    PH = [pb(st, f"f_PH{l}_{i}", [P, 512]) for i in range(4)]
                    PY = [pb(st, f"f_PY{l}_{i}", [P, 512]) for i in range(2)]
                    PR = pb(st, f"f_PR{l}", [S, GT, HID])
                    block = st.enter_context(nc.Block())
                    gb = l * GROUPS
                    last_layer = l == LAYERS - 1

                    @block.vector
                    def _(dve):
                        def centre(k, src, g, b):
                            nc.vector.reduce_sum(SUM[b][:, k, :], src, AX_X).then_inc(sem(f"f_sum{k}"), 1)
                            dve.wait_ge(sem(f"f_sum{k}"), gb + g + 1)
                            nc.vector.scalar_tensor_tensor(
                                CEN[b][:, k], SUM[b][:, k, :].unsqueeze(2).broadcast_to([S, GT, HID]),
                                -1.0 / HID, src, ALU.mult, ALU.add).then_inc(sem(f"f_cen{k}"), 1)

                        def squares(k, g, b):
                            dve.wait_ge(sem(f"f_sq{k}"), gb + g + 1)
                            nc.vector.reduce_sum(SS[b][:, k, :], SQ[b][:, k], AX_X).then_inc(sem(f"f_ss{k}"), 1)

                        def scale(k, g, b, out_):
                            dve.wait_ge(sem(f"f_rs{k}"), gb + g + 1)
                            nc.vector.tensor_tensor(out_, CEN[b][:, k], RS[b][:, k, :].unsqueeze(2).broadcast_to([S, GT, HID]),
                                                    ALU.mult).then_inc(sem(f"f_norm{k}"), 1)

                        def scale_in(g, b):
                            if late(g):
                                dve.wait_ge(sem("f_xt"), gb + g - 1)
                            scale(0, g, b, XN[b][:])

                        def residual(g, b):
                            dve.wait_ge(sem("f_y"), gb + g + 1)
                            dve.wait_ge(sem("f_xt_sb"), gb + g + 1)
                            if late(g):
                                dve.wait_ge(sem("f_rt"), gb + g - 1)
                            nc.vector.scalar_tensor_tensor(R[b][:], PY[b][:, 0:NC], D2B[:, l:l + 1], XT[b][:], ALU.add,
                                                           ALU.add).then_inc(sem("f_r"), 1)

                        def centre_out(g, b):
                            dve.wait_ge(sem("f_rt"), gb + g + 1)
                            centre(1, PR[:], g, b)

                        def scale_out(g, b):
                            xg = X[0:S, ds(g * GT, GT), :]
                            if not last_layer:
                                scale(1, g, b, xg)
                                return
                            scale(1, g, b, HB[b][:])
                            dve.wait_ge(sem("f_norm1"), gb + g + 1)
                            nc.vector.tensor_tensor(HB[b][:], HB[b][:], LASTW[:].unsqueeze(1).broadcast_to([S, GT, HID]),
                                                    ALU.mult).then_inc(sem("f_lastw"), 1)
                            dve.wait_ge(sem("f_lastw"), g + 1)
                            nc.vector.tensor_tensor(xg, HB[b][:], LASTB[:].unsqueeze(1).broadcast_to([S, GT, HID]),
                                                    ALU.add).then_inc(sem("f_lastb"), 1)

                        pipelined(dve, GROUPS, 2, [
                            (lambda g, b: centre(0, Z[0:S, ds(g * GT, GT), :], g, b), 0), (scale_in, 1), (residual, 2),
                            (lambda g, b: squares(0, g, b), 0), (centre_out, 2), (scale_out, 3),
                            (lambda g, b: squares(1, g, b), 2)])

                    @block.scalar
                    def _(act):
                        def square(k, g, b):
                            act.wait_ge(sem(f"f_cen{k}"), gb + g + 1)
                            nc.scalar.activation(SQ[b][:, k], CEN[b][:, k], ACT.Square, scale=HID ** -0.5).then_inc(sem(f"f_sq{k}"), 1)

                        def affine(g, b):
                            act.wait_ge(sem("f_xt"), gb + g + 1)
                            if late(g):
                                act.wait_ge(sem("f_r"), gb + g - 1)
                            nc.scalar.activation(XT[b][:], PT[:, 0:NC], ACT.Identity, bias=FB[:, l:l + 1],
                                                 scale=FW[:, l:l + 1]).then_inc(sem("f_xt_sb"), 1)

                        def gelu(g, b):
                            if late(g):
                                act.wait_ge(sem("f_y"), gb + g - 1)
                            for i in range(4):
                                par, c = divmod(i, 2)
                                act.wait_ge(sem("f_h"), 4 * (gb + g) + i + 1)
                                nc.scalar.activation(G[b][:, par, c, :], PH[i][:, 0:NC], ACT.Gelu,
                                                     bias=D1B[:, l, c:c + 1]).then_inc(sem("f_gelu"), 1)
                        pipelined(act, GROUPS, 2, [(lambda g, b: square(0, g, b), 0), (affine, 1),
                                                   (gelu, 1), (lambda g, b: square(1, g, b), 2)])

                    @block.gpsimd
                    def _(pool):
                        def rstd(k, g, b):
                            pool.wait_ge(sem(f"f_ss{k}"), gb + g + 1)
                            nc.gpsimd.tensor_tensor(RS[b][:, k, :], SS[b][:, k, :], EPS_T[0:S, :], ALU.add).then_inc(sem(f"f_var{k}"), 1)
                            pool.wait_ge(sem(f"f_var{k}"), gb + g + 1)
                            nc.gpsimd.tensor_tensor(RS[b][:, k, :], RS[b][:, k, :], NHALF[0:S, 0:GT],
                                                    ALU.pow).then_inc(sem(f"f_rs{k}"), 1)
                        pipelined(pool, GROUPS, 2, [(lambda g, b: rstd(0, g, b), 0), (lambda g, b: rstd(1, g, b), 2)])

                    @block.tensor
                    def _(pe):
                        def transpose_in(g, b):
                            pe.wait_ge(sem("f_norm0"), gb + g + 1)
                            if not first(g):
                                pe.wait_ge(sem("f_xt_sb"), gb + g)
                            for p in range(GT // 2):
                                last = nc.tensor.transpose(PT[:, p * S:(p + 1) * S], XN[b][:, 2 * p:2 * p + 2, :],
                                                           EYE[0:S, 0:S])
                            last.then_inc(sem("f_xt"), 1)

                        def up(g, b):
                            pe.wait_ge(sem("f_xt_sb"), gb + g + 1)
                            for i in range(4):
                                par, c = divmod(i, 2)
                                if not first(g):
                                    pe.wait_ge(sem("f_gelu"), 4 * (gb + g) + i - 3)
                                nc.tensor.matmul(PH[i][:, 0:NC], D1Z[:, l, par, c * P:(c + 1) * P], XT[b][:],
                                                 start=True, stop=True).then_inc(sem("f_h"), 1)

                        def down(g, b):
                            pe.wait_ge(sem("f_gelu"), 4 * (gb + g) + 4)
                            if late(g):
                                pe.wait_ge(sem("f_r"), gb + g - 1)
                            for c in range(2):
                                for par in range(2):
                                    last = nc.tensor.matmul(PY[b][par * HID:(par + 1) * HID, 0:NC], D2[:, l, c, :],
                                                            G[b][:, par, c, :], start=(c == 0), stop=(c == 1))
                            last.then_inc(sem("f_y"), 1)

                        def transpose_out(g, b):
                            pe.wait_ge(sem("f_r"), gb + g + 1)
                            if not first(g):
                                pe.wait_ge(sem("f_cen1"), gb + g)
                            for p in range(GT // 2):
                                last = nc.tensor.transpose(PR[:, 2 * p:2 * p + 2, :], R[b][:, p * S:(p + 1) * S],
                                                           EYE[:])
                            last.then_inc(sem("f_rt"), 1)
                        pipelined(pe, GROUPS, 2, [(transpose_in, 1), (transpose_out, 2), (up, 1), (down, 1)])

        with ExitStack() as st:
            def two(name, shape, dt=F32):
                return [sb(st, f"{name}_{i}", shape, dt) for i in range(2)]
            SUM, SS, RS = two("a_SUM", [S, PT_]), two("a_SS", [S, PT_]), two("a_RS", [S, PT_])
            CEN, SQ, XN = two("a_CEN", [S, PT_, HID]), two("a_SQ", [S, PT_, HID]), two("a_XN", [S, PT_, 2, HID])
            H2, L2 = two("a_H2", [P, NC], F16), two("a_L2", [P, NC], F16)
            U = two("a_U", [S, PT_, HEADS, HID])
            TS = two("a_TS", [P, NC], F16)
            AT = two("a_AT", [S, 2, NC])
            RO = two("a_RO", [P, SEQ])
            PT = pb(st, "a_PT", [P, 512])
            PU = pb(st, "a_PU", [P, 512])
            PTT = pb(st, "a_PTT", [P, 512])
            PO = pb(st, "a_PO", [P, 512])
            PS = [pb(st, f"a_PS{i}", [P, 2, 512]) for i in range(2)]
            block = st.enter_context(nc.Block())

            def exists(p):
                return not isinstance(p, int) or 0 <= p < PAIRS

            def tiles_of(p):
                return X[0:S, ds(p * PT_, PT_), :]

            @block.vector
            def _(dve):
                def centre(p, b):
                    nc.vector.reduce_sum(SUM[b][:], tiles_of(p), AX_X).then_inc(sem("a_sum"), 1)
                    dve.wait_ge(sem("a_sum"), p + 1)
                    nc.vector.scalar_tensor_tensor(CEN[b][:], SUM[b][:].unsqueeze(2).broadcast_to([S, PT_, HID]),
                                                   -1.0 / HID, tiles_of(p), ALU.mult, ALU.add).then_inc(sem("a_cen"), 1)

                def squares(p, b):
                    dve.wait_ge(sem("a_sq"), p + 1)
                    nc.vector.reduce_sum(SS[b][:], SQ[b][:], AX_X).then_inc(sem("a_ss"), 1)

                def scale(p, b):
                    dve.wait_ge(sem("a_rs"), p + 1)
                    if late(p):
                        dve.wait_ge(sem("a_xt"), p - 1)
                    nc.vector.tensor_tensor(XN[b][:], CEN[b][:].unsqueeze(2).broadcast_to([S, PT_, 2, HID]),
                                            RS[b][:].unsqueeze(2).unsqueeze(3).broadcast_to([S, PT_, 2, HID]),
                                            ALU.mult).then_inc(sem("a_norm"), 1)

                def low(p, b):
                    dve.wait_ge(sem("a_h2"), p + 1)
                    nc.vector.tensor_tensor(L2[b][:], PT[:, 0:NC], H2[b][:], ALU.subtract).then_inc(sem("a_l2"), 1)

                def values(p, b, i):
                    dve.wait_ge(sem("a_u"), p * PT_ + i + 1)
                    nc.vector.tensor_copy(U[b][:, i, :, :].rearrange("s h d -> s (h d)"),
                                          PU[0:S, :]).then_inc(sem("a_u_sb"), 1)

                def query_low(n, k):
                    dve.wait_ge(sem("a_tcast"), n + 1)
                    nc.vector.tensor_tensor(TS[k][HID:, :], PTT[HID:, 0:NC], TS[k][HID:, :],
                                            ALU.subtract).then_inc(sem("a_tlow"), 1)

                def add(p):
                    dve.wait_ge(sem("a_ot"), p + 1)
                    xv = tiles_of(p).rearrange("s (b u) d -> s u b d", u=2)
                    nc.vector.tensor_tensor(xv, xv, PU[0:S, 0:2 * P].rearrange("s (u b d) -> s u b d", u=2, b=2),
                                            ALU.add).then_inc(sem("a_added"), 1)

                def begin(p, b):
                    if first(p):
                        centre(0, 0)
                        squares(0, 0)
                        scale(0, 0)
                        low(0, 0)
                        for i in range(PT_):
                            values(0, 0, i)
                        query_low(0, 0)

                def main(p, b):
                    nxt, nb = p + 1, 1 - b
                    for h in range(HEADS):
                        n = p * HEADS + h
                        if h < HEADS - 1 or exists(nxt):
                            query_low(n + 1, (h + 1) % 2)
                        if h == 2 and exists(p - 1):
                            add(p - 1)
                        if exists(nxt):
                            if h == 0:
                                centre(nxt, nb)
                            if h == 1:
                                squares(nxt, nb)
                            if h == 2:
                                scale(nxt, nb)
                            if h == 4:
                                low(nxt, nb)
                            if h >= 4:
                                values(nxt, nb, h - 4)
                pipelined(dve, PAIRS, 2, [(begin, 0), (main, 1)])
                add(PAIRS - 1)

            @block.gpsimd
            def _(pool):
                def rstd(p, b):
                    pool.wait_ge(sem("a_ss"), p + 1)
                    nc.gpsimd.tensor_tensor(RS[b][:], SS[b][:], EPS_L[0:S, 0:PT_], ALU.add).then_inc(sem("a_var"), 1)
                    pool.wait_ge(sem("a_var"), p + 1)
                    nc.gpsimd.tensor_tensor(RS[b][:], RS[b][:], NHALF[0:S, 0:PT_], ALU.pow).then_inc(sem("a_rs"), 1)
                pipelined(pool, PAIRS, 2, [(rstd, 0)])

            @block.scalar
            def _(act):
                def square(p, b):
                    act.wait_ge(sem("a_cen"), p + 1)
                    nc.scalar.activation(SQ[b][:], CEN[b][:], ACT.Square, scale=HID ** -0.5).then_inc(sem("a_sq"), 1)

                def high(p, b):
                    act.wait_ge(sem("a_xt"), p + 1)
                    nc.scalar.copy(H2[b][:], PT[:, 0:NC]).then_inc(sem("a_h2"), 1)

                def query_high(n, k):
                    act.wait_ge(sem("a_t"), n + 1)
                    nc.scalar.copy(TS[k][:], PTT[:, 0:NC]).then_inc(sem("a_tcast"), 1)

                def sigmoid(n, k):
                    act.wait_ge(sem("a_s"), n + 1)
                    if late(n):
                        act.wait_ge(sem("a_av"), n - 1)
                    nc.scalar.activation(AT[k][:], PS[k][0:S, :, 0:NC], ACT.Sigmoid,
                                         scale=SC[0:S, 0:1]).then_inc(sem("a_sig"), 1)

                def relu(p, b):
                    act.wait_ge(sem("a_av"), (p + 1) * HEADS)
                    if late(p):
                        act.wait_ge(sem("a_ot"), p - 1)
                    nc.scalar.activation(RO[b][:], PO[:, 0:SEQ], ACT.Relu, scale=SC[:, 1:2]).then_inc(sem("a_relu"), 1)

                def begin(p, b):
                    if first(p):
                        square(0, 0)
                        high(0, 0)
                        query_high(0, 0)

                def main(p, b):
                    nxt, nb = p + 1, 1 - b
                    for h in range(HEADS):
                        n = p * HEADS + h
                        if h < HEADS - 1 or exists(nxt):
                            query_high(n + 1, (h + 1) % 2)
                        if h == 4 and exists(nxt):
                            high(nxt, nb)
                        sigmoid(n, h % 2)
                        if h == 0 and exists(p - 1):
                            relu(p - 1, nb)
                        if exists(nxt) and h == 0:
                            square(nxt, nb)
                pipelined(act, PAIRS, 2, [(begin, 0), (main, 1)])
                relu(PAIRS - 1, (PAIRS - 1) % 2)

            @block.tensor
            def _(pe):
                def transpose_in(p, b):
                    pe.wait_ge(sem("a_norm"), p + 1)
                    if not first(p):
                        pe.wait_ge(sem("a_l2"), p)
                    for i in range(PT_):
                        last = nc.tensor.transpose(PT[:, i * S:(i + 1) * S],
                                                   XN[b][:, i, :, :], EYE[0:S, 0:S])
                    last.then_inc(sem("a_xt"), 1)

                def values(p, b, i):
                    pe.wait_ge(sem("a_l2"), p + 1)
                    if not (isinstance(p, int) and p == 0 and i == 0):
                        pe.wait_ge(sem("a_u_sb"), p * PT_ + i)
                    cols = slice(i * S, (i + 1) * S)
                    nc.tensor.matmul(PU[0:S, :], H2[b][:, cols], BS[:], start=True, stop=False)
                    nc.tensor.matmul(PU[0:S, :], L2[b][:, cols], BS[:], start=False, stop=True).then_inc(sem("a_u"), 1)

                def query(n, b, h):
                    if not first(n):
                        pe.wait_ge(sem("a_tlow"), n)
                    nc.tensor.matmul(PTT[:, 0:NC], AS[:, h, :], H2[b][:], start=True, stop=False)
                    nc.tensor.matmul(PTT[:, 0:NC], AS[:, h, :], L2[b][:], start=False, stop=True).then_inc(sem("a_t"), 1)

                def scores(n, b, h):
                    pe.wait_ge(sem("a_tlow"), n + 1)
                    if late(n):
                        pe.wait_ge(sem("a_sig"), n - 1)
                    for bb in range(2):
                        for jc in range(2):
                            cols = slice((2 * bb + jc) * S, (2 * bb + jc + 1) * S)
                            o = PS[h % 2][0:S, bb, jc * SEQ:(jc + 1) * SEQ]
                            q = TS[h % 2][:, bb * SEQ:(bb + 1) * SEQ]
                            nc.tensor.matmul(o, H2[b][:, cols], q, start=True, stop=False)
                            last = nc.tensor.matmul(o, L2[b][:, cols], q, start=False, stop=True)
                    last.then_inc(sem("a_s"), 1)

                def mix(n, b, h):
                    pe.wait_ge(sem("a_sig"), n + 1)
                    for jc in range(2):
                        for bb in range(2):
                            last = nc.tensor.matmul(PO[bb * HID:(bb + 1) * HID, 0:SEQ], U[b][:, 2 * bb + jc, h, :],
                                                    AT[h % 2][:, bb, jc * SEQ:(jc + 1) * SEQ],
                                                    start=(h == 0 and jc == 0), stop=(h == HEADS - 1 and jc == 1))
                    last.then_inc(sem("a_av"), 1)

                def transpose_out(p, b):
                    pe.wait_ge(sem("a_relu"), p + 1)
                    for u in range(2):
                        last = nc.tensor.transpose(PU[0:S, u * P:(u + 1) * P], RO[b][:, u * S:(u + 1) * S], EYE[:])
                    last.then_inc(sem("a_ot"), 1)

                def begin(p, b):
                    if first(p):
                        transpose_in(0, 0)
                        for i in range(PT_):
                            values(0, 0, i)
                        query(0, 0, 0)

                def main(p, b):
                    nxt, nb = p + 1, 1 - b
                    for h in range(HEADS):
                        n = p * HEADS + h
                        if h < HEADS - 1:
                            query(n + 1, b, h + 1)
                        elif exists(nxt):
                            query(n + 1, nb, 0)
                        scores(n, b, h)
                        if h > 0:
                            if h == 1 and exists(p - 1):
                                pe.wait_ge(sem("a_relu"), p)
                            mix(n - 1, b, h - 1)
                        elif exists(p - 1):
                            mix(n - 1, nb, HEADS - 1)
                        if h == 1 and exists(p - 1):
                            transpose_out(p - 1, nb)
                        if exists(nxt):
                            if h == 3:
                                transpose_in(nxt, nb)
                            if h == 4 and exists(p - 1):
                                pe.wait_ge(sem("a_added"), p)
                            if h >= 4:
                                values(nxt, nb, h - 4)
                pipelined(pe, PAIRS, 2, [(begin, 0), (main, 1)])
                mix(PAIRS * HEADS - 1, (PAIRS - 1) % 2, HEADS - 1)
                transpose_out(PAIRS - 1, (PAIRS - 1) % 2)

        with ExitStack() as st:
            def two(name, shape, dt=F32):
                return [sb(st, f"{name}_{i}", shape, dt) for i in range(2)]
            SUM, SS, RS, RV, VR = (two(f"m_{n}", [S, GT]) for n in ("SUM", "SS", "RS", "RV", "VR"))
            CEN, SQ, XN = two("m_CEN", [S, GT, HID]), two("m_SQ", [S, GT, HID]), two("m_XN", [S, GT, 2, HID])
            H2, L2 = two("m_H2", [P, 2, NC], F16), two("m_L2", [P, 2, NC], F16)
            LOG, EQ, OH1, OH2 = (sb(st, f"m_{n}", [S, GT, EXPERTS]) for n in ("LOG", "EQ", "OH1", "OH2"))
            M1, M2, I1, I2, DF, EX, WA, WB_ = (sb(st, f"m_{n}", [S, GT]) for n in
                                               ("M1", "M2", "I1", "I2", "DF", "EX", "WA", "WB"))
            ETILE = sb(st, "m_E", [S, GT])
            WG = sb(st, "m_WG", [S, GT, EXPERTS])
            WP = sb(st, "m_WP", [S, GT, P], F16)
            EYE16 = sb(st, "m_EYE16", [S, S], F16)
            WT = two("m_WT", [P, 2, NC], F16)
            G = two("m_G", [P, 2, 2, NC])
            WBS = two("m_WBS", [P, NC])
            YW = two("m_YW", [P, NC])
            ACC = two("m_ACC", [P, NC])
            ZERO = sb(st, "m_ZERO", [P, NC])
            OUT = two("m_OUT", [S, GT, HID])
            PT = [pb(st, f"m_PT{i}", [P, 512]) for i in range(2)]
            PL = PT[0]
            PH = [pb(st, f"m_PH{i}", [P, 512]) for i in range(4)]
            PY = pb(st, "m_PY", [P, 512])
            PW = pb(st, "m_PW", [P, 512])
            PW16 = PT[1][:, 0:NC].bitcast(F16)
            out_v = out.rearrange("b (u s) h -> s (b u) h", u=2)
            block = st.enter_context(nc.Block())

            def exists(g):
                return not isinstance(g, int) or 0 <= g < GROUPS

            @block.sync
            def _(sp):
                for g in range(GROUPS):
                    sp.wait_ge(sem("m_out"), g + 1)
                    sp.dma_start(out_v[:, g * GT:(g + 1) * GT, :], OUT[g % 2][:]).then_inc(sem(f"m_stored{g % 2}"), 16)
                for b in range(2):
                    sp.wait_ge(sem(f"m_stored{b}"), 16 * (GROUPS // 2))

            NR = 17

            @block.vector
            def _(dve):
                nc.vector.memset(WP[:], 0.0).then_inc(sem("m_init"), 1)
                nc.vector.memset(ZERO[:], 0.0).then_inc(sem("m_init"), 1)
                nc.vector.memset(ETILE[:], 2.718281828459045).then_inc(sem("m_init"), 1)
                nc.vector.tensor_copy(EYE16[:], EYE[0:S, 0:S]).then_inc(sem("m_init"), 1)
                dve.wait_ge(sem("m_init"), 4)

                def tiles_of(g):
                    return X[0:S, ds(g * GT, GT), :]

                def centre(g, b):
                    nc.vector.reduce_sum(SUM[b][:], tiles_of(g), AX_X).then_inc(sem("m_sum"), 1)
                    dve.wait_ge(sem("m_sum"), g + 1)
                    nc.vector.scalar_tensor_tensor(CEN[b][:], SUM[b][:].unsqueeze(2).broadcast_to([S, GT, HID]),
                                                   -1.0 / HID, tiles_of(g), ALU.mult, ALU.add).then_inc(sem("m_cen"), 1)

                def squares(g, b):
                    dve.wait_ge(sem("m_sq"), g + 1)
                    nc.vector.reduce_sum(SS[b][:], SQ[b][:], AX_X).then_inc(sem("m_ss"), 1)

                def scale(g, b):
                    dve.wait_ge(sem("m_rs"), g + 1)
                    nc.vector.tensor_tensor(XN[b][:], CEN[b][:].unsqueeze(2).broadcast_to([S, GT, 2, HID]),
                                            RS[b][:].unsqueeze(2).unsqueeze(3).broadcast_to([S, GT, 2, HID]),
                                            ALU.mult).then_inc(sem("m_norm"), 1)

                def low(g, b):
                    for i in range(2):
                        dve.wait_ge(sem("m_h2"), 2 * g + i + 1)
                        nc.vector.tensor_tensor(L2[b][:, i, :], PT[i][:, 0:NC], H2[b][:, i, :],
                                                ALU.subtract).then_inc(sem("m_l2"), 1)

                def route(g, b, part):
                    step = [NR * g + (0, 7, 13)[part]]

                    def link(ins):
                        ins.then_inc(sem("m_route"), 1)
                        step[0] = step[0] + 1
                        dve.wait_ge(sem("m_route"), step[0])

                    def bc(t):
                        return t[:].unsqueeze(2).broadcast_to([S, GT, EXPERTS])
                    iota = IOTA[:].unsqueeze(1).broadcast_to([S, GT, EXPERTS])
                    v = nc.vector
                    if part == 0:
                        dve.wait_ge(sem("m_logits"), g + 1)
                        dve.wait_ge(sem("m_rv"), g + 1)
                        link(v.tensor_tensor(LOG[:], PL[0:S, 0:GT * EXPERTS].rearrange("s (t e) -> s t e", e=EXPERTS),
                                             bc(RV[b]), ALU.mult))
                        link(v.tensor_tensor(LOG[:], LOG[:], BR[:].unsqueeze(1).broadcast_to([S, GT, EXPERTS]), ALU.add))
                        link(v.reduce_max(M1[:], LOG[:], AX_X))
                        link(v.tensor_tensor(EQ[:], LOG[:], bc(M1), ALU.is_equal))
                        link(v.tensor_tensor(EQ[:], EQ[:], iota, ALU.mult))
                        link(v.tensor_reduce(I1[:], EQ[:], AX_X, ALU.min))
                        link(v.tensor_tensor(OH1[:], iota, bc(I1), ALU.is_equal))
                    elif part == 1:
                        link(v.scalar_tensor_tensor(LOG[:], OH1[:], -1e38, LOG[:], ALU.mult, ALU.add))
                        link(v.reduce_max(M2[:], LOG[:], AX_X))
                        link(v.tensor_tensor(EQ[:], LOG[:], bc(M2), ALU.is_equal))
                        link(v.tensor_tensor(EQ[:], EQ[:], iota, ALU.mult))
                        link(v.tensor_reduce(I2[:], EQ[:], AX_X, ALU.min))
                        link(v.tensor_tensor(OH2[:], iota, bc(I2), ALU.is_equal))
                        v.tensor_tensor(DF[:], M2[:], M1[:], ALU.subtract).then_inc(sem("m_diff"), 1)
                    else:
                        dve.wait_ge(sem("m_exp"), g + 1)
                        link(v.tensor_scalar(WA[:], EX[:], 1.0, None, ALU.add))
                        link(v.reciprocal(WA[:], WA[:]))
                        link(v.tensor_tensor(WB_[:], EX[:], WA[:], ALU.mult))
                        v.tensor_tensor(OH1[:], OH1[:], bc(WA), ALU.mult).then_inc(sem("m_oh1"), 1)
                        link(v.tensor_tensor(OH2[:], OH2[:], bc(WB_), ALU.mult))
                        dve.wait_ge(sem("m_oh1"), g + 1)
                        v.tensor_tensor(WG[:], OH1[:], OH2[:], ALU.add).then_inc(sem("m_wg"), 1)
                        dve.wait_ge(sem("m_wg"), g + 1)
                        if not first(g):
                            dve.wait_ge(sem("m_wt_ps"), g)
                        v.tensor_copy(WP[:, :, 0:EXPERTS], WG[:]).then_inc(sem("m_wphigh"), 1)
                        dve.wait_ge(sem("m_wphigh"), g + 1)
                        v.tensor_tensor(WP[:, :, HID:HID + EXPERTS], WG[:], WP[:, :, 0:EXPERTS],
                                        ALU.subtract).then_inc(sem("m_wp"), 1)

                def weigh(n, e):
                    dve.wait_ge(sem("m_w"), n + 1)
                    nc.vector.tensor_copy(WBS[e % 2][:], PW[:, 0:NC]).then_inc(sem("m_wbs"), 1)
                    dve.wait_ge(sem("m_wbs"), n + 1)
                    dve.wait_ge(sem("m_y"), n + 1)
                    if late(n):
                        dve.wait_ge(sem("m_acc"), n - 1)
                    nc.vector.scalar_tensor_tensor(YW[e % 2][:], PY[:, 0:NC], B2S[:, e:e + 1], WBS[e % 2][:],
                                                   ALU.add, ALU.mult).then_inc(sem("m_yw"), 1)

                def finish(g, b):
                    dve.wait_ge(sem("m_ot"), g + 1)
                    if late(g):
                        if isinstance(g, int):
                            dve.wait_ge(sem(f"m_stored{b}"), 16 * (g // 2))
                        else:
                            dve.wait_ge(sem(f"m_stored{b}"), (g - b) * 8)
                    nc.vector.tensor_tensor(OUT[b][:].rearrange("s (k p) d -> s p k d", k=2),
                                            tiles_of(g).rearrange("s (k p) d -> s p k d", k=2),
                                            PT[0][0:S, :].rearrange("s (p k d) -> s p k d", p=GT // 2, k=2),
                                            ALU.add).then_inc(sem("m_out"), 1)

                def begin(g, b):
                    if first(g):
                        centre(0, 0)
                        squares(0, 0)
                        scale(0, 0)
                        low(0, 0)
                        route(0, 0, 0)
                        route(0, 0, 1)
                        route(0, 0, 2)

                def main(g, b):
                    nxt, nb = g + 1, 1 - b
                    for e in range(EXPERTS):
                        n = g * EXPERTS + e
                        if e == 3 and exists(g - 1):
                            finish(g - 1, nb)
                        if exists(nxt):
                            if e == 0:
                                centre(nxt, nb)
                            if e == 1:
                                squares(nxt, nb)
                            if e == 4:
                                scale(nxt, nb)
                            if e == 5:
                                low(nxt, nb)
                        if e > 0:
                            weigh(n - 1, e - 1)
                        elif exists(g - 1):
                            weigh(n - 1, EXPERTS - 1)
                        if exists(nxt) and e >= 5:
                            route(nxt, nb, e - 5)
                pipelined(dve, GROUPS, 2, [(begin, 0), (main, 1)])
                weigh(GROUPS * EXPERTS - 1, EXPERTS - 1)
                finish(GROUPS - 1, (GROUPS - 1) % 2)

            @block.gpsimd
            def _(pool):
                pool.wait_ge(sem("m_init"), 4)

                def rstd(g, b):
                    step = [3 * g]

                    def link(ins):
                        ins.then_inc(sem("m_stat"), 1)
                        step[0] = step[0] + 1
                        pool.wait_ge(sem("m_stat"), step[0])
                    q = nc.gpsimd
                    pool.wait_ge(sem("m_ss"), g + 1)
                    link(q.tensor_tensor(RV[b][:], SS[b][:], EPS_L[0:S, :], ALU.add))
                    link(q.tensor_tensor(VR[b][:], RV[b][:], EPS_L[0:S, :], ALU.mult))
                    link(q.tensor_tensor(VR[b][:], VR[b][:], SS[b][:], ALU.add))
                    q.tensor_tensor(RS[b][:], VR[b][:], NHALF[0:S, 0:GT], ALU.pow).then_inc(sem("m_rs"), 1)

                def logit_scale(g, b):
                    step = [3 * g]

                    def link(ins):
                        ins.then_inc(sem("m_stat2"), 1)
                        step[0] = step[0] + 1
                        pool.wait_ge(sem("m_stat2"), step[0])
                    q = nc.gpsimd
                    pool.wait_ge(sem("m_rs"), g + 1)
                    link(q.tensor_tensor(RV[b][:], RV[b][:], NHALF[0:S, 0:GT], ALU.pow))
                    link(q.tensor_tensor(RV[b][:], RV[b][:], VR[b][:], ALU.mult))
                    link(q.tensor_tensor(RV[b][:], RV[b][:], RS[b][:], ALU.mult))
                    q.tensor_tensor(RV[b][:], RV[b][:], SC[0:S, 3:4].broadcast_to([S, GT]), ALU.mult).then_inc(sem("m_rv"), 1)

                def exponent(g, b):
                    pool.wait_ge(sem("m_diff"), g + 1)
                    nc.gpsimd.tensor_tensor(EX[:], ETILE[:], DF[:], ALU.pow).then_inc(sem("m_exp"), 1)

                def accumulate(n, e, b):
                    pool.wait_ge(sem("m_yw"), n + 1)
                    if e == 0:
                        nc.gpsimd.tensor_tensor(ACC[b][:], YW[0][:], ZERO[:], ALU.add).then_inc(sem("m_acc"), 1)
                    else:
                        pool.wait_ge(sem("m_acc"), n)
                        nc.gpsimd.tensor_tensor(ACC[b][:], ACC[b][:], YW[e % 2][:], ALU.add).then_inc(sem("m_acc"), 1)

                def begin(g, b):
                    if first(g):
                        rstd(0, 0)
                        logit_scale(0, 0)
                        exponent(0, 0)

                def main(g, b):
                    nxt, nb = g + 1, 1 - b
                    for e in range(EXPERTS):
                        n = g * EXPERTS + e
                        if exists(nxt):
                            if e == 2:
                                rstd(nxt, nb)
                            if e == 3:
                                logit_scale(nxt, nb)
                            if e == 7:
                                exponent(nxt, nb)
                        if e > 0:
                            accumulate(n - 1, e - 1, b)
                        elif exists(g - 1):
                            accumulate(n - 1, EXPERTS - 1, nb)
                pipelined(pool, GROUPS, 2, [(begin, 0), (main, 1)])
                accumulate(GROUPS * EXPERTS - 1, EXPERTS - 1, (GROUPS - 1) % 2)

            @block.scalar
            def _(act):
                def square(g, b):
                    act.wait_ge(sem("m_cen"), g + 1)
                    nc.scalar.activation(SQ[b][:], CEN[b][:], ACT.Square, scale=HID ** -0.5).then_inc(sem("m_sq"), 1)

                def high(g, b):
                    act.wait_ge(sem("m_xt"), g + 1)
                    for i in range(2):
                        nc.scalar.copy(H2[b][:, i, :], PT[i][:, 0:NC]).then_inc(sem("m_h2"), 1)

                def weights(g, b):
                    act.wait_ge(sem("m_wt_ps"), g + 1)
                    nc.scalar.copy(WT[b][:].rearrange("p k c -> p (k c)"), PW16).then_inc(sem("m_wt"), 1)

                def gelu(n, e):
                    if late(n):
                        act.wait_ge(sem("m_y"), n - 1)
                    for i in range(4):
                        k, c = divmod(i, 2)
                        act.wait_ge(sem("m_h"), 4 * n + i + 1)
                        nc.scalar.activation(G[e % 2][:, k, c, :], PH[i][:, 0:NC], ACT.Gelu, bias=B1S[:, e, c:c + 1],
                                             scale=SC[:, 2:3]).then_inc(sem("m_gelu"), 1)

                def begin(g, b):
                    if first(g):
                        square(0, 0)
                        high(0, 0)
                        weights(0, 0)

                def main(g, b):
                    nxt, nb = g + 1, 1 - b
                    for e in range(EXPERTS):
                        gelu(g * EXPERTS + e, e)
                        if exists(nxt):
                            if e == 0:
                                square(nxt, nb)
                            if e == 4:
                                high(nxt, nb)
                        if e == 0 and not first(g):
                            weights(g, b)
                pipelined(act, GROUPS, 2, [(begin, 0), (main, 1)])

            @block.tensor
            def _(pe):
                pe.wait_ge(sem("m_init"), 4)

                def transpose_in(g, b):
                    pe.wait_ge(sem("m_norm"), g + 1)
                    if not first(g):
                        pe.wait_ge(sem("m_wt"), g)
                    if not isinstance(g, int) or g >= 2:
                        pe.wait_ge(sem("m_out"), g - 1)
                    for t in range(GT):
                        last = nc.tensor.transpose(PT[t // 4][:, (t % 4) * S:(t % 4 + 1) * S],
                                                   XN[b][:, t, :, :], EYE[0:S, 0:S])
                    last.then_inc(sem("m_xt"), 1)

                def logits(g, b):
                    pe.wait_ge(sem("m_l2"), 2 * g + 2)
                    for t in range(GT):
                        cols = slice((t % 4) * S, (t % 4 + 1) * S)
                        o = PL[0:S, t * EXPERTS:(t + 1) * EXPERTS]
                        nc.tensor.matmul(o, H2[b][:, t // 4, cols], WRS[:], start=True, stop=False)
                        last = nc.tensor.matmul(o, L2[b][:, t // 4, cols], WRS[:], start=False, stop=True)
                    last.then_inc(sem("m_logits"), 1)

                def transpose_weights(g, b):
                    pe.wait_ge(sem("m_wp"), g + 1)
                    for t in range(GT):
                        last = nc.tensor.transpose(PW16[:, t * S:(t + 1) * S], WP[:, t, :], EYE16[:])
                    last.then_inc(sem("m_wt_ps"), 1)

                def up(n, e, b, i):
                    k, c = divmod(i, 2)
                    if not first(n):
                        pe.wait_ge(sem("m_gelu"), 4 * n + i - 3)
                    w = W1S[:, e, c * P:(c + 1) * P]
                    nc.tensor.matmul(PH[i][:, 0:NC], w, H2[b][:, k, :], start=True, stop=False)
                    nc.tensor.matmul(PH[i][:, 0:NC], w, L2[b][:, k, :], start=False, stop=True).then_inc(sem("m_h"), 1)

                def down(n, e, b, group):
                    if not first(n):
                        pe.wait_ge(sem("m_wbs"), n)
                        pe.wait_ge(sem("m_yw"), n)
                    if e == 0:
                        pe.wait_ge(sem("m_wt"), group + 1)
                    for k in range(2):
                        last = nc.tensor.matmul(PW[k * HID:(k + 1) * HID, 0:NC], SEL[:, e, :], WT[b][:, k, :],
                                                start=True, stop=True)
                    last.then_inc(sem("m_w"), 1)
                    pe.wait_ge(sem("m_gelu"), 4 * n + 4)
                    for c in range(2):
                        for k in range(2):
                            last = nc.tensor.matmul(PY[k * HID:(k + 1) * HID, 0:NC], W2S[:, e, c, :],
                                                    G[e % 2][:, k, c, :], start=(c == 0), stop=(c == 1))
                    last.then_inc(sem("m_y"), 1)

                def transpose_out(g, b):
                    pe.wait_ge(sem("m_acc"), EXPERTS * (g + 1))
                    for p in range(GT // 2):
                        last = nc.tensor.transpose(PT[0][0:S, p * P:(p + 1) * P], ACC[b][:, p * S:(p + 1) * S], EYE[:])
                    last.then_inc(sem("m_ot"), 1)

                def begin(g, b):
                    if first(g):
                        transpose_in(0, 0)
                        logits(0, 0)
                        transpose_weights(0, 0)
                        pe.wait_ge(sem("m_wt"), 1)

                def main(g, b):
                    nxt, nb = g + 1, 1 - b
                    for e in range(EXPERTS):
                        n = g * EXPERTS + e
                        for i in range(4):
                            up(n, e, b, i)
                        if e > 0:
                            down(n - 1, e - 1, b, g)
                        elif exists(g - 1):
                            down(n - 1, EXPERTS - 1, nb, g - 1)
                        if e == 0 and not first(g):
                            transpose_weights(g, b)
                        if e == 2 and exists(g - 1):
                            transpose_out(g - 1, nb)
                        if exists(nxt):
                            if e == 4:
                                transpose_in(nxt, nb)
                            if e == 5:
                                logits(nxt, nb)
                pipelined(pe, GROUPS, 2, [(begin, 0), (main, 1)])
                down(GROUPS * EXPERTS - 1, EXPERTS - 1, (GROUPS - 1) % 2, GROUPS - 1)
                transpose_out(GROUPS - 1, (GROUPS - 1) % 2)


_INS = ["x", "L0_tok_item_emb", "L0_tok_pos_emb", "L0_tok_ln0_w", "L0_tok_ln0_b", "L0_tok_cw", "L0_tok_fln_w",
        "L0_tok_fln_b", "L0_tok_d1_w", "L0_tok_d1_b", "L0_tok_d2_w", "L0_tok_d2_b", "L0_tok_iln_w", "L0_tok_iln_b",
        "L0_attn_Wq", "L0_attn_Wk", "L0_attn_Wv", "L0_attn_Wo", "L0_ffn_Wr", "L0_ffn_br", "L0_ffn_ln_g",
        "L0_ffn_ln_b", "L0_ffn_W1", "L0_ffn_b1", "L0_ffn_W2", "L0_ffn_b2"]


def kernel(**inputs):
    import numpy as _np
    import concourse.bacc as _bacc
    from concourse import mybir as _mybir
    from concourse.bass_utils import run_bass_kernel_spmd as _run

    nc = _bacc.Bacc("TRN2", target_bir_lowering=False, num_devices=1)
    k = _np.arange(NBIN)[:, None]
    lag = _np.arange(LAGS)
    lags = _np.stack([S - 1 - lag, lag - (S - 1)]) % SEQ
    fold = _np.where((k == 0) | (k == SEQ // 2), 1.0, 2.0) / SEQ
    sel = _np.zeros((P, EXPERTS, HID), _np.float16)
    for e in range(EXPERTS):
        sel[e, e, :] = 1
        sel[HID + e, e, :] = 1
    angle = 2 * _np.pi * ((k * lags[:, None]) % SEQ) / SEQ
    consts = {
        "dft_re": (fold * _np.cos(angle)).astype(_np.float32),
        "dft_im": (-fold * _np.sin(angle)).astype(_np.float32),
        "eye": _np.eye(P, dtype=_np.float32),
        "selector": sel,
        "iota8": (_np.arange(EXPERTS) - EXPERTS).astype(_np.float32),
    }
    arrays, args = {}, []
    for name in _INS + list(consts):
        a = _np.ascontiguousarray(inputs[name] if name in inputs else consts[name])
        arrays[f"in_{name}_dram"] = a
        args.append(nc.dram_tensor(f"in_{name}_dram", a.shape, _mybir.dt.from_np(a.dtype), kind="ExternalInput").ap())
    args.append(nc.dram_tensor("kernels_dram", (LAYERS, HID, LAGS), F32, kind="Internal").ap())
    args.append(nc.dram_tensor("out_0_dram", (BATCH, SEQ, HID), F32, kind="ExternalOutput").ap())
    build(nc, *args)
    r = _run(nc, [arrays], core_ids=[0])
    return r.results[0]["out_0_dram"]
```

```python
from contextlib import ExitStack

import concourse.bass as bass
from concourse import mybir

F32 = mybir.dt.float32
F16 = mybir.dt.float16
I32 = mybir.dt.int32
ALU = mybir.AluOpType
ACT = mybir.ActivationFunctionType
AX_X = mybir.AxisListType.X
RMAX = bass.bass_isa.ReduceOp.max

BATCH = 64
SEQ = 200
HID = 64
DFF = 256
HEADS = 8
EXPERTS = 8
EDIM = 256
LAYERS = 2
P = 128
S = SEQ // 2
TILES = 2 * BATCH
GT = 8
GROUPS = TILES // GT
NC = GT // 2 * S
PT_ = 4
PAIRS = BATCH // 2
AHEAD = 2
NBIN = SEQ // 2 + 1
LAGS = SEQ + S
CH = 4
CSTEPS = HID // CH
NBUF = 4
EPS_TOK = 1e-12
EPS_LN = 1e-5
ds = bass.ds


def late(g):
    return not isinstance(g, int) or g >= 2


def first(g):
    return isinstance(g, int) and g == 0


def pipelined(eng, count, unroll, stages):
    lag = max(k for _, k in stages)
    start = unroll
    while start < lag + 2:
        start += unroll
    start = min(start, count)
    rounds = (count - start) // unroll

    def one(step, phase):
        for stage, k in stages:
            if isinstance(step, int) and not 0 <= step - k < count:
                continue
            stage(step - k, (phase - k) % unroll)

    for step in range(start):
        one(step, step % unroll)
    if rounds:
        with eng.Fori(start // unroll, start // unroll + rounds) as i:
            for u in range(unroll):
                for stage, k in stages:
                    stage(i * unroll + (u - k), (u - k) % unroll)
    for step in range(start + rounds * unroll, count + lag):
        one(step, step % unroll)


def build(nc, x, emb, pos, ln0_w, ln0_b, cw, fln_w, fln_b, d1_w, d1_b, d2_w, d2_b, iln_w, iln_b,
          wq, wk, wv, wo, wr, br, ln_g, ln_b, w1, b1, w2, b2, dft_re, dft_im, eye, selector, iota8,
          kern_dram, turn_dram, out):
    ctx = ExitStack()
    names = {}

    def sem(name):
        if name not in names:
            names[name] = ctx.enter_context(nc.semaphore(name))
        return names[name]

    def sb(stack, name, shape, dt=F32):
        return stack.enter_context(nc.sbuf_tensor(name, shape, dt))

    def pb(stack, name, shape, dt=F32):
        return stack.enter_context(nc.psum_tensor(name, shape, dt))

    with ctx:
        X = sb(ctx, "X", [P, TILES, HID])
        EYE = sb(ctx, "EYE", [P, P])
        NHALF = sb(ctx, "NHALF", [P, GT])
        EPS_T, EPS_L = sb(ctx, "EPS_T", [P, GT]), sb(ctx, "EPS_L", [P, GT])
        D1Z = sb(ctx, "D1Z", [P, LAYERS, 2, DFF])
        D2 = sb(ctx, "D2", [P, LAYERS, 2, HID])
        D1B = sb(ctx, "D1B", [P, LAYERS, 2])
        D2B = sb(ctx, "D2B", [P, LAYERS])
        BSUM = sb(ctx, "BSUM", [P, HID])
        FW = sb(ctx, "FW", [P, LAYERS])
        FB = sb(ctx, "FB", [P, LAYERS])
        LASTW = sb(ctx, "LASTW", [S, HID])
        LASTB = sb(ctx, "LASTB", [S, HID])
        CBIAS = sb(ctx, "CBIAS", [S, LAYERS, HID])
        AS = sb(ctx, "AS", [P, HEADS, HID], F16)
        BS = sb(ctx, "BS", [P, HEADS, HID], F16)
        W1S = sb(ctx, "W1S", [P, EXPERTS, EDIM], F16)
        WRS = sb(ctx, "WRS", [P, EXPERTS], F16)
        W2S = sb(ctx, "W2S", [P, EXPERTS, 2, HID])
        B1S = sb(ctx, "B1S", [P, EXPERTS, 2])
        B2S = sb(ctx, "B2S", [P, EXPERTS])
        BR = sb(ctx, "BR", [S, EXPERTS])
        SEL = sb(ctx, "SEL", [P, EXPERTS, HID], F16)
        IOTA = sb(ctx, "IOTA", [S, EXPERTS])
        MX = sb(ctx, "MX", [P, 4])
        SC = sb(ctx, "SC", [P, 4])
        ESUM, ESS, ERS, ERV, EVR = ([sb(ctx, f"m_{n}_{i}", [S, GT]) for i in range(2)] for n in ("SUM", "SS", "RS", "RV", "VR"))
        ECEN, ESQ = ([sb(ctx, f"m_{n}_{i}", [S, GT, HID]) for i in range(2)] for n in ("CEN", "SQ"))
        EXN = [sb(ctx, f"m_XN_{i}", [S, GT, 2, HID]) for i in range(2)]
        EH2, EL2 = ([sb(ctx, f"m_{n}_{i}", [P, 2, NC], F16) for i in range(2)] for n in ("H2", "L2"))

        zs = ctx.enter_context(ExitStack())
        T = [sb(zs, f"T{i}", [S, CH, SEQ]) for i in range(NBUF)]

        def load_filter(sp, l, g):
            src = bass.AP(tensor=kern_dram.tensor, offset=(l * HID + g * CH) * LAGS, ap=[[1, S], [LAGS, CH], [1, SEQ]])
            sp.dma_start(T[g % NBUF][:], src).then_inc(sem(f"filter_loaded{g % NBUF}"), 16)

        with ExitStack() as st:
            IDX = sb(st, "IDX", [P, S], I32)
            POS = sb(st, "POS", [P, S, HID])
            POS2 = sb(st, "POS2", [S, 2, HID])
            CWT = sb(st, "CWT", [NBIN, LAYERS, HID, 2])
            DRE = sb(st, "DRE", [NBIN, LAYERS, LAGS])
            DIM = sb(st, "DIM", [NBIN, LAYERS, LAGS])
            GAIN = sb(st, "GAIN", [HID, LAYERS])
            GB = sb(st, "GB", [S, LAYERS, HID])
            CW0 = sb(st, "CW0", [S, LAYERS, HID, 2])
            KERN = sb(st, "KERN", [HID, LAYERS, LAGS])
            WX = sb(st, "WX", [HID, 3, HEADS * HID])
            WXT = sb(st, "WXT", [HID, 3, HEADS, 2, HID])
            WO = sb(st, "WO", [HID, HEADS, HID])
            AN = sb(st, "AN", [P, HEADS, HID])
            BN = sb(st, "BN", [P, HEADS, HID])
            W1N = sb(st, "W1N", [P, EXPERTS, EDIM])
            W1R = sb(st, "W1R", [HID, EXPERTS, EDIM])
            LG = sb(st, "LG", [P, EXPERTS])
            LB = sb(st, "LB", [HID, EXPERTS])
            WRN = sb(st, "WRN", [P, EXPERTS])
            MXP = sb(st, "MXP", [P, 4])
            INV = sb(st, "INV", [P, 4])
            KP = pb(st, "KP", [HID, LAYERS, 512])
            TP = pb(st, "TP", [HID, 3, HEADS, HID])
            AP_ = pb(st, "AP_", [P, HEADS, HID])
            BP_ = pb(st, "BP_", [P, HEADS, HID])
            B1P = pb(st, "B1P", [P, EXPERTS, 2])
            LOADS = {}
            NT = 2 * GT
            SHORT = 5 * NT
            STEPS = [(t, NT) for t in range(0, SHORT, NT)] + [(SHORT, GT), (SHORT + GT, GT), (SHORT + NT, S - SHORT - NT)]
            AT_ONCE = 4
            MAX_AT = 3 * NT
            NSTEPS = len(STEPS)
            TURNED = STEPS[-1][0]
            ROOTS = 3
            NEWTON = 3 + 3 * ROOTS
            SUM, CEN, SQ = ([sb(st, f"n_{n}{i}", shape) for i in range(2)] for n, shape in
                            (("SUM", [P, NT]), ("CEN", [P, NT, HID]), ("SQ", [P, NT, HID])))
            SS, RS, RT = (sb(st, f"n_{n}", [P, NT]) for n in ("SS", "RS", "RT"))

            block = st.enter_context(nc.Block())

            def turn_tokens(eng, half):
                eng.wait_ge(sem("n_norm"), NSTEPS)
                for token in range(TURNED + half, S, 2):
                    eng.dma_start(X[token:token + 1, S:TILES, :], X[S:TILES, token, :]).then_inc(sem("turned"), 16)

            @block.sync
            def _(sp):
                small = sem("small_loads")
                n = 0
                with nc.allow_non_contiguous_dma(reason="small parameters"):
                    ids = x.rearrange("b (u s) -> (b u) s", u=2)
                    sp.dma_start(IDX[0:S, :], ids[0:S, :].rearrange("t s -> s t")).then_inc(sem("ids_loaded"), 16)
                    sp.dma_start(IDX[S:P, :], ids[S:TILES, :]).then_inc(sem("ids_loaded"), 16)
                    sp.dma_start(POS2[:], pos.rearrange("(u s) h -> s u h", u=2)).then_inc(sem("pos_loaded"), 16)
                    for u in range(2):
                        sp.dma_start(POS[S + u:P:2, :, :], pos[u * S:(u + 1) * S, :].partition_broadcast((P - S) // 2)
                                     ).then_inc(sem("turn_pos_loaded"), 16)
                    todo = [
                        (CWT[:], cw.rearrange("l k h c -> k l h c")),
                        (DRE[:], dft_re.rearrange("l k n -> k l n")), (DIM[:], dft_im.rearrange("l k n -> k l n")),
                        (GAIN[:, 0:1], ln0_w.rearrange("(h o) -> h o", o=1)),
                        (GAIN[:, 1:2], iln_w[0:1, :].rearrange("l h -> h l")),
                        (GB[:, 0, :], ln0_b.partition_broadcast(S)),
                        (GB[:, 1, :], iln_b[0, :].partition_broadcast(S)),
                        (CW0[:], cw[:, 0, :, :].partition_broadcast(S)),
                        (EYE[:], eye),
                        (WX[:, 0, :], wq), (WX[:, 1, :], wk), (WX[:, 2, :], wv),
                        (WO[:], wo.rearrange("(m h) d -> m h d", h=HEADS)),
                        (W1R[:], w1.rearrange("e d f -> d e f")),
                        (LB[:], ln_b.rearrange("e d -> d e")),
                        (B1S[:], b1.rearrange("e (c f) -> f e c", c=2)),
                        (W2S[:], w2.rearrange("e (c f) d -> f e c d", c=2)),
                        (BR[:], br.partition_broadcast(S)),
                        (IOTA[:], iota8.partition_broadcast(S)),
                        (SEL[:], selector),
                        (LASTW[:], iln_w[1, :].partition_broadcast(S)),
                        (LASTB[:], iln_b[1, :].partition_broadcast(S)),
                        (D2[:], d2_w.rearrange("l (c f) h -> f l c h", c=2)),
                        (D1B[:], d1_b.rearrange("l (c f) -> f l c", c=2)),
                    ]
                    for half in range(2):
                        r = slice(half * HID, (half + 1) * HID)
                        todo += [
                            (W1N[r, :, :], w1.rearrange("e d f -> d e f")),
                            (LG[r, :], ln_g.rearrange("e d -> d e")),
                            (WRN[r, :], wr),
                            (B2S[r, :], b2.rearrange("e d -> d e")),
                            (D2B[r, :], d2_b.rearrange("l h -> h l")),
                            (FW[r, :], fln_w.rearrange("l h -> h l")),
                            (FB[r, :], fln_b.rearrange("l h -> h l")),
                        ]
                    for dst, src in todo:
                        sp.dma_start(dst, src).then_inc(small, 16)
                        n += 16
                    sp.wait_ge(sem("cleared"), 1)
                    for half in range(2):
                        r = slice(half * HID, (half + 1) * HID)
                        sp.dma_start(D1Z[r, :, half, :], d1_w.rearrange("l h f -> h l f")).then_inc(small, 16)
                        n += 16
                LOADS["small"] = n
                sp.wait_ge(sem("kernel_ready"), LAYERS)
                for l in range(LAYERS):
                    sp.dma_start(kern_dram[l], KERN[:, l, :]).then_inc(sem("kernel_stored"), 16)
                sp.wait_ge(sem("kernel_stored"), 16 * LAYERS)
                for g in range(NBUF):
                    load_filter(sp, 0, g)
                sp.wait_ge(small, n)
                most = slice(0, TURNED)
                sp.wait_ge(sem("n_norm"), NSTEPS - 1)
                sp.dma_start(turn_dram[:, most, :], X[S:TILES, most, :]).then_inc(sem("put"), 16)
                sp.wait_ge(sem("put"), 16)
                sp.dma_start(X[most, S:TILES, :], turn_dram[:, most, :].rearrange("t s h -> s t h")).then_inc(sem("turned"), 16)
                turn_tokens(sp, 0)
                sp.wait_ge(sem("turned"), 16 * (1 + S - TURNED))

            n_small = LOADS["small"]

            @block.gpsimd
            def _(pool):
                pool.wait_ge(sem("ids_loaded"), 32)
                for t in range(S):
                    nc.gpsimd.indirect_dma_start(
                        X[:, t, :], None, emb, bass.IndirectOffsetOnAxis(ap=IDX[:, t:t + 1], axis=0)
                    ).then_inc(sem(f"gathered{t // GT}"), 16)
                    if t == MAX_AT:
                        pool.wait_ge(sem("maxima"), 4)
                        nc.gpsimd.partition_all_reduce(MX[:], MXP[:], P, RMAX).then_inc(sem("max_all"), 1)

            @block.scalar
            def _(act):
                act.wait_ge(sem("pos_loaded"), 16)
                for t, n in STEPS:
                    nc.scalar.copy(POS[0:S, t:t + n, :].rearrange("s (b u) h -> s b u h", u=2),
                                   POS2[:].unsqueeze(1).broadcast_to([S, n // 2, 2, HID])).then_inc(sem("pos_filled"), 1)
                act.wait_ge(sem("wx_transposed"), 1)
                for i in range(3):
                    for d in range(2):
                        nc.scalar.copy(WXT[:, i, :, d, :], TP[:, i, :, :]).then_inc(sem("wxt_ready"), 1)
                act.wait_ge(sem("a_done"), 1)
                nc.scalar.copy(AN[:], AP_[:]).then_inc(sem("ab_copied"), 1)
                act.wait_ge(sem("b_done"), 1)
                nc.scalar.copy(BN[:], BP_[:]).then_inc(sem("ab_copied"), 1)
                for g in range(NSTEPS):
                    act.wait_ge(sem("n_cen"), g + 1)
                    n = STEPS[g][1]
                    nc.scalar.activation(SQ[g % 2][:, 0:n], CEN[g % 2][:, 0:n], ACT.Square,
                                         scale=HID ** -0.5).then_inc(sem("n_sq"), 1)
                turn_tokens(act, 1)

            @block.tensor
            def _(pe):
                pe.wait_ge(sem("small_loads"), n_small)
                for l in range(LAYERS):
                    nc.tensor.matmul(KP[:, l, 0:LAGS], CWT[:, l, :, 0], DRE[:, l, :], start=True, stop=False)
                    nc.tensor.matmul(KP[:, l, 0:LAGS], CWT[:, l, :, 1], DIM[:, l, :], start=False,
                                     stop=True).then_inc(sem("kernel_summed"), 1)
                for i in range(3):
                    for h in range(HEADS):
                        last = nc.tensor.transpose(TP[:, i, h, :], WX[:, i, h::HEADS], EYE[0:HID, 0:HID])
                last.then_inc(sem("wx_transposed"), 1)
                pe.wait_ge(sem("wxt_ready"), 6)
                for h in range(HEADS):
                    last = nc.tensor.matmul(AP_[:, h, :], WXT[:, 0, h, :, :], WXT[:, 1, h, 0, :], start=True, stop=True)
                last.then_inc(sem("a_done"), 1)
                for h in range(HEADS):
                    last = nc.tensor.matmul(BP_[:, h, :], WXT[:, 2, h, :, :], WO[:, h, :], start=True, stop=True)
                last.then_inc(sem("b_done"), 1)
                for e in range(EXPERTS):
                    for c in range(2):
                        last = nc.tensor.matmul(B1P[:, e, c:c + 1], W1R[:, e, c * P:(c + 1) * P], LB[:, e:e + 1],
                                                start=True, stop=True)
                last.then_inc(sem("b1_done"), 1)

            @block.vector
            def _(dve):
                nc.vector.memset(D1Z[:], 0.0).then_inc(sem("cleared"), 1)
                for tile, value in ((NHALF, -0.5), (EPS_T, EPS_TOK), (EPS_L, EPS_LN)):
                    nc.vector.memset(tile[:], value)
                def centre(g, b):
                    t, n = STEPS[g]
                    for part in range(t // GT, -(-(t + n) // GT)):
                        dve.wait_ge(sem(f"gathered{part}"), 16 * min(GT, S - part * GT))
                    xg = X[:, t:t + n, :]
                    dve.wait_ge(sem("pos_filled"), g + 1)
                    nc.vector.tensor_tensor(xg, xg, POS[:, t:t + n, :], ALU.add).then_inc(sem("pos_added"), 1)
                    dve.wait_ge(sem("pos_added"), g + 1)
                    nc.vector.reduce_sum(SUM[b][:, 0:n], xg, AX_X).then_inc(sem("n_sum"), 1)
                    dve.wait_ge(sem("n_sum"), g + 1)
                    nc.vector.scalar_tensor_tensor(CEN[b][:, 0:n], SUM[b][:, 0:n].unsqueeze(2).broadcast_to([P, n, HID]),
                                                   -1.0 / HID, xg, ALU.mult, ALU.add).then_inc(sem("n_cen"), 1)

                def scale(g, b):
                    dve.wait_ge(sem("n_sq"), g + 1)
                    t, n = STEPS[g]
                    steps = [NEWTON * g]

                    def chain(ins):
                        ins.then_inc(sem("n_newton"), 1)
                        steps[0] += 1
                        dve.wait_ge(sem("n_newton"), steps[0])
                    v = nc.vector
                    ss, rs, rt = SS[:, 0:n], RS[:, 0:n], RT[:, 0:n]
                    chain(v.reduce_sum(ss, SQ[b][:, 0:n], AX_X))
                    chain(v.tensor_scalar(ss, ss, EPS_TOK, None, ALU.add))
                    chain(v.tensor_scalar(rs.bitcast(I32), ss.bitcast(I32), -0.5, float(0x5F3759DF), ALU.mult, ALU.add))
                    for _ in range(ROOTS):
                        chain(v.tensor_tensor(rt, rs, rs, ALU.mult))
                        chain(v.scalar_tensor_tensor(rt, rt, -0.5, ss, ALU.mult, ALU.mult))
                        chain(v.scalar_tensor_tensor(rs, rt, 1.5, rs, ALU.add, ALU.mult))
                    v.tensor_tensor(X[:, t:t + n, :], CEN[b][:, 0:n], rs.unsqueeze(2).broadcast_to([P, n, HID]),
                                    ALU.mult).then_inc(sem("n_norm"), 1)

                def tokens(g):
                    at_once = g >= AT_ONCE
                    if g == AT_ONCE:
                        scale(g - 1, (g - 1) % 2)
                    centre(g, g % 2)
                    if at_once:
                        scale(g, g % 2)
                    elif g > 0:
                        scale(g - 1, (g - 1) % 2)
                dve.wait_ge(sem("turn_pos_loaded"), 32)
                tokens(0)
                dve.wait_ge(sem("small_loads"), n_small)
                count = [0]

                def link(ins):
                    ins.then_inc(sem("prepared"), 1)
                    count[0] += 1
                    dve.wait_ge(sem("prepared"), count[0])
                for l in range(LAYERS):
                    dve.wait_ge(sem("kernel_summed"), l + 1)
                    link(nc.vector.tensor_copy(KERN[:, l, :], KP[:, l, 0:LAGS]))
                    link(nc.vector.tensor_scalar(KERN[:, l, S - 1:S], KERN[:, l, S - 1:S], 1.0, None, ALU.add))
                    nc.vector.tensor_scalar(KERN[:, l, :], KERN[:, l, :], GAIN[:, l:l + 1], None,
                                            ALU.mult).then_inc(sem("kernel_ready"), 1)
                    link(nc.vector.tensor_scalar(CBIAS[:, l, :], CW0[:, l, :, 0], 1.0, None, ALU.add))
                    nc.vector.tensor_tensor(CBIAS[:, l, :], CBIAS[:, l, :], GB[:, l, :], ALU.mult)
                nc.vector.tensor_tensor(W1N[:], W1N[:], LG[:].unsqueeze(2).broadcast_to([P, EXPERTS, EDIM]),
                                        ALU.mult).then_inc(sem("w1_scaled"), 1)
                tokens(1)
                dve.wait_ge(sem("b1_done"), 1)
                nc.vector.tensor_tensor(B1S[:], B1S[:], B1P[:], ALU.add)
                dve.wait_ge(sem("ab_copied"), 2)
                dve.wait_ge(sem("w1_scaled"), 1)
                flat = [AN[:].rearrange("p h d -> p (h d)"), BN[:].rearrange("p h d -> p (h d)"),
                        W1N[:].rearrange("p h d -> p (h d)"), WRN[:]]
                for i, w in enumerate(flat):
                    nc.vector.reduce_max(MXP[:, i:i + 1], w, AX_X, apply_absolute_value=True).then_inc(sem("maxima"), 1)
                for g in range(2, MAX_AT // NT):
                    tokens(g)
                dve.wait_ge(sem("max_all"), 1)
                link(nc.vector.tensor_scalar(MX[:], MX[:], 1e-30, None, ALU.max))
                nc.vector.tensor_copy(SC[:, 2:4], MX[:, 2:4])
                nc.vector.tensor_scalar(SC[:, 0:1], MX[:, 0:1], 0.5 * float(HID) ** 0.5, None, ALU.mult)
                nc.vector.tensor_scalar(SC[:, 1:2], MX[:, 1:2], 0.5, None, ALU.mult)
                link(nc.vector.reciprocal(INV[:], MX[:]))
                dst = [AS[:], BS[:], W1S[:], WRS[:]]
                src = [AN[:], BN[:], W1N[:], WRN[:]]
                for i in range(4):
                    link(nc.vector.tensor_scalar(src[i], src[i], INV[:, i:i + 1], None, ALU.mult))
                    link(nc.vector.tensor_copy(dst[i], src[i]))
                    nc.vector.tensor_tensor(dst[i][HID:], src[i][HID:], dst[i][HID:], ALU.subtract)
                link(nc.vector.reduce_sum(BSUM[:], BN[:].rearrange("p h d -> p d h"), AX_X))
                nc.vector.tensor_scalar(BSUM[:], BSUM[:], 0.5, None, ALU.mult)
                for g in range(MAX_AT // NT, NSTEPS):
                    tokens(g)

        Z = sb(zs, "Z", [P, TILES, HID])
        for l in range(LAYERS):
            with ExitStack() as st:
                YP = [pb(st, f"YP{l}_{i}", [S, CH, TILES]) for i in range(NBUF)]
                block = st.enter_context(nc.Block())
                cb = l * CSTEPS

                @block.sync
                def _(sp):
                    for g in range(NBUF, CSTEPS):
                        sp.wait_ge(sem("conv_mm"), cb + g - NBUF + 1)
                        load_filter(sp, l, g)

                @block.tensor
                def _(pe):
                    def conv(g, b):
                        pe.wait_ge(sem(f"filter_loaded{b}"), 16 * (l * CSTEPS // NBUF + g // NBUF + 1))
                        if g >= NBUF:
                            pe.wait_ge(sem("conv_out"), cb + g - NBUF + 1)
                        for c in range(CH):
                            h = g * CH + c
                            xh = X[0:S, :, h]
                            swap = xh.rearrange("s (b u) -> s b u", u=2)[:, :, ::-1]
                            yp = YP[b][:, c, :]
                            nc.tensor.matmul(yp, T[b][:, c, 0:S], xh, start=True, stop=False)
                            last = nc.tensor.matmul(yp, T[b][:, c, S:], swap, start=False, stop=True)
                        last.then_inc(sem("conv_mm"), 1)
                    for g in range(CSTEPS):
                        conv(g, g % NBUF)

                @block.vector
                def _(dve):
                    def store(g, b):
                        dve.wait_ge(sem("conv_mm"), cb + g + 1)
                        nc.vector.tensor_tensor(
                            Z[0:S, :, g * CH:(g + 1) * CH].rearrange("s t c -> s c t"), YP[b][:],
                            CBIAS[:, l, g * CH:(g + 1) * CH].unsqueeze(2).broadcast_to([S, CH, TILES]),
                            ALU.add).then_inc(sem("conv_out"), 1)
                    for g in range(CSTEPS):
                        store(g, g % NBUF)

            with ExitStack() as st:
                def two(name, shape, dt=F32):
                    return [sb(st, f"{name}{l}_{i}", shape, dt) for i in range(2)]
                SUM, SS, RS = two("f_SUM", [S, 2, GT]), two("f_SS", [S, 2, GT]), two("f_RS", [S, 2, GT])
                CEN, SQ = two("f_CEN", [S, 2, GT, HID]), two("f_SQ", [S, 2, GT, HID])
                XN = two("f_XN", [S, GT, HID])
                XT = two("f_XT", [P, NC])
                G = two("f_G", [P, 2, 2, NC])
                R = two("f_R", [P, NC])
                HB = two("f_HB", [S, GT, HID])
                PT = pb(st, f"f_PT{l}", [P, 512])
                PH = [pb(st, f"f_PH{l}_{i}", [P, 512]) for i in range(4)]
                PY = [pb(st, f"f_PY{l}_{i}", [P, 512]) for i in range(2)]
                PR = pb(st, f"f_PR{l}", [S, GT, HID])
                block = st.enter_context(nc.Block())
                gb = l * GROUPS
                last_layer = l == LAYERS - 1
                count = AHEAD if last_layer else GROUPS

                if not last_layer:
                    @block.sync
                    def _(sp):
                        for g in range(NBUF):
                            load_filter(sp, l + 1, g)

                @block.vector
                def _(dve):
                    def centre(k, src, g, b):
                        nc.vector.reduce_sum(SUM[b][:, k, :], src, AX_X).then_inc(sem(f"f_sum{k}"), 1)
                        dve.wait_ge(sem(f"f_sum{k}"), gb + g + 1)
                        nc.vector.scalar_tensor_tensor(
                            CEN[b][:, k], SUM[b][:, k, :].unsqueeze(2).broadcast_to([S, GT, HID]),
                            -1.0 / HID, src, ALU.mult, ALU.add).then_inc(sem(f"f_cen{k}"), 1)

                    def squares(k, g, b):
                        dve.wait_ge(sem(f"f_sq{k}"), gb + g + 1)
                        nc.vector.reduce_sum(SS[b][:, k, :], SQ[b][:, k], AX_X).then_inc(sem(f"f_ss{k}"), 1)

                    def scale_in(g, b):
                        dve.wait_ge(sem("f_rs0"), gb + g + 1)
                        if late(g):
                            dve.wait_ge(sem("f_xt"), gb + g - 1)
                        nc.vector.tensor_tensor(XN[b][:], CEN[b][:, 0],
                                                RS[b][:, 0, :].unsqueeze(2).broadcast_to([S, GT, HID]),
                                                ALU.mult).then_inc(sem("f_norm0"), 1)

                    def residual(g, b):
                        dve.wait_ge(sem("f_y"), gb + g + 1)
                        dve.wait_ge(sem("f_xt_sb"), gb + g + 1)
                        if late(g):
                            dve.wait_ge(sem("f_rt"), gb + g - 1)
                        nc.vector.scalar_tensor_tensor(R[b][:], PY[b][:, 0:NC], D2B[:, l:l + 1], XT[b][:], ALU.add,
                                                       ALU.add).then_inc(sem("f_r"), 1)

                    def centre_out(g, b):
                        dve.wait_ge(sem("f_rt"), gb + g + 1)
                        if late(g):
                            dve.wait_ge(sem("f_norm1"), gb + g - 1)
                        centre(1, PR[:], g, b)

                    def affine_out(g, b):
                        dve.wait_ge(sem("f_rs1"), gb + g + 1)
                        nc.vector.tensor_tensor(HB[b][:], CEN[b][:, 1], RS[b][:, 1, :].unsqueeze(2).broadcast_to([S, GT, HID]),
                                                ALU.mult).then_inc(sem("f_norm1"), 1)
                        dve.wait_ge(sem("f_norm1"), gb + g + 1)
                        nc.vector.tensor_tensor(HB[b][:], HB[b][:], LASTW[:].unsqueeze(1).broadcast_to([S, GT, HID]),
                                                ALU.mult).then_inc(sem("f_lastw"), 1)
                        dve.wait_ge(sem("f_lastw"), g + 1)
                        nc.vector.tensor_tensor(X[0:S, ds(g * GT, GT), :], HB[b][:],
                                                LASTB[:].unsqueeze(1).broadcast_to([S, GT, HID]), ALU.add)

                    def centre_in(g, b):
                        centre(0, Z[0:S, ds(g * GT, GT), :], g, b)

                    def squares_in(g, b):
                        squares(0, g, b)

                    def squares_out(g, b):
                        squares(1, g, b)
                    if last_layer:
                        pipelined(dve, count, 2, [(centre_in, 0), (scale_in, 1), (squares_in, 0), (residual, 2),
                                                  (centre_out, 2), (squares_out, 2), (affine_out, 3)])
                    else:
                        pipelined(dve, count, 2, [(scale_in, 1), (centre_in, 0), (residual, 3), (squares_in, 0),
                                                  (squares_out, 4), (centre_out, 3)])

                @block.scalar
                def _(act):
                    def square(k, g, b):
                        act.wait_ge(sem(f"f_cen{k}"), gb + g + 1)
                        nc.scalar.activation(SQ[b][:, k], CEN[b][:, k], ACT.Square, scale=HID ** -0.5).then_inc(sem(f"f_sq{k}"), 1)

                    def affine(g, b):
                        act.wait_ge(sem("f_xt"), gb + g + 1)
                        if late(g):
                            act.wait_ge(sem("f_r"), gb + g - 1)
                        nc.scalar.activation(XT[b][:], PT[:, 0:NC], ACT.Identity, bias=FB[:, l:l + 1],
                                             scale=FW[:, l:l + 1]).then_inc(sem("f_xt_sb"), 1)

                    def gelu(g, b):
                        if late(g):
                            act.wait_ge(sem("f_y"), gb + g - 1)
                        for i in range(4):
                            par, c = divmod(i, 2)
                            act.wait_ge(sem("f_h"), 4 * (gb + g) + i + 1)
                            nc.scalar.activation(G[b][:, par, c, :], PH[i][:, 0:NC], ACT.Gelu,
                                                 bias=D1B[:, l, c:c + 1]).then_inc(sem("f_gelu"), 1)
                    pipelined(act, count, 2, [(lambda g, b: square(0, g, b), 0), (affine, 1),
                                               (gelu, 1), (lambda g, b: square(1, g, b), 2 if last_layer else 3)])

                @block.gpsimd
                def _(pool):
                    def rstd(k, g, b):
                        pool.wait_ge(sem(f"f_ss{k}"), gb + g + 1)
                        nc.gpsimd.tensor_tensor(RS[b][:, k, :], SS[b][:, k, :], EPS_T[0:S, :], ALU.add).then_inc(sem(f"f_var{k}"), 1)
                        pool.wait_ge(sem(f"f_var{k}"), gb + g + 1)
                        nc.gpsimd.tensor_tensor(RS[b][:, k, :], RS[b][:, k, :], NHALF[0:S, 0:GT],
                                                ALU.pow).then_inc(sem(f"f_rs{k}"), 1)

                    def scale_out(g, b):
                        pool.wait_ge(sem("f_rs1"), gb + g + 1)
                        nc.gpsimd.tensor_tensor(X[0:S, ds(g * GT, GT), :], CEN[b][:, 1],
                                                RS[b][:, 1, :].unsqueeze(2).broadcast_to([S, GT, HID]),
                                                ALU.mult).then_inc(sem("f_norm1"), 1)
                    pipelined(pool, count, 2, [(lambda g, b: rstd(0, g, b), 0),
                                               (lambda g, b: rstd(1, g, b), 2 if last_layer else 4)]
                              + ([] if last_layer else [(scale_out, 4)]))

                @block.tensor
                def _(pe):
                    def transpose_in(g, b):
                        pe.wait_ge(sem("f_norm0"), gb + g + 1)
                        if not first(g):
                            pe.wait_ge(sem("f_xt_sb"), gb + g)
                        for p in range(GT // 2):
                            last = nc.tensor.transpose(PT[:, p * S:(p + 1) * S], XN[b][:, 2 * p:2 * p + 2, :],
                                                       EYE[0:S, 0:S])
                        last.then_inc(sem("f_xt"), 1)

                    def up(g, b):
                        pe.wait_ge(sem("f_xt_sb"), gb + g + 1)
                        for i in range(4):
                            par, c = divmod(i, 2)
                            if not first(g):
                                pe.wait_ge(sem("f_gelu"), 4 * (gb + g) + i - 3)
                            nc.tensor.matmul(PH[i][:, 0:NC], D1Z[:, l, par, c * P:(c + 1) * P], XT[b][:],
                                             start=True, stop=True).then_inc(sem("f_h"), 1)

                    def down(g, b):
                        pe.wait_ge(sem("f_gelu"), 4 * (gb + g) + 4)
                        if late(g):
                            pe.wait_ge(sem("f_r"), gb + g - 1)
                        for c in range(2):
                            for par in range(2):
                                last = nc.tensor.matmul(PY[b][par * HID:(par + 1) * HID, 0:NC], D2[:, l, c, :],
                                                        G[b][:, par, c, :], start=(c == 0), stop=(c == 1))
                        last.then_inc(sem("f_y"), 1)

                    def transpose_out(g, b):
                        pe.wait_ge(sem("f_r"), gb + g + 1)
                        if not first(g):
                            pe.wait_ge(sem("f_cen1"), gb + g)
                        for p in range(GT // 2):
                            last = nc.tensor.transpose(PR[:, 2 * p:2 * p + 2, :], R[b][:, p * S:(p + 1) * S],
                                                       EYE[:])
                        last.then_inc(sem("f_rt"), 1)
                    if last_layer:
                        pipelined(pe, count, 2, [(transpose_in, 0), (up, 0), (transpose_out, 1), (down, 0)])
                    else:
                        pipelined(pe, count, 2, [(transpose_in, 1), (down, 2), (transpose_out, 3), (up, 1)])

        def expert_norm_vector(dve, PT):
            def tiles_of(g):
                return X[0:S, ds(g * GT, GT), :]

            def centre(g, b):
                nc.vector.reduce_sum(ESUM[b][:], tiles_of(g), AX_X).then_inc(sem("m_sum"), 1)
                dve.wait_ge(sem("m_sum"), g + 1)
                nc.vector.scalar_tensor_tensor(ECEN[b][:], ESUM[b][:].unsqueeze(2).broadcast_to([S, GT, HID]),
                                               -1.0 / HID, tiles_of(g), ALU.mult, ALU.add).then_inc(sem("m_cen"), 1)

            def squares(g, b):
                dve.wait_ge(sem("m_sq"), g + 1)
                nc.vector.reduce_sum(ESS[b][:], ESQ[b][:], AX_X).then_inc(sem("m_ss"), 1)

            def scale(g, b):
                dve.wait_ge(sem("m_rs"), g + 1)
                nc.vector.tensor_tensor(EXN[b][:], ECEN[b][:].unsqueeze(2).broadcast_to([S, GT, 2, HID]),
                                        ERS[b][:].unsqueeze(2).unsqueeze(3).broadcast_to([S, GT, 2, HID]),
                                        ALU.mult).then_inc(sem("m_norm"), 1)

            def low(g, b):
                for i in range(2):
                    dve.wait_ge(sem("m_h2"), 2 * g + i + 1)
                    nc.vector.tensor_tensor(EL2[b][:, i, :], PT[i][:, 0:NC], EH2[b][:, i, :],
                                            ALU.subtract).then_inc(sem("m_l2"), 1)
            return centre, squares, scale, low

        def expert_norm_pool(pool):
            def rstd(g, b):
                step = [3 * g]

                def link(ins):
                    ins.then_inc(sem("m_stat"), 1)
                    step[0] = step[0] + 1
                    pool.wait_ge(sem("m_stat"), step[0])
                q = nc.gpsimd
                pool.wait_ge(sem("m_ss"), g + 1)
                link(q.tensor_tensor(ERV[b][:], ESS[b][:], EPS_L[0:S, :], ALU.add))
                link(q.tensor_tensor(EVR[b][:], ERV[b][:], EPS_L[0:S, :], ALU.mult))
                link(q.tensor_tensor(EVR[b][:], EVR[b][:], ESS[b][:], ALU.add))
                q.tensor_tensor(ERS[b][:], EVR[b][:], NHALF[0:S, 0:GT], ALU.pow).then_inc(sem("m_rs"), 1)

            def logit_scale(g, b):
                step = [3 * g]

                def link(ins):
                    ins.then_inc(sem("m_stat2"), 1)
                    step[0] = step[0] + 1
                    pool.wait_ge(sem("m_stat2"), step[0])
                q = nc.gpsimd
                pool.wait_ge(sem("m_rs"), g + 1)
                link(q.tensor_tensor(ERV[b][:], ERV[b][:], NHALF[0:S, 0:GT], ALU.pow))
                link(q.tensor_tensor(ERV[b][:], ERV[b][:], EVR[b][:], ALU.mult))
                link(q.tensor_tensor(ERV[b][:], ERV[b][:], ERS[b][:], ALU.mult))
                q.tensor_tensor(ERV[b][:], ERV[b][:], SC[0:S, 3:4].broadcast_to([S, GT]), ALU.mult).then_inc(sem("m_rv"), 1)
            return rstd, logit_scale

        def expert_norm_scalar(act, PT):
            def square(g, b):
                act.wait_ge(sem("m_cen"), g + 1)
                nc.scalar.activation(ESQ[b][:], ECEN[b][:], ACT.Square, scale=HID ** -0.5).then_inc(sem("m_sq"), 1)

            def high(g, b):
                act.wait_ge(sem("m_xt"), g + 1)
                for i in range(2):
                    nc.scalar.copy(EH2[b][:, i, :], PT[i][:, 0:NC]).then_inc(sem("m_h2"), 1)
            return square, high

        def expert_norm_tensor(pe, PT):
            def transpose_in(g, b):
                pe.wait_ge(sem("m_norm"), g + 1)
                if not first(g):
                    pe.wait_ge(sem("m_wt"), g)
                if not isinstance(g, int) or g >= 2:
                    pe.wait_ge(sem("m_out"), g - 1)
                for t in range(GT):
                    last = nc.tensor.transpose(PT[t // 4][:, (t % 4) * S:(t % 4 + 1) * S],
                                               EXN[b][:, t, :, :], EYE[0:S, 0:S])
                last.then_inc(sem("m_xt"), 1)
            return transpose_in

        with ExitStack() as st:
            def two(name, shape, dt=F32):
                return [sb(st, f"{name}_{i}", shape, dt) for i in range(2)]
            SUM, SS, RS = two("a_SUM", [S, PT_]), two("a_SS", [S, PT_]), two("a_RS", [S, PT_])
            CEN, SQ, XN = two("a_CEN", [S, PT_, HID]), two("a_SQ", [S, PT_, HID]), two("a_XN", [S, PT_, 2, HID])
            H2, L2 = two("a_H2", [P, NC], F16), two("a_L2", [P, NC], F16)
            U = two("a_U", [S, PT_, HEADS, HID])
            TS = two("a_TS", [P, 2, NC], F16)
            AT = two("a_AT", [S, 2, NC])
            RO = two("a_RO", [P, SEQ])
            XS = two("a_XS", [P, 2])
            CB = two("a_CB", [P, 1])
            PU = pb(st, "a_PU", [P, 512])
            PT = PU
            fSUM, fSS, fRS = (sb(st, f"x_{n}", [S, 2, GT]) for n in ("SUM", "SS", "RS"))
            fCEN, fSQ = (sb(st, f"x_{n}", [S, 2, GT, HID]) for n in ("CEN", "SQ"))
            fXN, fHB = (sb(st, f"x_{n}", [S, GT, HID]) for n in ("XN", "HB"))
            fXT, fR = (sb(st, f"x_{n}", [P, NC]) for n in ("XT", "R"))
            fG = sb(st, "x_G", [P, 4, NC])
            PF = pb(st, "x_PF", [P, 512])
            PFR = PF[0:S, :].rearrange("s (t h) -> s t h", h=HID)
            L1 = LAYERS - 1
            PTT = pb(st, "a_PTT", [P, 512])
            PO = pb(st, "a_PO", [P, 512])
            PS = [pb(st, f"a_PS{i}", [P, 2, 512]) for i in range(2)]
            block = st.enter_context(nc.Block())

            def exists(p):
                return not isinstance(p, int) or 0 <= p < PAIRS

            def last_pair(p):
                return isinstance(p, int) and p == PAIRS - 1

            def tiles_of(p):
                return X[0:S, ds(p * PT_, PT_), :]

            def grouped(eng, begin, main):
                begin()
                main(0)
                main(1)
                with eng.Fori(2, GROUPS - AHEAD) as g:
                    main(g)
                for g in range(GROUPS - AHEAD, GROUPS):
                    main(g)

            def fed(g):
                return not isinstance(g, int) or 0 <= g < GROUPS - AHEAD

            def along(step, g, k):
                if fed(g):
                    step(g, k)
                if fed(g - 1):
                    step(g - 1, 2 * HEADS + k)

            @block.vector
            def _(dve):
                expert_centre, expert_squares, expert_scale, expert_low = expert_norm_vector(dve, (PF, PTT))

                def centre(p, b):
                    nc.vector.reduce_sum(SUM[b][:], tiles_of(p), AX_X).then_inc(sem("a_sum"), 1)
                    dve.wait_ge(sem("a_sum"), p + 1)
                    nc.vector.scalar_tensor_tensor(CEN[b][:], SUM[b][:].unsqueeze(2).broadcast_to([S, PT_, HID]),
                                                   -1.0 / HID, tiles_of(p), ALU.mult, ALU.add).then_inc(sem("a_cen"), 1)

                def squares(p, b):
                    dve.wait_ge(sem("a_sq"), p + 1)
                    nc.vector.reduce_sum(SS[b][:], SQ[b][:], AX_X).then_inc(sem("a_ss"), 1)

                def scale(p, b):
                    dve.wait_ge(sem("a_rs"), p + 1)
                    if late(p):
                        dve.wait_ge(sem("a_xt"), p - 1)
                    nc.vector.tensor_tensor(XN[b][:], CEN[b][:].unsqueeze(2).broadcast_to([S, PT_, 2, HID]),
                                            RS[b][:].unsqueeze(2).unsqueeze(3).broadcast_to([S, PT_, 2, HID]),
                                            ALU.mult).then_inc(sem("a_norm"), 1)

                def low(p, b):
                    dve.wait_ge(sem("a_h2"), 2 * p + 2)
                    nc.vector.tensor_tensor(L2[b][:], PT[:, 0:NC], H2[b][:], ALU.subtract).then_inc(sem("a_l2"), 1)

                def values(p, b, i):
                    dve.wait_ge(sem("a_u"), p * PT_ + i + 1)
                    nc.vector.tensor_copy(U[b][:, i, :, :].rearrange("s h d -> s (h d)"),
                                          PU[0:S, :]).then_inc(sem("a_u_sb"), 1)

                def query_low(n, h):
                    own, other = slice((h % 2) * HID, (h % 2 + 1) * HID), slice((1 - h % 2) * HID, (2 - h % 2) * HID)
                    ts = TS[h // 2 % 2]
                    dve.wait_ge(sem("a_tcast"), n + 1)
                    nc.vector.tensor_tensor(ts[other, h % 2, :], PTT[own, 0:NC], ts[own, h % 2, :],
                                            ALU.subtract).then_inc(sem("a_tlow"), 1)

                def feed_forward(g, k):
                    v = nc.vector
                    zg = Z[0:S, ds((g + AHEAD) * GT, GT), :]

                    def wide(t):
                        return t.unsqueeze(2).broadcast_to([S, GT, HID])
                    if k in (1, 15):
                        i = k // 15
                        src = (zg, PFR)[i]
                        if i:
                            dve.wait_ge(sem("x_rt"), g + 1)
                        v.reduce_sum(fSUM[:, i, :], src, AX_X).then_inc(sem(f"x_sum{i}"), 1)
                        dve.wait_ge(sem(f"x_sum{i}"), g + 1)
                        v.scalar_tensor_tensor(fCEN[:, i], wide(fSUM[:, i, :]), -1.0 / HID, src, ALU.mult,
                                               ALU.add).then_inc(sem(f"x_cen{i}"), 1)
                    if k in (4, 18):
                        i = k // 18
                        dve.wait_ge(sem(f"x_sq{i}"), g + 1)
                        v.reduce_sum(fSS[:, i, :], fSQ[:, i], AX_X).then_inc(sem(f"x_ss{i}"), 1)
                    if k in (6, 21):
                        i = k // 21
                        if i and not first(g):
                            dve.wait_ge(sem("x_b"), g)
                        dve.wait_ge(sem(f"x_rs{i}"), g + 1)
                        v.tensor_tensor((fXN, fHB)[i][:], fCEN[:, i], wide(fRS[:, i, :]), ALU.mult).then_inc(sem(f"x_norm{i}"), 1)
                    if k == 13:
                        dve.wait_ge(sem("x_y"), g + 1)
                        v.scalar_tensor_tensor(fR[:], PF[:, 0:NC], D2B[:, L1:L1 + 1], fXT[:], ALU.add,
                                               ALU.add).then_inc(sem("x_r"), 1)

                def constant(p, b):
                    dve.wait_ge(sem("a_c"), p + 1)
                    nc.vector.tensor_scalar(CB[b][:], PU[:, 2 * P:2 * P + 1], SC[:, 1:2], None, ALU.mult).then_inc(sem("a_cb"), 1)

                def add(p):
                    dve.wait_ge(sem("a_ot"), p + 1)
                    xv = tiles_of(p).rearrange("s (b u) d -> s u b d", u=2)
                    nc.vector.tensor_tensor(xv, xv, PU[0:S, 0:2 * P].rearrange("s (u b d) -> s u b d", u=2, b=2),
                                            ALU.add).then_inc(sem("a_added"), 1)

                def begin():
                    centre(0, 0)
                    squares(0, 0)
                    scale(0, 0)
                    low(0, 0)
                    query_low(0, 0)
                    query_low(1, 1)
                    for i in range(PT_):
                        values(0, 0, i)

                def main(g):
                    for b in range(2):
                        p = 2 * g + b
                        nxt, nb = p + 1, 1 - b
                        for h in range(HEADS):
                            n = p * HEADS + h
                            if exists(nxt):
                                if h == 0:
                                    if b and not first(g):
                                        dve.wait_ge(sem("x_b"), g)
                                    centre(nxt, nb)
                                if h == 2:
                                    squares(nxt, nb)
                                if h == 5:
                                    low(nxt, nb)
                            if h == 0 and not first(p):
                                values(p, b, PT_ - 1)
                            if h < HEADS - 2 or exists(nxt):
                                query_low(n + 2, (h + 2) % HEADS)
                            if h == 3:
                                constant(p, b)
                                if exists(p - 1):
                                    add(p - 1)
                                if exists(nxt):
                                    scale(nxt, nb)
                            if h >= 5 and exists(nxt):
                                values(nxt, nb, h - 5)
                            along(feed_forward, g, b * HEADS + h)
                            if last_pair(p):
                                if h == 1:
                                    expert_centre(0, 0)
                                if h == 3:
                                    expert_squares(0, 0)
                                if h == 6:
                                    expert_scale(0, 0)
                grouped(dve, begin, main)
                add(PAIRS - 1)
                expert_low(0, 0)

            @block.gpsimd
            def _(pool):
                expert_rstd, expert_logit_scale = expert_norm_pool(pool)

                def rstd(p, b):
                    pool.wait_ge(sem("a_ss"), p + 1)
                    nc.gpsimd.tensor_tensor(RS[b][:], SS[b][:], EPS_L[0:S, 0:PT_], ALU.add).then_inc(sem("a_var"), 1)
                    pool.wait_ge(sem("a_var"), p + 1)
                    nc.gpsimd.tensor_tensor(RS[b][:], RS[b][:], NHALF[0:S, 0:PT_], ALU.pow).then_inc(sem("a_rs"), 1)

                def feed_forward(g, i):
                    pool.wait_ge(sem(f"x_ss{i}"), g + 1)
                    nc.gpsimd.tensor_tensor(fRS[:, i, :], fSS[:, i, :], EPS_T[0:S, :], ALU.add).then_inc(sem(f"x_var{i}"), 1)
                    pool.wait_ge(sem(f"x_var{i}"), g + 1)
                    nc.gpsimd.tensor_tensor(fRS[:, i, :], fRS[:, i, :], NHALF[0:S, :], ALU.pow).then_inc(sem(f"x_rs{i}"), 1)

                def affine(g):
                    pool.wait_ge(sem("x_norm1"), g + 1)
                    nc.gpsimd.tensor_tensor(fHB[:], fHB[:], LASTW[:].unsqueeze(1).broadcast_to([S, GT, HID]),
                                            ALU.mult).then_inc(sem("x_w"), 1)
                    pool.wait_ge(sem("x_w"), g + 1)
                    nc.gpsimd.tensor_tensor(X[0:S, ds((g + AHEAD) * GT, GT), :], fHB[:],
                                            LASTB[:].unsqueeze(1).broadcast_to([S, GT, HID]),
                                            ALU.add).then_inc(sem("x_b"), 1)

                def main(g):
                    rstd(2 * g + 1, 1)
                    if fed(g - 1):
                        feed_forward(g - 1, 1)
                    if fed(g):
                        feed_forward(g, 0)
                    if fed(g - 1):
                        affine(g - 1)
                    if exists(2 * g + 2):
                        rstd(2 * g + 2, 0)
                grouped(pool, lambda: rstd(0, 0), main)
                expert_rstd(0, 0)
                expert_logit_scale(0, 0)

            @block.scalar
            def _(act):
                expert_square, expert_high = expert_norm_scalar(act, (PF, PTT))

                def square(p, b):
                    act.wait_ge(sem("a_cen"), p + 1)
                    nc.scalar.activation(SQ[b][:], CEN[b][:], ACT.Square, scale=HID ** -0.5).then_inc(sem("a_sq"), 1)

                def high(p, b):
                    act.wait_ge(sem("a_xt"), p + 1)
                    for bb in range(2):
                        cols = slice(bb * SEQ, (bb + 1) * SEQ)
                        nc.scalar.activation(H2[b][:, cols], PT[:, cols], ACT.Identity,
                                             accum_out=XS[b][:, bb:bb + 1]).then_inc(sem("a_h2"), 1)

                def query_high(pair, h):
                    own = slice((h % 2) * HID, (h % 2 + 1) * HID)
                    act.wait_ge(sem("a_t"), pair + 1)
                    nc.scalar.copy(TS[h // 2 % 2][own, h % 2, :], PTT[own, 0:NC]).then_inc(sem("a_tcast"), 1)

                def feed_forward(g, k):
                    if k in (2, 17):
                        i = k // 17
                        act.wait_ge(sem(f"x_cen{i}"), g + 1)
                        nc.scalar.activation(fSQ[:, i], fCEN[:, i], ACT.Square, scale=HID ** -0.5).then_inc(sem(f"x_sq{i}"), 1)
                    if k == 7:
                        act.wait_ge(sem("x_xt"), g + 1)
                        nc.scalar.activation(fXT[:], PF[:, 0:NC], ACT.Identity, bias=FB[:, L1:L1 + 1],
                                             scale=FW[:, L1:L1 + 1]).then_inc(sem("x_xt_sb"), 1)
                    if 8 <= k <= 11:
                        i = k - 8
                        act.wait_ge(sem("x_h"), 4 * g + i + 1)
                        nc.scalar.activation(fG[:, i, :], PF[:, 0:NC], ACT.Gelu,
                                             bias=D1B[:, L1, i % 2:i % 2 + 1]).then_inc(sem("x_g"), 1)

                def tanh(n, k):
                    act.wait_ge(sem("a_s"), n + 1)
                    if late(n):
                        act.wait_ge(sem("a_av"), n - 1)
                    nc.scalar.activation(AT[k][:], PS[k][0:S, :, 0:NC], ACT.Tanh,
                                         scale=SC[0:S, 0:1]).then_inc(sem("a_tanh"), 1)

                def relu(p, b):
                    act.wait_ge(sem("a_av"), (p + 1) * HEADS)
                    if late(p):
                        act.wait_ge(sem("a_ot"), p - 1)
                    act.wait_ge(sem("a_cb"), p + 1)
                    nc.scalar.activation(RO[b][:], PO[:, 0:SEQ], ACT.Relu, bias=CB[b][:], scale=SC[:, 1:2]).then_inc(sem("a_relu"), 1)

                def begin():
                    square(0, 0)
                    high(0, 0)
                    query_high(0, 0)
                    query_high(0, 1)

                def main(g):
                    for b in range(2):
                        p = 2 * g + b
                        nxt, nb = p + 1, 1 - b
                        for h in range(HEADS):
                            n = p * HEADS + h
                            if h < HEADS - 2 or exists(nxt):
                                query_high(p * (HEADS // 2) + h // 2 + 1, (h + 2) % HEADS)
                            tanh(n, h % 2)
                            if exists(nxt):
                                if h == 1:
                                    square(nxt, nb)
                                if h == 4:
                                    high(nxt, nb)
                            along(feed_forward, g, b * HEADS + h)
                            if h == 0 and exists(p - 1):
                                relu(p - 1, nb)
                            if last_pair(p) and h == 2:
                                expert_square(0, 0)
                grouped(act, begin, main)
                relu(PAIRS - 1, (PAIRS - 1) % 2)
                expert_high(0, 0)

            @block.tensor
            def _(pe):
                expert_transpose = expert_norm_tensor(pe, (PF, PTT))

                def transpose_in(p, b):
                    pe.wait_ge(sem("a_norm"), p + 1)
                    if not first(p):
                        pe.wait_ge(sem("a_u_sb"), p * PT_)
                    for i in range(PT_):
                        last = nc.tensor.transpose(PT[:, i * S:(i + 1) * S],
                                                   XN[b][:, i, :, :], EYE[0:S, 0:S])
                    last.then_inc(sem("a_xt"), 1)

                def values(p, b, i):
                    pe.wait_ge(sem("a_l2"), p + 1)
                    if not (isinstance(p, int) and p == 0 and i == 0):
                        pe.wait_ge(sem("a_u_sb"), p * PT_ + i)
                    cols = slice(i * S, (i + 1) * S)
                    nc.tensor.matmul(PU[0:S, :], H2[b][:, cols], BS[:], start=True, stop=False)
                    nc.tensor.matmul(PU[0:S, :], L2[b][:, cols], BS[:], start=False, stop=True).then_inc(sem("a_u"), 1)

                def query(pair, b, h):
                    if not first(pair):
                        pe.wait_ge(sem("a_tlow"), 2 * pair)
                    w = AS[:, h:h + 2, :]
                    nc.tensor.matmul(PTT[:, 0:NC], w, H2[b][:], start=True, stop=False)
                    nc.tensor.matmul(PTT[:, 0:NC], w, L2[b][:], start=False, stop=True).then_inc(sem("a_t"), 1)

                def feed_forward(g, k):
                    if k == 7:
                        pe.wait_ge(sem("x_norm0"), g + 1)
                        if not first(g):
                            pe.wait_ge(sem("x_cen1"), g)
                        for p in range(GT // 2):
                            last = nc.tensor.transpose(PF[:, p * S:(p + 1) * S], fXN[:, 2 * p:2 * p + 2, :], EYE[0:S, 0:S])
                        last.then_inc(sem("x_xt"), 1)
                    if 8 <= k <= 11:
                        i = k - 8
                        if i == 0:
                            pe.wait_ge(sem("x_xt_sb"), g + 1)
                        else:
                            pe.wait_ge(sem("x_g"), 4 * g + i)
                        nc.tensor.matmul(PF[:, 0:NC], D1Z[:, L1, i // 2, i % 2 * P:(i % 2 + 1) * P], fXT[:],
                                         start=True, stop=True).then_inc(sem("x_h"), 1)
                    if k == 12:
                        pe.wait_ge(sem("x_g"), 4 * g + 4)
                        for c in range(2):
                            for par in range(2):
                                last = nc.tensor.matmul(PF[par * HID:(par + 1) * HID, 0:NC], D2[:, L1, c, :],
                                                        fG[:, 2 * par + c, :], start=(c == 0), stop=(c == 1))
                        last.then_inc(sem("x_y"), 1)
                    if k == 14:
                        pe.wait_ge(sem("x_r"), g + 1)
                        for p in range(GT // 2):
                            last = nc.tensor.transpose(PFR[:, 2 * p:2 * p + 2, :], fR[:, p * S:(p + 1) * S], EYE[:])
                        last.then_inc(sem("x_rt"), 1)

                def scores(n, b, h):
                    pe.wait_ge(sem("a_tlow"), n + 1)
                    if late(n):
                        pe.wait_ge(sem("a_tanh"), n - 1)
                    for bb in range(2):
                        for jc in range(2):
                            cols = slice((2 * bb + jc) * S, (2 * bb + jc + 1) * S)
                            o = PS[h % 2][0:S, bb, jc * SEQ:(jc + 1) * SEQ]
                            q = TS[h // 2 % 2][:, h % 2, bb * SEQ:(bb + 1) * SEQ]
                            nc.tensor.matmul(o, H2[b][:, cols], q, start=True, stop=False)
                            last = nc.tensor.matmul(o, L2[b][:, cols], q, start=False, stop=True)
                    last.then_inc(sem("a_s"), 1)

                def constant(p, b):
                    for bb in range(2):
                        last = nc.tensor.matmul(PU[bb * HID:(bb + 1) * HID, 2 * P:2 * P + 1], BSUM[:], XS[b][:, bb:bb + 1],
                                                start=True, stop=True)
                    last.then_inc(sem("a_c"), 1)

                def mix(n, b, h):
                    pe.wait_ge(sem("a_tanh"), n + 1)
                    for jc in range(2):
                        for bb in range(2):
                            last = nc.tensor.matmul(PO[bb * HID:(bb + 1) * HID, 0:SEQ], U[b][:, 2 * bb + jc, h, :],
                                                    AT[h % 2][:, bb, jc * SEQ:(jc + 1) * SEQ],
                                                    start=(h == 0 and jc == 0), stop=(h == HEADS - 1 and jc == 1))
                    last.then_inc(sem("a_av"), 1)

                def transpose_out(p, b):
                    pe.wait_ge(sem("a_relu"), p + 1)
                    for u in range(2):
                        last = nc.tensor.transpose(PU[0:S, u * P:(u + 1) * P], RO[b][:, u * S:(u + 1) * S], EYE[:])
                    last.then_inc(sem("a_ot"), 1)

                def begin():
                    transpose_in(0, 0)
                    pe.wait_ge(sem("a_l2"), 1)
                    query(0, 0, 0)
                    for i in range(PT_):
                        values(0, 0, i)

                def main(g):
                    for b in range(2):
                        p = 2 * g + b
                        nxt, nb = p + 1, 1 - b
                        for h in range(HEADS):
                            n = p * HEADS + h
                            if h % 2 == 0:
                                pair = p * (HEADS // 2) + h // 2 + 1
                                if h < HEADS - 2:
                                    query(pair, b, h + 2)
                                elif exists(nxt):
                                    query(pair, nb, 0)
                            scores(n, b, h)
                            if h == 0:
                                if not first(p):
                                    values(p, b, PT_ - 1)
                                if exists(p - 1):
                                    mix(n - 1, nb, HEADS - 1)
                            if h == 2:
                                if exists(p - 1):
                                    transpose_out(p - 1, nb)
                                constant(p, b)
                            if exists(nxt):
                                if h == 4:
                                    pe.wait_ge(sem("a_cb"), p + 1)
                                    if exists(p - 1):
                                        pe.wait_ge(sem("a_added"), p)
                                    transpose_in(nxt, nb)
                                if h >= 6:
                                    values(nxt, nb, h - 5)
                            along(feed_forward, g, b * HEADS + h)
                            if h > 0:
                                if h == 1:
                                    pe.wait_ge(sem("a_u_sb"), (p + 1) * PT_)
                                    if exists(p - 1):
                                        pe.wait_ge(sem("a_relu"), p)
                                mix(n - 1, b, h - 1)
                            if last_pair(p) and h == HEADS - 1:
                                pe.wait_ge(sem("a_tlow"), PAIRS * HEADS)
                                expert_transpose(0, 0)
                            if h == 5 and exists(nxt):
                                values(nxt, nb, 0)
                grouped(pe, begin, main)
                mix(PAIRS * HEADS - 1, (PAIRS - 1) % 2, HEADS - 1)
                transpose_out(PAIRS - 1, (PAIRS - 1) % 2)

        zs.close()

        with ExitStack() as st:
            def two(name, shape, dt=F32):
                return [sb(st, f"{name}_{i}", shape, dt) for i in range(2)]
            LOG, EQ, OH1, OH2 = (sb(st, f"m_{n}", [S, GT, EXPERTS]) for n in ("LOG", "EQ", "OH1", "OH2"))
            M1, M2, I1, I2, DF, EX, WA, WB_ = (sb(st, f"m_{n}", [S, GT]) for n in
                                               ("M1", "M2", "I1", "I2", "DF", "EX", "WA", "WB"))
            ETILE = sb(st, "m_E", [S, GT])
            WG = sb(st, "m_WG", [S, GT, EXPERTS])
            WP = sb(st, "m_WP", [S, GT, P], F16)
            EYE16 = sb(st, "m_EYE16", [S, S], F16)
            WT = two("m_WT", [P, 2, NC], F16)
            G = two("m_G", [P, 2, 2, NC])
            WBS = two("m_WBS", [P, NC])
            YW = two("m_YW", [P, NC])
            ACC = two("m_ACC", [P, NC])
            ZERO = sb(st, "m_ZERO", [P, NC])
            OUT = two("m_OUT", [S, GT, HID])
            PT = [pb(st, f"m_PT{i}", [P, 512]) for i in range(2)]
            PL = PT[0]
            PH = [pb(st, f"m_PH{i}", [P, 512]) for i in range(4)]
            PY = pb(st, "m_PY", [P, 512])
            PW = pb(st, "m_PW", [P, 512])
            PW16 = PT[1][:, 0:NC].bitcast(F16)
            out_v = out.rearrange("b (u s) h -> s (b u) h", u=2)
            block = st.enter_context(nc.Block())

            def exists(g):
                return not isinstance(g, int) or 0 <= g < GROUPS

            @block.sync
            def _(sp):
                for g in range(GROUPS):
                    sp.wait_ge(sem("m_out"), g + 1)
                    sp.dma_start(out_v[:, g * GT:(g + 1) * GT, :], OUT[g % 2][:]).then_inc(sem(f"m_stored{g % 2}"), 16)
                for b in range(2):
                    sp.wait_ge(sem(f"m_stored{b}"), 16 * (GROUPS // 2))

            NR = 20

            @block.vector
            def _(dve):
                nc.vector.memset(WP[:], 0.0).then_inc(sem("m_init"), 1)
                nc.vector.memset(ZERO[:], 0.0).then_inc(sem("m_init"), 1)
                nc.vector.memset(ETILE[:], 2.718281828459045).then_inc(sem("m_init"), 1)
                nc.vector.tensor_copy(EYE16[:], EYE[0:S, 0:S]).then_inc(sem("m_init"), 1)
                dve.wait_ge(sem("m_init"), 4)
                centre, squares, scale, low = expert_norm_vector(dve, PT)

                def route(g, b, part):
                    step = [NR * g + (0, 7, 13)[part]]

                    def link(ins):
                        ins.then_inc(sem("m_route"), 1)
                        step[0] = step[0] + 1
                        dve.wait_ge(sem("m_route"), step[0])

                    def bc(t):
                        return t[:].unsqueeze(2).broadcast_to([S, GT, EXPERTS])
                    iota = IOTA[:].unsqueeze(1).broadcast_to([S, GT, EXPERTS])
                    v = nc.vector
                    if part == 0:
                        dve.wait_ge(sem("m_logits"), g + 1)
                        dve.wait_ge(sem("m_rv"), g + 1)
                        link(v.tensor_tensor(LOG[:], PL[0:S, 0:GT * EXPERTS].rearrange("s (t e) -> s t e", e=EXPERTS),
                                             bc(ERV[b]), ALU.mult))
                        link(v.tensor_tensor(LOG[:], LOG[:], BR[:].unsqueeze(1).broadcast_to([S, GT, EXPERTS]), ALU.add))
                        link(v.reduce_max(M1[:], LOG[:], AX_X))
                        link(v.tensor_tensor(EQ[:], LOG[:], bc(M1), ALU.is_equal))
                        link(v.tensor_tensor(EQ[:], EQ[:], iota, ALU.mult))
                        link(v.tensor_reduce(I1[:], EQ[:], AX_X, ALU.min))
                        link(v.tensor_tensor(OH1[:], iota, bc(I1), ALU.is_equal))
                    elif part == 1:
                        link(v.scalar_tensor_tensor(LOG[:], OH1[:], -1e38, LOG[:], ALU.mult, ALU.add))
                        link(v.reduce_max(M2[:], LOG[:], AX_X))
                        link(v.tensor_tensor(EQ[:], LOG[:], bc(M2), ALU.is_equal))
                        link(v.tensor_tensor(EQ[:], EQ[:], iota, ALU.mult))
                        link(v.tensor_reduce(I2[:], EQ[:], AX_X, ALU.min))
                        link(v.tensor_tensor(OH2[:], iota, bc(I2), ALU.is_equal))
                        v.tensor_tensor(DF[:], M2[:], M1[:], ALU.subtract).then_inc(sem("m_diff"), 1)
                    else:
                        dve.wait_ge(sem("m_exp"), g + 1)
                        link(v.tensor_scalar(WA[:], EX[:], 1.0, None, ALU.add))
                        link(v.reciprocal(WA[:], WA[:]))
                        link(v.tensor_tensor(WB_[:], EX[:], WA[:], ALU.mult))
                        link(v.tensor_tensor(OH1[:], OH1[:], bc(WA), ALU.mult))
                        link(v.tensor_tensor(OH2[:], OH2[:], bc(WB_), ALU.mult))
                        link(v.tensor_tensor(WG[:], OH1[:], OH2[:], ALU.add))
                        if not first(g):
                            dve.wait_ge(sem("m_wt_ps"), g)
                        link(v.tensor_copy(WP[:, :, 0:EXPERTS], WG[:]))
                        v.tensor_tensor(WP[:, :, HID:HID + EXPERTS], WG[:], WP[:, :, 0:EXPERTS],
                                        ALU.subtract).then_inc(sem("m_wp"), 1)

                def weigh(n, e):
                    dve.wait_ge(sem("m_w"), n + 1)
                    nc.vector.tensor_copy(WBS[e % 2][:], PW[:, 0:NC]).then_inc(sem("m_wbs"), 1)
                    dve.wait_ge(sem("m_wbs"), n + 1)
                    dve.wait_ge(sem("m_y"), n + 1)
                    if late(n):
                        dve.wait_ge(sem("m_acc"), n - 1)
                    nc.vector.scalar_tensor_tensor(YW[e % 2][:], PY[:, 0:NC], B2S[:, e:e + 1], WBS[e % 2][:],
                                                   ALU.add, ALU.mult).then_inc(sem("m_yw"), 1)

                def finish(g, b):
                    dve.wait_ge(sem("m_ot"), g + 1)
                    if late(g):
                        if isinstance(g, int):
                            dve.wait_ge(sem(f"m_stored{b}"), 16 * (g // 2))
                        else:
                            dve.wait_ge(sem(f"m_stored{b}"), (g - b) * 8)
                    nc.vector.tensor_tensor(OUT[b][:].rearrange("s (k p) d -> s p k d", k=2),
                                            X[0:S, ds(g * GT, GT), :].rearrange("s (k p) d -> s p k d", k=2),
                                            PT[0][0:S, :].rearrange("s (p k d) -> s p k d", p=GT // 2, k=2),
                                            ALU.add).then_inc(sem("m_out"), 1)

                def begin(g, b):
                    if first(g):
                        route(0, 0, 0)
                        route(0, 0, 1)
                        route(0, 0, 2)

                def main(g, b):
                    nxt, nb = g + 1, 1 - b
                    for e in range(EXPERTS):
                        n = g * EXPERTS + e
                        if e == 3 and exists(g - 1):
                            finish(g - 1, nb)
                        if exists(nxt):
                            if e == 2:
                                squares(nxt, nb)
                            if e == 4:
                                scale(nxt, nb)
                            if e == 5:
                                low(nxt, nb)
                        if e > 0:
                            weigh(n - 1, e - 1)
                        elif exists(g - 1):
                            weigh(n - 1, EXPERTS - 1)
                        if exists(nxt) and e == 0:
                            centre(nxt, nb)
                        if exists(nxt) and e >= 5:
                            route(nxt, nb, e - 5)
                pipelined(dve, GROUPS, 2, [(begin, 0), (main, 1)])
                weigh(GROUPS * EXPERTS - 1, EXPERTS - 1)
                finish(GROUPS - 1, (GROUPS - 1) % 2)

            @block.gpsimd
            def _(pool):
                pool.wait_ge(sem("m_init"), 4)
                rstd, logit_scale = expert_norm_pool(pool)

                def exponent(g, b):
                    pool.wait_ge(sem("m_diff"), g + 1)
                    nc.gpsimd.tensor_tensor(EX[:], ETILE[:], DF[:], ALU.pow).then_inc(sem("m_exp"), 1)

                def accumulate(n, e, b):
                    pool.wait_ge(sem("m_yw"), n + 1)
                    if e == 0:
                        nc.gpsimd.tensor_tensor(ACC[b][:], YW[0][:], ZERO[:], ALU.add).then_inc(sem("m_acc"), 1)
                    else:
                        pool.wait_ge(sem("m_acc"), n)
                        nc.gpsimd.tensor_tensor(ACC[b][:], ACC[b][:], YW[e % 2][:], ALU.add).then_inc(sem("m_acc"), 1)

                def begin(g, b):
                    if first(g):
                        exponent(0, 0)

                def main(g, b):
                    nxt, nb = g + 1, 1 - b
                    for e in range(EXPERTS):
                        n = g * EXPERTS + e
                        if exists(nxt):
                            if e == 2:
                                rstd(nxt, nb)
                            if e == 3:
                                logit_scale(nxt, nb)
                            if e == 7:
                                exponent(nxt, nb)
                        if e > 0:
                            accumulate(n - 1, e - 1, b)
                        elif exists(g - 1):
                            accumulate(n - 1, EXPERTS - 1, nb)
                pipelined(pool, GROUPS, 2, [(begin, 0), (main, 1)])
                accumulate(GROUPS * EXPERTS - 1, EXPERTS - 1, (GROUPS - 1) % 2)

            @block.scalar
            def _(act):
                square, high = expert_norm_scalar(act, PT)

                def weights(g, b):
                    act.wait_ge(sem("m_wt_ps"), g + 1)
                    nc.scalar.copy(WT[b][:].rearrange("p k c -> p (k c)"), PW16).then_inc(sem("m_wt"), 1)

                def gelu(n, e):
                    if late(n):
                        act.wait_ge(sem("m_y"), n - 1)
                    for i in range(4):
                        k, c = divmod(i, 2)
                        act.wait_ge(sem("m_h"), 4 * n + i + 1)
                        nc.scalar.activation(G[e % 2][:, k, c, :], PH[i][:, 0:NC], ACT.Gelu, bias=B1S[:, e, c:c + 1],
                                             scale=SC[:, 2:3]).then_inc(sem("m_gelu"), 1)

                def main(g, b):
                    nxt, nb = g + 1, 1 - b
                    for e in range(EXPERTS):
                        gelu(g * EXPERTS + e, e)
                        if e == 0:
                            weights(g, b)
                        if exists(nxt):
                            if e == 1:
                                square(nxt, nb)
                            if e == 4:
                                high(nxt, nb)
                pipelined(act, GROUPS, 2, [(main, 1)])

            @block.tensor
            def _(pe):
                transpose_in = expert_norm_tensor(pe, PT)

                def logits(g, b):
                    pe.wait_ge(sem("m_l2"), 2 * g + 2)
                    for t in range(GT):
                        cols = slice((t % 4) * S, (t % 4 + 1) * S)
                        o = PL[0:S, t * EXPERTS:(t + 1) * EXPERTS]
                        nc.tensor.matmul(o, EH2[b][:, t // 4, cols], WRS[:], start=True, stop=False)
                        last = nc.tensor.matmul(o, EL2[b][:, t // 4, cols], WRS[:], start=False, stop=True)
                    last.then_inc(sem("m_logits"), 1)

                def transpose_weights(g, b):
                    if first(g):
                        pe.wait_ge(sem("m_init"), 4)
                    pe.wait_ge(sem("m_wp"), g + 1)
                    for t in range(GT):
                        last = nc.tensor.transpose(PW16[:, t * S:(t + 1) * S], WP[:, t, :], EYE16[:])
                    last.then_inc(sem("m_wt_ps"), 1)

                def up(n, e, b, i):
                    k, c = divmod(i, 2)
                    if not first(n):
                        pe.wait_ge(sem("m_gelu"), 4 * n + i - 3)
                    w = W1S[:, e, c * P:(c + 1) * P]
                    nc.tensor.matmul(PH[i][:, 0:NC], w, EH2[b][:, k, :], start=True, stop=False)
                    nc.tensor.matmul(PH[i][:, 0:NC], w, EL2[b][:, k, :], start=False, stop=True).then_inc(sem("m_h"), 1)

                def down(n, e, b, group):
                    if not first(n):
                        pe.wait_ge(sem("m_wbs"), n)
                        pe.wait_ge(sem("m_yw"), n)
                    if e == 0:
                        pe.wait_ge(sem("m_wt"), group + 1)
                    for k in range(2):
                        last = nc.tensor.matmul(PW[k * HID:(k + 1) * HID, 0:NC], SEL[:, e, :], WT[b][:, k, :],
                                                start=True, stop=True)
                    last.then_inc(sem("m_w"), 1)
                    pe.wait_ge(sem("m_gelu"), 4 * n + 4)
                    for c in range(2):
                        for k in range(2):
                            last = nc.tensor.matmul(PY[k * HID:(k + 1) * HID, 0:NC], W2S[:, e, c, :],
                                                    G[e % 2][:, k, c, :], start=(c == 0), stop=(c == 1))
                    last.then_inc(sem("m_y"), 1)

                def transpose_out(g, b):
                    pe.wait_ge(sem("m_acc"), EXPERTS * (g + 1))
                    for p in range(GT // 2):
                        last = nc.tensor.transpose(PT[0][0:S, p * P:(p + 1) * P], ACC[b][:, p * S:(p + 1) * S], EYE[:])
                    last.then_inc(sem("m_ot"), 1)

                def begin(g, b):
                    if first(g):
                        logits(0, 0)

                def main(g, b):
                    nxt, nb = g + 1, 1 - b
                    for e in range(EXPERTS):
                        n = g * EXPERTS + e
                        for i in range(4):
                            up(n, e, b, i)
                        if e == 1 and first(g):
                            transpose_weights(g, b)
                        if e > 0:
                            down(n - 1, e - 1, b, g)
                        elif exists(g - 1):
                            down(n - 1, EXPERTS - 1, nb, g - 1)
                        if e == 0 and not first(g):
                            transpose_weights(g, b)
                        if e == 2 and exists(g - 1):
                            transpose_out(g - 1, nb)
                        if exists(nxt):
                            if e == 4:
                                transpose_in(nxt, nb)
                            if e == 5:
                                logits(nxt, nb)
                pipelined(pe, GROUPS, 2, [(begin, 0), (main, 1)])
                down(GROUPS * EXPERTS - 1, EXPERTS - 1, (GROUPS - 1) % 2, GROUPS - 1)
                transpose_out(GROUPS - 1, (GROUPS - 1) % 2)


_INS = ["x", "L0_tok_item_emb", "L0_tok_pos_emb", "L0_tok_ln0_w", "L0_tok_ln0_b", "L0_tok_cw", "L0_tok_fln_w",
        "L0_tok_fln_b", "L0_tok_d1_w", "L0_tok_d1_b", "L0_tok_d2_w", "L0_tok_d2_b", "L0_tok_iln_w", "L0_tok_iln_b",
        "L0_attn_Wq", "L0_attn_Wk", "L0_attn_Wv", "L0_attn_Wo", "L0_ffn_Wr", "L0_ffn_br", "L0_ffn_ln_g",
        "L0_ffn_ln_b", "L0_ffn_W1", "L0_ffn_b1", "L0_ffn_W2", "L0_ffn_b2"]


def kernel(**inputs):
    import numpy as _np
    import concourse.bacc as _bacc
    from concourse import mybir as _mybir
    from concourse.bass_utils import run_bass_kernel_spmd as _run

    nc = _bacc.Bacc("TRN2", target_bir_lowering=False, num_devices=1)
    k = _np.arange(NBIN)[:, None]
    lag = _np.arange(LAGS)
    lags = _np.stack([S - 1 - lag, lag - (S - 1)]) % SEQ
    fold = _np.where((k == 0) | (k == SEQ // 2), 1.0, 2.0) / SEQ
    sel = _np.zeros((P, EXPERTS, HID), _np.float16)
    for e in range(EXPERTS):
        sel[e, e, :] = 1
        sel[HID + e, e, :] = 1
    angle = 2 * _np.pi * ((k * lags[:, None]) % SEQ) / SEQ
    consts = {
        "dft_re": (fold * _np.cos(angle)).astype(_np.float32),
        "dft_im": (-fold * _np.sin(angle)).astype(_np.float32),
        "eye": _np.eye(P, dtype=_np.float32),
        "selector": sel,
        "iota8": (_np.arange(EXPERTS) - EXPERTS).astype(_np.float32),
    }
    arrays, args = {}, []
    for name in _INS + list(consts):
        a = _np.ascontiguousarray(inputs[name] if name in inputs else consts[name])
        arrays[f"in_{name}_dram"] = a
        args.append(nc.dram_tensor(f"in_{name}_dram", a.shape, _mybir.dt.from_np(a.dtype), kind="ExternalInput").ap())
    args.append(nc.dram_tensor("kernels_dram", (LAYERS, HID, LAGS), F32, kind="Internal").ap())
    args.append(nc.dram_tensor("turn_dram", (TILES - S, S, HID), F32, kind="Internal").ap())
    args.append(nc.dram_tensor("out_0_dram", (BATCH, SEQ, HID), F32, kind="ExternalOutput").ap())
    build(nc, *args)
    r = _run(nc, [arrays], core_ids=[0])
    return r.results[0]["out_0_dram"]
```
